# Optimizing a Trainium2 kernel written in Bass

```python
import numpy as np
import jax
import jax.numpy as jnp

def _softmax(x, axis=-1):
    return jax.nn.softmax(x, axis=axis)

def _gelu(x):
    return jax.nn.gelu(x, approximate=True)

def _silu(x):
    return jax.nn.silu(x)

def _sigmoid(x):
    return jax.nn.sigmoid(x)

def _layernorm(x, axis=-1, eps=1e-05):
    m = jnp.mean(x, axis=axis, keepdims=True)
    v = jnp.var(x, axis=axis, keepdims=True)
    return (x - m) / jnp.sqrt(v + eps)

def _scatter_add(tgt, idx, src, axis=0):
    return tgt.at[idx].add(src)

def _segment_sum(src, seg, n):
    return jax.ops.segment_sum(src, seg, n)
kernel_name = 'mk_decoder_preln_d1_seqx_r8_44514e'

def setup_inputs(seed: int=0):
    np.random.seed(seed)
    _w = jnp.asarray

    def _rec_inputs():
        import jax
        import jax.numpy as jnp
        _rk = jax.random.key(seed)
        x = -0.0005207 + 1.001 * jax.random.normal(jax.random.fold_in(_rk, 1), (4, 256, 128), jnp.float32)
        _lenS = 256 - jax.random.randint(jax.random.fold_in(_rk, 7), (4,), 0, max(1, 256 // 4) + 1, jnp.int32)
        _lenS2 = 512 - jax.random.randint(jax.random.fold_in(_rk, 8), (4,), 0, max(1, 512 // 4) + 1, jnp.int32)
        _ctx_1024P = jax.random.normal(jax.random.fold_in(_rk, 11), (4, 16, 128), jnp.float32)
        _ctx_1024c = jax.random.dirichlet(jax.random.fold_in(_rk, 511), 0.3 * jnp.ones((16,), jnp.float32), (4, 512))
        _ctx_1024t = jnp.einsum('bsk,bkd->bsd', _ctx_1024c, _ctx_1024P)
        _ctx_1024t = _ctx_1024t * jax.lax.rsqrt(jnp.mean(jnp.square(_ctx_1024t)) + 1e-12) * 0.953939
        ctx_1024 = -1.52775e-05 + 0.999936 * (_ctx_1024t + 0.3 * jax.random.normal(jax.random.fold_in(_rk, 611), (4, 512, 128), jnp.float32))
        return (x, ctx_1024)
    x, ctx_1024 = _rec_inputs()

    def _L0_attn_setup():
        import math
        import jax, jax.numpy as jnp
        import numpy as np
        HID = 128
        H = 8
        D = HID // H
        CHUNK = 12
        PAST = 13 - 1
        FUT = 0
        CTX = CHUNK + PAST + FUT
        SOFTCAP = 50.0
        Q_SCALE = D ** (-0.5) / math.log(2)
        K_SCALE = math.log(1.0 + math.e) / math.log(2)

        def _extract_block_context(x, num_blocks):
            xp = jnp.pad(x, ((0, 0), (PAST, FUT + CHUNK - 1), (0, 0), (0, 0)))
            idx = jnp.arange(num_blocks)[:, None] * CHUNK + jnp.arange(CTX)[None, :]
            return xp[:, idx]

        def _rel_shift(x):
            B, Hh, nb, bs, pos_len = x.shape
            x = jnp.pad(x, ((0, 0), (0, 0), (0, 0), (0, 0), (0, CTX + 1 - pos_len)))
            x = x.reshape(B, Hh, nb, bs * (CTX + 1))[..., :bs * CTX]
            return x.reshape(B, Hh, nb, bs, CTX)
        key = jax.random.key(seed)
        ks = jax.random.split(key, 8)
        B, S = (4, 768)
        P = CTX + 1
        std = HID ** (-0.5)
        return {'hidden_states': jax.random.normal(ks[0], (B, S, HID), jnp.float32), 'position_embeddings': jax.random.normal(ks[1], (P, HID), jnp.float32), 'Wq': jax.random.normal(ks[2], (HID, HID), jnp.float32) * std, 'Wk': jax.random.normal(ks[3], (HID, HID), jnp.float32) * std, 'Wv': jax.random.normal(ks[4], (HID, HID), jnp.float32) * std, 'Wpost': jax.random.normal(ks[5], (HID, HID), jnp.float32) * std, 'Wrel': jax.random.normal(ks[6], (HID, HID), jnp.float32) * std, 'per_dim_scale': jnp.zeros((D,), jnp.float32)}
    _L0_attn_all = _L0_attn_setup()
    _L0_attn_in = {k: v for k, v in _L0_attn_all.items() if k in ('position_embeddings', 'Wq', 'Wk', 'Wv', 'Wpost', 'Wrel', 'per_dim_scale')}
    del _L0_attn_all

    def _L0_xattn_setup():
        import jax, jax.numpy as jnp
        import numpy as np
        DIM = 128
        HEADS = 16
        DHEAD = 64
        INNER = HEADS * DHEAD
        EPS = 1e-05

        def layer_norm(x, g, b):
            mu = jnp.mean(x, axis=-1, keepdims=True)
            var = jnp.mean(jnp.square(x - mu), axis=-1, keepdims=True)
            return (x - mu) * jax.lax.rsqrt(var + EPS) * g + b

        def apply_rope(x, cos, sin):
            d2 = x.shape[-1] // 2
            x1, x2 = (x[..., :d2], x[..., d2:])
            return jnp.concatenate([x1 * cos - x2 * sin, x2 * cos + x1 * sin], axis=-1)
        key = jax.random.key(seed)
        ks = jax.random.split(key, 10)
        B, N, S = (8, 32, 512)
        latents = jax.random.normal(ks[0], (B, N, DIM), dtype=jnp.float32)
        context = jax.random.normal(ks[1], (B, S, DIM), dtype=jnp.float32)
        cos = jax.random.uniform(ks[2], (S, DHEAD // 2), dtype=jnp.float32)
        sin = jax.random.uniform(ks[3], (S, DHEAD // 2), dtype=jnp.float32)
        init = lambda k, shp, fan_in: jax.random.normal(k, shp, dtype=jnp.float32) / np.sqrt(fan_in)
        return {'latents': latents, 'context': context, 'cos': cos, 'sin': sin, 'ln_lat_g': jnp.ones((DIM,), jnp.float32), 'ln_lat_b': jnp.zeros((DIM,), jnp.float32), 'ln_ctx_g': jnp.ones((DIM,), jnp.float32), 'ln_ctx_b': jnp.zeros((DIM,), jnp.float32), 'Wq': init(ks[4], (DIM, INNER), DIM), 'Wkv': init(ks[5], (DIM, 2 * INNER), DIM), 'Wo': init(ks[6], (INNER, DIM), INNER), 'bo': jnp.zeros((DIM,), jnp.float32)}
    _L0_xattn_all = _L0_xattn_setup()
    _L0_xattn_in = {k: v for k, v in _L0_xattn_all.items() if k in ('cos', 'sin', 'ln_lat_g', 'ln_lat_b', 'ln_ctx_g', 'ln_ctx_b', 'Wq', 'Wkv', 'Wo', 'bo')}
    del _L0_xattn_all

    def _L0_ffn_setup():
        import jax, jax.numpy as jnp
        import numpy as np
        K = 3
        TAU = 1.0
        EPS = 1e-08

        def _route_dense(z, k, tau):
            topi = jax.lax.top_k(z, k)[1]
            topv = jnp.take_along_axis(z, topi, axis=1)
            w = jax.nn.softmax(topv / (tau + EPS), axis=1)
            N, L = z.shape
            dw = jnp.zeros((N, L), z.dtype)
            dw = dw.at[jnp.arange(N)[:, None], topi].add(w)
            return dw

        def _apply_mixture(x, dw, W):
            y = jnp.zeros((x.shape[0], W.shape[1]), x.dtype)
            for e in range(W.shape[0]):
                y = y + x @ W[e].T * dw[:, e:e + 1]
            return y
        key = jax.random.key(seed)
        ks = jax.random.split(key, 8)
        B, T, D_in, H, D_out, L, d_addr = (4, 256, 128, 512, 128, 12, 64)

        def unitize(U):
            U = U - U.mean(axis=1, keepdims=True)
            return U / (jnp.linalg.norm(U, axis=1, keepdims=True) + EPS)
        x = jax.random.normal(ks[0], (B, T, D_in), jnp.float32)
        P_w = jax.random.normal(ks[1], (d_addr, D_in), jnp.float32) / np.sqrt(D_in)
        U1 = unitize(jax.random.normal(ks[2], (L, d_addr), jnp.float32))
        U2 = unitize(jax.random.normal(ks[3], (L, d_addr), jnp.float32))
        U3 = unitize(jax.random.normal(ks[4], (L, d_addr), jnp.float32))
        W1 = jax.random.normal(ks[5], (L, H, D_in), jnp.float32)
        W1 = W1 / jnp.linalg.norm(W1.reshape(L, -1), axis=1)[:, None, None]
        W2 = jax.random.normal(ks[6], (L, D_out, H), jnp.float32)
        W2 = W2 / jnp.linalg.norm(W2.reshape(L, -1), axis=1)[:, None, None]
        b2 = jax.random.normal(ks[7], (L, D_out), jnp.float32)
        b2 = b2 / jnp.linalg.norm(b2, axis=1, keepdims=True)
        return {'x': x, 'P_w': P_w, 'U1': U1, 'U2': U2, 'U3': U3, 'W1': W1, 'W2': W2, 'b2': b2}
    _L0_ffn_all = _L0_ffn_setup()
    _L0_ffn_in = {k: v for k, v in _L0_ffn_all.items() if k in ('P_w', 'U1', 'U2', 'U3', 'W1', 'W2', 'b2')}
    del _L0_ffn_all
    return {'x': x, 'ctx_1024': ctx_1024, 'L0_attn_position_embeddings': _L0_attn_in['position_embeddings'], 'L0_attn_Wq': _L0_attn_in['Wq'], 'L0_attn_Wk': _L0_attn_in['Wk'], 'L0_attn_Wv': _L0_attn_in['Wv'], 'L0_attn_Wpost': _L0_attn_in['Wpost'], 'L0_attn_Wrel': _L0_attn_in['Wrel'], 'L0_attn_per_dim_scale': _L0_attn_in['per_dim_scale'], 'L0_xattn_cos': _L0_xattn_in['cos'], 'L0_xattn_sin': _L0_xattn_in['sin'], 'L0_xattn_ln_lat_g': _L0_xattn_in['ln_lat_g'], 'L0_xattn_ln_lat_b': _L0_xattn_in['ln_lat_b'], 'L0_xattn_ln_ctx_g': _L0_xattn_in['ln_ctx_g'], 'L0_xattn_ln_ctx_b': _L0_xattn_in['ln_ctx_b'], 'L0_xattn_Wq': _L0_xattn_in['Wq'], 'L0_xattn_Wkv': _L0_xattn_in['Wkv'], 'L0_xattn_Wo': _L0_xattn_in['Wo'], 'L0_xattn_bo': _L0_xattn_in['bo'], 'L0_ffn_P_w': _L0_ffn_in['P_w'], 'L0_ffn_U1': _L0_ffn_in['U1'], 'L0_ffn_U2': _L0_ffn_in['U2'], 'L0_ffn_U3': _L0_ffn_in['U3'], 'L0_ffn_W1': _L0_ffn_in['W1'], 'L0_ffn_W2': _L0_ffn_in['W2'], 'L0_ffn_b2': _L0_ffn_in['b2']}

def reference(x, ctx_1024, L0_attn_position_embeddings, L0_attn_Wq, L0_attn_Wk, L0_attn_Wv, L0_attn_Wpost, L0_attn_Wrel, L0_attn_per_dim_scale, L0_xattn_cos, L0_xattn_sin, L0_xattn_ln_lat_g, L0_xattn_ln_lat_b, L0_xattn_ln_ctx_g, L0_xattn_ln_ctx_b, L0_xattn_Wq, L0_xattn_Wkv, L0_xattn_Wo, L0_xattn_bo, L0_ffn_P_w, L0_ffn_U1, L0_ffn_U2, L0_ffn_U3, L0_ffn_W1, L0_ffn_W2, L0_ffn_b2):
    import jax
    import jax.numpy as jnp

    def _L0_attn_ref(hidden_states, position_embeddings, Wq, Wk, Wv, Wpost, Wrel, per_dim_scale):
        import math
        import jax, jax.numpy as jnp
        import numpy as np
        HID = 128
        H = 8
        D = HID // H
        CHUNK = 12
        PAST = 13 - 1
        FUT = 0
        CTX = CHUNK + PAST + FUT
        SOFTCAP = 50.0
        Q_SCALE = D ** (-0.5) / math.log(2)
        K_SCALE = math.log(1.0 + math.e) / math.log(2)

        def _extract_block_context(x, num_blocks):
            xp = jnp.pad(x, ((0, 0), (PAST, FUT + CHUNK - 1), (0, 0), (0, 0)))
            idx = jnp.arange(num_blocks)[:, None] * CHUNK + jnp.arange(CTX)[None, :]
            return xp[:, idx]

        def _rel_shift(x):
            B, Hh, nb, bs, pos_len = x.shape
            x = jnp.pad(x, ((0, 0), (0, 0), (0, 0), (0, 0), (0, CTX + 1 - pos_len)))
            x = x.reshape(B, Hh, nb, bs * (CTX + 1))[..., :bs * CTX]
            return x.reshape(B, Hh, nb, bs, CTX)
        B, S, _ = hidden_states.shape
        nb = (S + CHUNK - 1) // CHUNK
        pad = nb * CHUNK - S
        q = (hidden_states @ Wq.T).reshape(B, S, H, D)
        k = (hidden_states @ Wk.T).reshape(B, S, H, D)
        v = (hidden_states @ Wv.T).reshape(B, S, H, D)
        q = q * (Q_SCALE * jax.nn.softplus(per_dim_scale))
        k = k * K_SCALE
        q_blocked = jnp.pad(q, ((0, 0), (0, pad), (0, 0), (0, 0))).reshape(B, nb, CHUNK, H, D)
        k_ctx = _extract_block_context(k, nb)
        v_ctx = _extract_block_context(v, nb)
        matrix_ac = jnp.einsum('bnchd,bnkhd->bhnck', q_blocked, k_ctx)
        rel_k = (position_embeddings @ Wrel.T).reshape(-1, H, D)
        matrix_bd = jnp.einsum('bnchd,phd->bhncp', q_blocked, rel_k)
        matrix_bd = _rel_shift(matrix_bd)
        logits = matrix_ac + matrix_bd
        logits = jnp.tanh(logits / SOFTCAP) * SOFTCAP
        attn = jax.nn.softmax(logits, axis=-1)
        out = jnp.einsum('bhnck,bnkhd->bnchd', attn, v_ctx)
        out = out.reshape(B, nb * CHUNK, H * D)[:, :S]
        return out @ Wpost.T

    def _L0_xattn_ref(latents, context, cos, sin, ln_lat_g, ln_lat_b, ln_ctx_g, ln_ctx_b, Wq, Wkv, Wo, bo):
        import jax, jax.numpy as jnp
        import numpy as np
        DIM = 128
        HEADS = 16
        DHEAD = 64
        INNER = HEADS * DHEAD
        EPS = 1e-05

        def layer_norm(x, g, b):
            mu = jnp.mean(x, axis=-1, keepdims=True)
            var = jnp.mean(jnp.square(x - mu), axis=-1, keepdims=True)
            return (x - mu) * jax.lax.rsqrt(var + EPS) * g + b

        def apply_rope(x, cos, sin):
            d2 = x.shape[-1] // 2
            x1, x2 = (x[..., :d2], x[..., d2:])
            return jnp.concatenate([x1 * cos - x2 * sin, x2 * cos + x1 * sin], axis=-1)
        b, n, _ = latents.shape
        s = context.shape[1]
        lat = layer_norm(latents, ln_lat_g, ln_lat_b)
        ctx = layer_norm(context, ln_ctx_g, ln_ctx_b)
        q = (lat @ Wq).reshape(b, n, HEADS, DHEAD).transpose(0, 2, 1, 3)
        kv = ctx @ Wkv
        k, v = jnp.split(kv, 2, axis=-1)
        k = k.reshape(b, s, HEADS, DHEAD).transpose(0, 2, 1, 3)
        v = v.reshape(b, s, HEADS, DHEAD).transpose(0, 2, 1, 3)
        k = apply_rope(k, cos[None, None], sin[None, None])
        scale = DHEAD ** (-0.5)
        attn = jnp.einsum('bhnd,bhsd->bhns', q, k) * scale
        attn = jnp.clip(attn, -11.0, 11.0)
        attn = jax.nn.softmax(attn, axis=-1)
        out = jnp.einsum('bhns,bhsd->bhnd', attn, v)
        out = out.transpose(0, 2, 1, 3).reshape(b, n, INNER)
        return out @ Wo + bo

    def _L0_ffn_ref(x, P_w, U1, U2, U3, W1, W2, b2):
        import jax, jax.numpy as jnp
        import numpy as np
        K = 3
        TAU = 1.0
        EPS = 1e-08

        def _route_dense(z, k, tau):
            topi = jax.lax.top_k(z, k)[1]
            topv = jnp.take_along_axis(z, topi, axis=1)
            w = jax.nn.softmax(topv / (tau + EPS), axis=1)
            N, L = z.shape
            dw = jnp.zeros((N, L), z.dtype)
            dw = dw.at[jnp.arange(N)[:, None], topi].add(w)
            return dw

        def _apply_mixture(x, dw, W):
            y = jnp.zeros((x.shape[0], W.shape[1]), x.dtype)
            for e in range(W.shape[0]):
                y = y + x @ W[e].T * dw[:, e:e + 1]
            return y
        B, T, D = x.shape
        x_flat = x.reshape(B * T, D)
        x_addr = x_flat @ P_w.T
        dw1 = _route_dense(x_addr @ U1.T, K, TAU)
        dw2 = _route_dense(x_addr @ U2.T, K, TAU)
        dw3 = _route_dense(x_addr @ U3.T, K, TAU)
        h = _apply_mixture(x_flat, dw1, W1)
        h = jax.nn.gelu(h, approximate=False)
        y = _apply_mixture(h, dw2, W2)
        y = y + dw3 @ b2
        return y.reshape(B, T, -1)
    x = x + _L0_attn_ref(_layernorm(x, axis=-1), L0_attn_position_embeddings, L0_attn_Wq, L0_attn_Wk, L0_attn_Wv, L0_attn_Wpost, L0_attn_Wrel, L0_attn_per_dim_scale)
    x = x + _L0_xattn_ref(_layernorm(x, axis=-1), ctx_1024, L0_xattn_cos, L0_xattn_sin, L0_xattn_ln_lat_g, L0_xattn_ln_lat_b, L0_xattn_ln_ctx_g, L0_xattn_ln_ctx_b, L0_xattn_Wq, L0_xattn_Wkv, L0_xattn_Wo, L0_xattn_bo)
    x = x + _L0_ffn_ref(_layernorm(x, axis=-1), L0_ffn_P_w, L0_ffn_U1, L0_ffn_U2, L0_ffn_U3, L0_ffn_W1, L0_ffn_W2, L0_ffn_b2)
    return x

_drawn_inputs = setup_inputs


def setup_inputs(seed=0):
    import zlib

    import numpy as np

    out = dict(_drawn_inputs(seed))
    spreads = {'L0_attn_per_dim_scale': (0.0, 0.1),
     'L0_xattn_ln_lat_g': (1.0, 0.6),
     'L0_xattn_ln_lat_b': (0.0, 0.694),
     'L0_xattn_ln_ctx_g': (1.0, 0.2),
     'L0_xattn_ln_ctx_b': (0.0, 0.1),
     'L0_xattn_bo': (0.0, 0.1)}
    factors = {'L0_xattn_cos': 4.535,
     'L0_xattn_sin': 4.505,
     'L0_ffn_U1': 8.0,
     'L0_ffn_U2': 8.0,
     'L0_ffn_W1': 8.0,
     'L0_ffn_W2': 8.0}
    for name, (base, spread) in spreads.items():
        noise = np.random.default_rng([zlib.crc32(name.encode()), seed]).standard_normal(out[name].shape)
        drawn = base * np.exp(spread * noise) if base else spread * noise
        out[name] = jnp.asarray(drawn.astype(out[name].dtype))
    for name, factor in factors.items():
        out[name] = (out[name] * factor).astype(out[name].dtype)
    return out
```

```python
from contextlib import ExitStack

import numpy as np

import concourse.bass as bass
from concourse import mybir

P = 128
BANK = 512
F32 = mybir.dt.float32
F32R = mybir.dt.float32r
ALU = mybir.AluOpType
ACT = mybir.ActivationFunctionType
AX_X = mybir.AxisListType.X


def decoder_layer(nc, x, ctx_in, pos, a_wq, a_wk, a_wv, a_wpost, a_wrel, a_pds,
                  rope_cos, rope_sin, lat_g, lat_b, ctx_g, ctx_b, x_wq, x_wkv, x_wo, x_bo,
                  f_pw, f_u1, f_u2, f_u3, f_w1, f_w2, f_b2, out):
    B, S, D = x.shape
    NT = B * S // P
    TPB = S // P
    HALF_TOK = B * S // 2
    EPS = 1e-5

    HA, CH, PAST = 8, 12, 12
    DA = D // HA
    CTX = CH + PAST
    NPOS = pos.shape[0]
    NB = -(-S // CH)
    SPAD = PAST + NB * CH
    G = 4
    GK = G * CTX
    RPAD = PAST + NPOS + CTX
    Q_SCALE = DA ** -0.5 / float(np.log(2))
    K_SCALE = float(np.log(1 + np.e) / np.log(2))
    CAP = 50.0
    VG = 4
    NV = B * NB // VG
    NVP = NV // 2

    SC = ctx_in.shape[1]
    KC = SC // P
    NCT = B * KC
    HX, DX = 16, 64
    HG = 8
    NG = B * HX // HG
    STEPS = B * HX
    GC = HG * DX
    PAIRS = HX // 2
    X_SCALE = DX ** -0.5
    E_LO, E_HI = float(np.exp(-11.0)), float(np.exp(11.0))
    UNITS = 2 * KC
    CHK = HX * DX // P

    NE, HID = f_w1.shape[0], f_w1.shape[1]
    HC = HID // P
    DADDR = f_pw.shape[0]
    NR, TOPK = 3, 3
    FILL = 8 - TOPK
    LOWEST, TAKEN = -3.0e38, 3.0e38
    RING = 4
    EG = BANK // D
    NEG = NE // EG

    assert B == 4 and S == 256 and D == P and SC == BANK and GC == BANK and NV % 2 == 0

    with ExitStack() as ctx:
        def sb(name, shape, dt=F32, where=ctx):
            return where.enter_context(nc.sbuf_tensor(name, shape, dt))

        def sem(name):
            return ctx.enter_context(nc.semaphore(name))

        psum = ctx.enter_context(nc.psum_tensor("psum", [P, 8, BANK], F32))

        def bank(i, parts=P):
            return psum[0:parts, i, :]

        ident = sb("ident", [P, P])
        mask8 = sb("mask8", [P, HA])
        mask4 = sb("mask4", [P, G])
        mask_kg = sb("mask_kg", [GK, G])
        mask_v = sb("mask_v", [GK, G, DA])
        neghalf = sb("neghalf", [P, NCT])
        x_sb = sb("x_sb", [P, NT, D])
        xn = sb("xn", [P, NT, D])
        LN_X, LN_C, LN_1, LN_2, LN_F = 0, NT, NT + NCT, NT + NCT + 2, NT + NCT + 2 * NT
        NSTAT = LN_F + NT
        stats = sb("stats", [P, NSTAT, 6])
        mv = sb("mv", [P, NSTAT, 2])
        veps = sb("veps", [P, NSTAT])
        rstd = sb("rstd", [P, NSTAT])
        affine = sb("affine", [P, 4])
        bo_all = sb("bo_all", [P, D])

        cross = ExitStack()
        ctx_sb = sb("ctx_sb", [P, NCT, D], F32, cross)
        ctx_f = sb("ctx_f", [P, SC], F32, cross)
        ctx_hi = sb("ctx_hi", [P, 2, SC], F32R, cross)
        ctx_lo = sb("ctx_lo", [P, 2, SC], F32R, cross)
        raw = sb("raw", [P, 2, GC], F32, cross)
        rope_a = sb("rope_a", [P, 2, GC], F32, cross)
        rope_b = sb("rope_b", [P, 2, GC], F32, cross)
        k_f = sb("k_f", [P, 2, GC], F32, cross)
        wkv_hi = sb("wkv_hi", [P, 2 * HX * DX], F32R, cross)
        wkv_lo = sb("wkv_lo", [P, 2 * HX * DX], F32R, cross)
        wq_hi = sb("wq_hi", [P, HX, 2, DX], F32R, cross)
        wq_lo = sb("wq_lo", [P, HX, 2, DX], F32R, cross)
        wo_sb = sb("wo_sb", [P, CHK, D], F32, cross)
        cos_sb = sb("cos_sb", [P, KC, DX // 2], F32, cross)
        sin_sb = sb("sin_sb", [P, KC, 2, DX // 2], F32, cross)
        k_split = [sb("k_split0", [P, KC, HG, 2, DX], F32R, cross)]
        v_sb = [sb("v_sb0", [P, KC, HG, DX + 1], F32, cross)]

        first = ExitStack()
        xT = sb("xT", [P, B, S], F32, first)
        xT4 = sb("xT4", [P, B, SPAD, G], F32, first)
        aw = sb("aw", [P, 5, D], F32, first)
        awT = sb("awT", [P, 5, D], F32, first)
        pos_sb = sb("pos_sb", [NPOS, D], F32, first)
        posT = sb("posT", [P, NPOS], F32, first)
        pds = sb("pds", [P, 4], F32, first)
        relM = sb("relM", [P, RPAD, G], F32, first)
        qT = sb("qT", [P, B * S], F32, first)
        kM = sb("kM", [P, B, SPAD, G], F32, first)
        vbd = sb("vbd", [GK, B * NB // 2, D], F32, first)
        capped = sb("capped", [GK, 2, BANK], F32, first)
        pr = sb("pr", [GK, 2, B * S], F32, first)
        rec = sb("rec", [P, BANK], F32, first)
        oT = sb("oT", [P, B * S], F32, first)
        first.close()

        second = ExitStack()
        k_split.append(sb("k_split1", [P, KC, HG, 2, DX], F32R, second))
        v_sb.append(sb("v_sb1", [P, KC, HG, DX + 1], F32, second))
        lat_f = sb("lat_f", [P, BANK], F32, second)
        lat_hi = sb("lat_hi", [P, B * S], F32R, second)
        lat_lo = sb("lat_lo", [P, B * S], F32R, second)
        q_hi = sb("q_hi", [P, 2, 2 * S], F32R, second)
        q_lo = sb("q_lo", [P, 2, 2 * S], F32R, second)
        kT = sb("kT", [P, 3, SC], F32R, second)
        e_sb = sb("e_sb", [P, 3, KC * S], F32, second)
        den = sb("den", [P, 2, TPB], F32, second)
        o_sb = sb("o_sb", [P, 2, TPB, HX * DX], F32, second)
        oxT = sb("oxT", [P, CHK, P], F32, second)
        second.close()
        cross.close()

        third = ExitStack()
        w_raw = sb("w_raw", [P, RING, HC, P], F32, third)
        w1T_hi = sb("w1T_hi", [P, NE, HC, P], F32R, third)
        w1T_lo = sb("w1T_lo", [P, NE, HC, P], F32R, third)
        w2T_hi = sb("w2T_hi", [P, HC, NE, D], F32R, third)
        w2T_lo = sb("w2T_lo", [P, HC, NE, D], F32R, third)
        pw_sb = sb("pw_sb", [DADDR, D], F32, third)
        u_sb = sb("u_sb", [NR * NE, DADDR], F32, third)
        b2_sb = sb("b2_sb", [NE, D], F32, third)
        pwT = sb("pwT", [P, DADDR], F32, third)
        uT = sb("uT", [DADDR, NR * NE], F32, third)
        xnT = sb("xnT", [P, 4 * P], F32, third)
        addrT = sb("addrT", [DADDR, 4 * P], F32, third)
        z = sb("z", [P, 4 * NR, NE + FILL], F32, third)
        zr = sb("zr", [P, 4 * NR, NE + FILL], F32, third)
        top8 = sb("top8", [P, 4 * NR, 8], F32, third)
        top3 = sb("top3", [P, 4 * NR, 8], F32, third)
        chosen = sb("chosen", [P, 4 * NR, NE], F32, third)
        zsh = sb("zsh", [P, 4 * NR, NE], F32, third)
        ez = sb("ez", [P, 4 * NR, NE], F32, third)
        zsum = sb("zsum", [P, 4 * NR], F32, third)
        dw = sb("dw", [P, 2, 4, NR, NE], F32, third)
        dw3T = sb("dw3T", [NE, 4 * P], F32, third)
        xe = sb("xe", [P, 3, 4, P], F32, third)
        xeT_hi = sb("xeT_hi", [P, 3, 4 * P], F32R, third)
        xeT_lo = sb("xeT_lo", [P, 3, 4 * P], F32R, third)
        h_f = sb("h_f", [P, 2, 4 * P], F32, third)
        h_hi = sb("h_hi", [P, HC, 4 * P], F32R, third)
        h_lo = sb("h_lo", [P, HC, 4 * P], F32R, third)
        third.close()

        NAMES = """ld_x0 ld_x1 ld_aw ld_pos ld_pds ld_ctx0 ld_ctx1 ld_ctx2 ld_ctx3 ld_raw0 ld_raw1 ld_rope ld_affine ld_wo ld_bo stored
          consts chain_pool chain_dve chain_act stats_done mv_done rstd_done xn_done
          mask_done absneg_done softplus_done qscale_done
          awT_ps awT_done xT_ps xT_done xT4_done rel_ps relM_done q_ps k_ps qT_done kM_done vwin_ps vbd_done
          logit_ps capped_done prob_done oa_ps oT_done ya_ps x1_done
          w_hi_done w_lo_done ctxn_done sin_done ct_ps ctx_f_done ctx_hi_done ctx_lo_done
          unit_ps rope_done kf_done k_hi_done k_split_done v_done ones_done
          xn1_done lat_in_done lat_ps lat_f_done lat_hi_done lat_lo_done bo_added
          kt_ps kt_done qx_ps qx_hi_done qx_lo_done score_ps exp_done clip_done pv_ps den_done ox_done
          extra_ps turned_done x2_done
          ld_w0 ld_w1 ld_w2 ld_w3 ld_pw ld_u ld_b2 wt_ps wt_hi_done wt_lo_done rt_ps rt_done fn_done fT_ps fT_done
          addr_ps addr_done z_ps z_done fill_done top_done top3_done zr_done chosen_done zsh_done ez_done wsel_done zsum_done zrec_done dw_done
          dw3_ps dw3_done xe_done xeT_ps xeT_hi_done xeT_lo_done h_ps h_f_done h_hi_done h_lo_done y_ps y_done bias_ps bias_done x3_done""".split()
        s = {n: sem(n) for n in NAMES}
        block = ctx.enter_context(nc.Block())

        def kv_counts(m):
            k = KC * (m // UNITS) + min(m % UNITS, KC)
            return k, m - k

        extras = {}
        for b in range(B + 1):
            if b + 1 < B:
                extras[b * HX + 1] = ("context", b + 1)
            if b == 0:
                extras[5] = ("latents", 1)
            else:
                for t in range(TPB):
                    extras[b * HX + 3 + 6 * t] = ("turn", b - 1, t, 0)
                    extras[b * HX + 5 + 6 * t] = ("turn", b - 1, t, 1)
                    extras[b * HX + 7 + 6 * t] = ("project", b - 1, t)
        extras = dict(sorted(extras.items()))
        EXTRA_NO = {i: n for n, i in enumerate(extras)}

        def last_turn(b):
            return EXTRA_NO[(b + 1) * HX + 5 + 6 * (TPB - 1)] + 1

        @block.sync
        def _(sp):
            sp.dma_start(x_sb[:, 0:NT // 2, :], x[0:B // 2].rearrange("b (t p) d -> p (b t) d", p=P)).then_inc(s["ld_x0"], 16)
            for i, w in enumerate((a_wq, a_wk, a_wv, a_wpost, a_wrel)):
                sp.dma_start(aw[:, i, :], w).then_inc(s["ld_aw"], 16)
            sp.dma_start(x_sb[:, NT // 2:NT, :], x[B // 2:B].rearrange("b (t p) d -> p (b t) d", p=P)).then_inc(s["ld_x1"], 16)
            sp.dma_start(pos_sb[:, :], pos).then_inc(s["ld_pos"], 16)
            for b in range(B):
                sp.dma_start(ctx_sb[:, KC * b:KC * b + KC, :], ctx_in[b].rearrange("(t p) d -> p t d", p=P)).then_inc(s[f"ld_ctx{b}"], 16)
            sp.dma_start(cos_sb[:, :, :], rope_cos.rearrange("(t p) d -> p t d", p=P)).then_inc(s["ld_rope"], 16)
            sp.dma_start(sin_sb[:, :, 1, :], rope_sin.rearrange("(t p) d -> p t d", p=P)).then_inc(s["ld_rope"], 16)
            for c in range(6):
                if c >= 2:
                    sp.wait_ge(s["w_lo_done"], c - 1)
                src = x_wkv[:, c * GC:(c + 1) * GC] if c < 4 else x_wq[:, (c - 4) * GC:(c - 3) * GC]
                sp.dma_start(raw[:, c % 2, :], src).then_inc(s[f"ld_raw{c % 2}"], 16)
            sp.dma_start(wo_sb[:, :, :], x_wo.rearrange("(c p) n -> p c n", p=P)).then_inc(s["ld_wo"], 16)
            sp.wait_ge(s["x2_done"], NT)
            sp.dma_start(pw_sb[:, :], f_pw).then_inc(s["ld_pw"], 16)
            for i, u in enumerate((f_u1, f_u2, f_u3)):
                sp.dma_start(u_sb[i * NE:(i + 1) * NE, :], u).then_inc(s["ld_u"], 16)
            sp.dma_start(b2_sb[:, :], f_b2).then_inc(s["ld_b2"], 16)
            for n in range(2 * NE):
                if n >= RING:
                    sp.wait_ge(s["wt_ps"], n - RING + 1)
                src = f_w1[n].rearrange("(c p) d -> p c d", p=P) if n < NE else f_w2[n - NE].rearrange("o (c q) -> o c q", q=P)
                sp.dma_start(w_raw[:, n % RING, :, :], src).then_inc(s[f"ld_w{n % RING}"], 16)
            for t in range(NT):
                sp.wait_ge(s["x3_done"], t + 1)
                b, q = divmod(t, TPB)
                sp.dma_start(out[b, q * P:(q + 1) * P, :], x_sb[:, t, :]).then_inc(s["stored"], 16)
            sp.wait_ge(s["stored"], 16 * NT)

        @block.gpsimd
        def _(pool):
            count = [0]

            def link(ins):
                count[0] += 1
                ins.then_inc(s["chain_pool"], 1)
                pool.wait_ge(s["chain_pool"], count[0])

            def rstd_of(lo, n):
                pool.wait_ge(s["mv_done"], lo + n)
                link(pool.tensor_scalar(veps[:, lo:lo + n], mv[:, lo:lo + n, 1], EPS, None, ALU.add))
                pool.tensor_tensor(rstd[:, lo:lo + n], veps[:, lo:lo + n], neghalf[:, 0:n], ALU.pow).then_inc(s["rstd_done"], 1)

            link(pool.memset(ident[:, :], 0.0))
            link(pool.affine_select(out=ident[:, :], in_=ident[:, :], compare_op=ALU.not_equal, fill=1.0,
                                    base=0, pattern=[[-1, P]], channel_multiplier=1))
            pool.memset(neghalf[:, :], -0.5).then_inc(s["consts"], 1)
            link(pool.memset(mask8[:, :], 1.0))
            link(pool.affine_select(out=mask8[:, :], in_=mask8[:, :], compare_op=ALU.is_ge, fill=0.0,
                                    base=0, pattern=[[-DA, HA]], channel_multiplier=1))
            link(pool.affine_select(out=mask8[:, :], in_=mask8[:, :], compare_op=ALU.is_ge, fill=0.0,
                                    base=DA - 1, pattern=[[DA, HA]], channel_multiplier=-1))
            link(pool.tensor_tensor(mask4[:, :], mask8[:, 0:G], mask8[:, G:HA], ALU.add))
            pool.memset(xT4[:, :, 0:PAST, :], 0.0).then_inc(s["consts"], 1)
            pool.memset(xT4[:, :, PAST + S:SPAD, :], 0.0).then_inc(s["consts"], 1)
            pool.wait_ge(s["consts"], 1)
            rstd_of(LN_X, NT)
            pool.memset(kM[:, :, 0:PAST, :], 0.0).then_inc(s["consts"], 1)
            pool.memset(kM[:, :, PAST + S:SPAD, :], 0.0).then_inc(s["consts"], 1)
            pool.memset(relM[:, :, :], 0.0).then_inc(s["consts"], 1)
            pool.memset(v_sb[0][:, :, :, DX:DX + 1], 1.0).then_inc(s["consts"], 1)
            for b in range(B):
                sl = LN_C + KC * b
                rstd_of(sl, KC)
            for c in range(6):
                pool.wait_ge(s[f"ld_raw{c % 2}"], 16 * (c // 2 + 1))
                if c < 4:
                    pool.tensor_copy(wkv_hi[:, c * GC:(c + 1) * GC], raw[:, c % 2, :]).then_inc(s["w_hi_done"], 1)
                else:
                    pool.tensor_copy(wq_hi[:, (c - 4) * HG:(c - 3) * HG, 0, :], raw[:, c % 2, :].rearrange("p (h d) -> p h d", d=DX)).then_inc(s["w_hi_done"], 1)

            def context_hi(b):
                pool.wait_ge(s["ctx_f_done"], b + 1)
                pool.tensor_copy(ctx_hi[:, b % 2, :], ctx_f[:, :]).then_inc(s["ctx_hi_done"], 1)

            def key_unit(m):
                k, _ = kv_counts(m)
                g, t = divmod(m, UNITS)
                pool.wait_ge(s["rope_done"], k + 1)
                if k >= 2:
                    pool.wait_ge(s["k_split_done"], k - 1)
                pool.tensor_tensor(k_f[:, k % 2, :], rope_a[:, k % 2, :], rope_b[:, k % 2, :], ALU.add).then_inc(s["kf_done"], 1)
                pool.wait_ge(s["kf_done"], k + 1)
                if g >= 2:
                    pool.wait_ge(s["kt_ps"], HG * (g - 1))
                full = k_f[:, k % 2, :].rearrange("p (h d) -> p h d", d=DX)
                pool.tensor_copy(k_split[g % 2][:, t, :, 0, :], full).then_inc(s["k_hi_done"], 1)
                pool.wait_ge(s["k_hi_done"], k + 1)
                pool.tensor_tensor(k_split[g % 2][:, t, :, 1, :], full, k_split[g % 2][:, t, :, 0, :].bitcast(F32),
                                   ALU.subtract).then_inc(s["k_split_done"], 1)

            context_hi(0)
            for m in range(KC):
                key_unit(m)
            for pair in range(2):
                rstd_of(LN_1 + pair * NT, NT // 2)
                rstd_of(LN_1 + pair * NT + NT // 2, NT // 2)
                if pair == 0:
                    pool.wait_ge(s["lat_f_done"], 1)
                    pool.tensor_copy(lat_hi[:, 0:HALF_TOK], lat_f[:, :]).then_inc(s["lat_hi_done"], 1)
            pool.wait_ge(s["x1_done"], NT)
            pool.memset(v_sb[1][:, :, :, DX:DX + 1], 1.0).then_inc(s["ones_done"], 1)
            for i in range(STEPS):
                if extras.get(i, [0])[0] == "context":
                    context_hi(extras[i][1])
                if extras.get(i, [0])[0] == "latents":
                    pool.wait_ge(s["lat_f_done"], 2)
                    pool.tensor_copy(lat_hi[:, HALF_TOK:2 * HALF_TOK], lat_f[:, :]).then_inc(s["lat_hi_done"], 1)
                m = i + UNITS
                if m < NG * UNITS and m % UNITS < KC:
                    key_unit(m)

            pool.wait_ge(s["x2_done"], NT)
            pool.memset(z[:, :, NE:NE + FILL], LOWEST).then_inc(s["fill_done"], 1)
            pool.memset(top3[:, :, TOPK:8], LOWEST).then_inc(s["fill_done"], 1)
            for half in range(2):
                rstd_of(LN_F + 4 * half, 4)
            for half in range(2):
                for e in range(NE):
                    n = half * NE + e
                    if e == 0:
                        pool.wait_ge(s["dw_done"], half + 1)
                    if n >= 3:
                        pool.wait_ge(s["xeT_ps"], n - 2)
                    pool.tensor_tensor(xe[:, n % 3, :, :], xn[:, 4 * half:4 * half + 4, :],
                                       dw[:, half, :, 0, e, None].to_broadcast([P, 4, D]), ALU.mult).then_inc(s["xe_done"], 1)
                for c in range(HC):
                    n = half * HC + c
                    pool.wait_ge(s["h_f_done"], n + 1)
                    if half and c == 0:
                        pool.wait_ge(s["y_ps"], 4 * NEG)
                    pool.tensor_copy(h_hi[:, c, :], h_f[:, n % 2, :]).then_inc(s["h_hi_done"], 1)

        @block.scalar
        def _(act):
            for h in range(HA):
                act.dma_start(pds[h * DA:(h + 1) * DA, 0:1], a_pds.rearrange("(d o) -> d o", o=1)).then_inc(s["ld_pds"], 16)
            for i, v in enumerate((lat_g, lat_b, ctx_g, ctx_b)):
                act.dma_start(affine[:, i:i + 1], v.rearrange("(d o) -> d o", o=1)).then_inc(s["ld_affine"], 16)
            act.dma_start(bo_all[:, :], x_bo.partition_broadcast(P)).then_inc(s["ld_bo"], 16)
            act.wait_ge(s["absneg_done"], 1)
            act.activation(pds[:, 2:3], pds[:, 1:2], ACT.Exp).then_inc(s["chain_act"], 1)
            act.wait_ge(s["chain_act"], 1)
            act.activation(pds[:, 2:3], pds[:, 2:3], ACT.Ln, bias=1.0).then_inc(s["softplus_done"], 1)
            act.preload_act_table(ACT.Exp)
            act.wait_ge(s["awT_ps"], 1)
            act.activation(awT[:, 0:4, :].rearrange("p a b -> p (a b)"), bank(0), ACT.Copy).then_inc(s["awT_done"], 1)
            act.wait_ge(s["awT_ps"], 2)
            act.activation(awT[:, 4, :], psum[:, 1, 0:D], ACT.Copy).then_inc(s["awT_done"], 1)
            act.activation(posT[:, :], psum[:, 1, D:D + NPOS], ACT.Copy).then_inc(s["awT_done"], 1)
            for j in range(2):
                act.wait_ge(s["xT_ps"], j + 1)
                act.activation(xT[:, 2 * j:2 * j + 2, :], bank(2 + j).rearrange("p (a b) -> p a b", a=2), ACT.Copy).then_inc(s["xT_done"], 1)
                if j == 0:
                    act.wait_ge(s["consts"], 3)
                for b2 in range(2):
                    act.activation(xT4[:, 2 * j + b2, PAST:PAST + S, :],
                                   psum[:, 2 + j, S * b2:S * b2 + S, None].to_broadcast([P, S, G]), ACT.Copy).then_inc(s["xT4_done"], 1)
            act.wait_ge(s["qscale_done"], 1)
            for j in range(2):
                act.wait_ge(s["q_ps"], j + 1)
                act.activation(qT[:, BANK * j:BANK * (j + 1)], bank(4 + j), ACT.Copy, scale=pds[:, 3:4]).then_inc(s["qT_done"], 1)
            act.wait_ge(s["ld_affine"], 64)

            def context_f(b):
                if b >= 1:
                    act.wait_ge(s["ctx_lo_done"], b)
                act.activation(ctx_f[:, :], bank(3 if b == 0 else 7), ACT.Identity, scale=affine[:, 2:3], bias=affine[:, 3:4])\
                   .then_inc(s["ctx_f_done"], 1)

            act.wait_ge(s["ct_ps"], 1)
            context_f(0)

            def value_unit(m):
                _, v = kv_counts(m)
                g, w = divmod(m, UNITS)
                act.wait_ge(s["unit_ps"], m + 1)
                if g >= 2:
                    act.wait_ge(s["pv_ps"], HG * (g - 1))
                act.activation(v_sb[g % 2][:, w - KC, :, 0:DX], bank(3 if g == 0 else 5).rearrange("p (h d) -> p h d", d=DX),
                               ACT.Copy).then_inc(s["v_done"], 1)

            def local_softmax(j):
                bp, half = divmod(j, 2)
                act.wait_ge(s["logit_ps"], j + 1)
                act.activation(capped[:, j % 2, :], bank(4 + j, GK), ACT.Tanh, scale=1.0 / CAP).then_inc(s["capped_done"], 1)
                act.wait_ge(s["capped_done"], j + 1)
                act.activation(pr[:, half, BANK * bp:BANK * (bp + 1)], capped[:, j % 2, :], ACT.Exp, scale=CAP).then_inc(s["prob_done"], 1)

            for j in range(4):
                local_softmax(j)
                if j >= 2:
                    for m in (2 * j, 2 * j + 1):
                        value_unit(m)

            def latents_f(pair):
                if pair:
                    act.wait_ge(s["lat_lo_done"], pair)
                else:
                    act.wait_ge(s["x1_done"], NT)
                act.activation(lat_f[:, :], bank(7 if pair else 0), ACT.Identity, scale=affine[:, 0:1], bias=affine[:, 1:2])\
                   .then_inc(s["lat_f_done"], 1)

            act.wait_ge(s["lat_ps"], 1)
            latents_f(0)

            def keys_turned(i):
                act.wait_ge(s["kt_ps"], i + 1)
                if i >= 3:
                    act.wait_ge(s["score_ps"], i - 2)
                act.activation(kT[:, i % 3, :], bank(6), ACT.Copy).then_inc(s["kt_done"], 1)

            def queries_hi(j):
                act.wait_ge(s["qx_ps"], j + 1)
                if j >= 2:
                    act.wait_ge(s["score_ps"], 2 * (j - 1))
                act.activation(q_hi[:, j % 2, :], bank(7), ACT.Copy).then_inc(s["qx_hi_done"], 1)

            def exponent(i):
                act.wait_ge(s["score_ps"], i + 1)
                if i >= 3:
                    act.wait_ge(s["pv_ps"], i - 2)
                a = 2 * (i % 2)
                act.activation(e_sb[:, i % 3, :], psum[:, a:a + 2, :].rearrange("p a b -> p (a b)"), ACT.Exp, scale=X_SCALE)\
                   .then_inc(s["exp_done"], 1)

            def extra(i):
                what = extras[i]
                if what[0] == "project":
                    return
                act.wait_ge(s["extra_ps"], EXTRA_NO[i] + 1)
                if what[0] == "context":
                    context_f(what[1])
                elif what[0] == "latents":
                    latents_f(what[1])
                else:
                    _, b, t, part = what
                    n = CHK // 2
                    act.activation(oxT[:, n * part:n * part + n, :].rearrange("p c q -> p (c q)"), bank(7), ACT.Copy)\
                       .then_inc(s["turned_done"], 1)

            keys_turned(0)
            keys_turned(1)
            queries_hi(0)
            exponent(0)
            for i in range(STEPS):
                if i + 2 < STEPS:
                    keys_turned(i + 2)
                if i % 2 == 0 and i + 2 < STEPS:
                    queries_hi(i // 2 + 1)
                if i in extras:
                    extra(i)
                if i + 1 < STEPS:
                    exponent(i + 1)
                m = i + UNITS
                if m < NG * UNITS and m % UNITS >= KC:
                    value_unit(m)
            for i in extras:
                if i >= STEPS:
                    extra(i)

            def weights_hi(n):
                act.wait_ge(s["wt_ps"], n + 1)
                ps = bank(6 + n % 2).rearrange("p (c q) -> p c q", q=P)
                dst = w1T_hi[:, n, :, :] if n < NE else w2T_hi[:, :, n - NE, :]
                act.activation(dst, ps, ACT.Copy).then_inc(s["wt_hi_done"], 1)

            def router(half):
                act.wait_ge(s["fT_ps"], half + 1)
                act.activation(xnT[:, :], bank(4), ACT.Copy).then_inc(s["fT_done"], 1)
                act.wait_ge(s["addr_ps"], half + 1)
                act.activation(addrT[:, :], bank(5, DADDR), ACT.Copy).then_inc(s["addr_done"], 1)
                act.wait_ge(s["zsh_done"], half + 1)
                act.activation(ez[:, :, :], zsh[:, :, :], ACT.Exp).then_inc(s["ez_done"], 1)

            def router_bias(half):
                act.wait_ge(s["dw3_ps"], half + 1)
                act.activation(dw3T[:, :], bank(5, NE), ACT.Copy).then_inc(s["dw3_done"], 1)

            def expert_tokens_hi(n):
                act.wait_ge(s["xeT_ps"], n + 1)
                if n >= 3:
                    act.wait_ge(s["h_ps"], n - 2)
                act.activation(xeT_hi[:, n % 3, :], bank(4 + n % 2), ACT.Copy).then_inc(s["xeT_hi_done"], 1)

            act.wait_ge(s["rt_ps"], 1)
            act.activation(pwT[:, :], psum[:, 5, 0:DADDR], ACT.Copy).then_inc(s["rt_done"], 1)
            act.activation(uT[:, :], psum[0:DADDR, 5, P:P + NR * NE], ACT.Copy).then_inc(s["rt_done"], 1)
            for n in range(NE):
                weights_hi(n)
            router(0)
            router_bias(0)
            router(1)
            for half in range(2):
                for e in range(NE):
                    expert_tokens_hi(half * NE + e)
                    if half == 0:
                        weights_hi(NE + e)
                for c in range(HC):
                    n = half * HC + c
                    act.wait_ge(s["h_ps"], NE * (half + 1))
                    if n >= 2:
                        act.wait_ge(s["h_lo_done"], n - 1)
                    act.activation(h_f[:, n % 2, :], bank(c), ACT.Gelu).then_inc(s["h_f_done"], 1)
                if half == 0:
                    router_bias(1)

        @block.tensor
        def _(pe):
            pe.wait_ge(s["chain_pool"], 2)
            pe.wait_ge(s["ld_aw"], 80)
            for i in range(4):
                mm = pe.transpose(psum[:, 0, i * P:(i + 1) * P], aw[:, i, :], ident[:, :])
            mm.then_inc(s["awT_ps"], 1)
            pe.wait_ge(s["ld_pos"], 16)
            pe.transpose(psum[:, 1, 0:P], aw[:, 4, :], ident[:, :])
            pe.transpose(psum[:, 1, P:P + NPOS], pos_sb[:, :], ident[0:NPOS, 0:NPOS]).then_inc(s["awT_ps"], 1)
            for i in range(NT):
                pe.wait_ge(s["xn_done"], i + 1)
                mm = pe.transpose(psum[:, 2 + i // 4, (i % 4) * P:(i % 4 + 1) * P], xn[:, i, :], ident[:, :])
                if i % 4 == 3:
                    mm.then_inc(s["xT_ps"], 1)
            pe.wait_ge(s["awT_done"], 3)
            pe.matmul(psum[:, 1, 256:256 + NPOS], awT[:, 4, :], posT[:, :], start=True, stop=True).then_inc(s["rel_ps"], 1)
            for w, at, ps in ((0, 4, "q_ps"), (1, 6, "k_ps")):
                for j in range(2):
                    pe.wait_ge(s["xT_done"], j + 1)
                    pe.matmul(bank(at + j), awT[:, w, :], xT[:, 2 * j:2 * j + 2, :], start=True, stop=True).then_inc(s[ps], 1)

            def value_windows(u):
                if u >= 3:
                    pe.wait_ge(s["vbd_done"], u - 2)
                for i in range(VG):
                    b, n = divmod(VG * u + i, NB)
                    mm = pe.matmul(psum[0:GK, u % 3, i * D:(i + 1) * D],
                                   xT4[:, b, CH * n:CH * n + CTX, :].rearrange("p t g -> p (t g)"), awT[:, 2, :], start=True, stop=True)
                mm.then_inc(s["vwin_ps"], 1)

            def turn_context(b, at, done):
                pe.wait_ge(s["ctxn_done"], KC * (b + 1))
                for t in range(KC):
                    mm = pe.transpose(psum[:, at, t * P:(t + 1) * P], ctx_sb[:, KC * b + t, :], ident[:, :])
                mm.then_inc(s[done], 1)

            def unit(m):
                g, w = divmod(m, UNITS)
                b, hg = divmod(g, HX // HG)
                k, v = kv_counts(m)
                if m and (m - 1) % UNITS < KC:
                    pe.wait_ge(s["rope_done"], k)
                elif m:
                    pe.wait_ge(s["v_done"], v)
                pe.wait_ge(s["ctx_lo_done"], b + 1)
                wc = (0 if w < KC else HX * DX) + hg * GC
                if m < 2 * UNITS:
                    pe.wait_ge(s["w_lo_done"], wc // GC + 1)
                t = w % KC
                o = bank(3 if g == 0 else 5)
                hi, lo = (c[:, b % 2, t * P:(t + 1) * P] for c in (ctx_hi, ctx_lo))
                pe.matmul(o, hi, wkv_hi[:, wc:wc + GC], start=True, stop=False)
                pe.matmul(o, hi, wkv_lo[:, wc:wc + GC], start=False, stop=False)
                pe.matmul(o, lo, wkv_hi[:, wc:wc + GC], start=False, stop=True).then_inc(s["unit_ps"], 1)

            def local_logits(j, first_unit):
                bp, half = divmod(j, 2)
                r = slice(64 * half, 64 * half + 64)
                q3 = qT[r, BANK * bp:BANK * (bp + 1)].rearrange("p (b t) -> p b t", b=2)
                o3 = bank(4 + j, GK).rearrange("p (b t) -> p b t", b=2)
                for b2 in range(2):
                    b = 2 * bp + b2
                    for n in range(NB):
                        e = min(CH * (n + 1), S)
                        pe.matmul(o3[:, b2, CH * n:e], kM[r, b, CH * n:CH * n + CTX, :].rearrange("p t g -> p (t g)"),
                                  q3[:, b2, CH * n:e], start=(b2 + n == 0), stop=False, skip_group_check=True)
                    if b2 == 0:
                        unit(first_unit)
                for c in range(CH):
                    nn = len(range(c, S, CH))
                    mm = pe.matmul(o3[:, :, c:S:CH], relM[r, PAST - c:PAST - c + CTX, :].rearrange("p t g -> p (t g)"),
                                   q3[:, :, c:S:CH], start=False, stop=(c == CH - 1), skip_group_check=True)
                    if c:
                        at = PAST + NPOS - c
                        mm = pe.matmul(o3[:, :, c:S:CH], relM[r, at:at + CTX, :].rearrange("p t g -> p (t g)"),
                                       q3[:, :, c - 1:c + (nn - 1) * CH:CH], start=False, stop=(c == CH - 1), skip_group_check=True)
                mm.then_inc(s["logit_ps"], 1)
                unit(first_unit + 1)

            def local_values(bp):
                for half in range(2):
                    pe.wait_ge(s["prob_done"], 2 * bp + half + 1)
                    r = slice(64 * half, 64 * half + 64)
                    for b2 in range(2):
                        b = 2 * bp + b2
                        for n in range(NB):
                            e = min(CH * (n + 1), S)
                            pe.matmul(psum[r, 4 + 2 * bp, b2 * S + CH * n:b2 * S + e], vbd[:, b2 * NB + n, r],
                                      pr[:, half, b * S + CH * n:b * S + e], start=True, stop=True)
                    mm = pe.matmul(psum[r, 5 + 2 * bp, :], mask_v[:, :, :].rearrange("p g d -> p (g d)"),
                                   pr[:, half, BANK * bp:BANK * (bp + 1)], start=True, stop=True)
                mm.then_inc(s["oa_ps"], 1)

            def local_project(bp):
                pe.wait_ge(s["oT_done"], bp + 1)
                for i in range(4):
                    t = 4 * bp + i
                    mm = pe.matmul(psum[:, 4 + 2 * bp, i * D:(i + 1) * D], oT[:, t * P:(t + 1) * P], awT[:, 3, :], start=True, stop=True)
                mm.then_inc(s["ya_ps"], 1)

            def turn_latents(pair, at, done):
                for i in range(4):
                    t = 4 * pair + i
                    pe.wait_ge(s["lat_in_done"], t + 1)
                    mm = pe.transpose(psum[:, at, i * P:(i + 1) * P], xn[:, t, :], ident[:, :])
                mm.then_inc(s[done], 1)

            pe.wait_ge(s["xT4_done"], 4)
            pe.wait_ge(s["relM_done"], G)
            for u in range(3):
                value_windows(u)
            turn_context(0, 3, "ct_ps")
            for u in range(3, NVP):
                value_windows(u)
            pe.wait_ge(s["qT_done"], 2)
            pe.wait_ge(s["kM_done"], 2 * G)
            pe.wait_ge(s["ctx_f_done"], 1)
            for j in range(4):
                local_logits(j, 2 * j)
            pe.wait_ge(s["mask_done"], 2)
            pe.wait_ge(s["vbd_done"], NVP)
            local_values(0)
            for u in range(NVP, NV):
                value_windows(u)
            local_project(0)
            pe.wait_ge(s["vbd_done"], NV)
            local_values(1)
            turn_latents(0, 0, "lat_ps")
            local_project(1)

            def turn_keys(i):
                g, h = divmod(i, HG)
                pe.wait_ge(s["k_split_done"], KC * (g + 1))
                if i:
                    pe.wait_ge(s["kt_done"], i)
                for t in range(KC):
                    mm = pe.transpose(psum[:, 6, t * P:(t + 1) * P],
                                      k_split[g % 2][:, t, h, :, :].rearrange("p a d -> p (a d)").bitcast(F32), ident[:, :])
                mm.then_inc(s["kt_ps"], 1)

            def extra_read(n):
                if n:
                    done = list(extras.values())[:n]
                    what = done[-1]
                    if what[0] == "context":
                        pe.wait_ge(s["ctx_f_done"], what[1] + 1)
                    elif what[0] == "latents":
                        pe.wait_ge(s["lat_f_done"], 2)
                    elif what[0] == "turn":
                        pe.wait_ge(s["turned_done"], sum(w[0] == "turn" for w in done))
                    else:
                        pe.wait_ge(s["x2_done"], TPB * what[1] + what[2] + 1)

            def queries(j):
                b, pair = divmod(j, PAIRS)
                pe.wait_ge(s["lat_lo_done"], b // 2 + 1)
                if j < PAIRS:
                    pe.wait_ge(s["w_lo_done"], 5 + 2 * pair // HG)
                if j:
                    pe.wait_ge(s["qx_hi_done"], j)
                    pe.wait_ge(s["qx_lo_done"], j)
                extra_read(sum(e < 2 * j - 2 for e in extras))
                toks = slice(b * S, (b + 1) * S)
                for a in range(2):
                    h = 2 * pair + a
                    o = psum[:, 7, a * S:(a + 1) * S]
                    hi, lo = (w[:, h, :, :].rearrange("p a d -> p (a d)") for w in (wq_hi, wq_lo))
                    pe.matmul(o, hi, lat_hi[:, toks], start=True, stop=False)
                    pe.matmul(o, hi, lat_lo[:, toks], start=False, stop=False)
                    mm = pe.matmul(o, lo, lat_hi[:, toks], start=False, stop=True)
                mm.then_inc(s["qx_ps"], 1)

            def scores(i):
                pe.wait_ge(s["kt_done"], i + 1)
                pe.wait_ge(s["qx_hi_done"], i // 2 + 1)
                pe.wait_ge(s["qx_lo_done"], i // 2 + 1)
                if i >= 2:
                    pe.wait_ge(s["exp_done"], i - 1)
                for t in range(KC):
                    o = psum[:, 2 * (i % 2) + t // 2, (t % 2) * S:(t % 2 + 1) * S]
                    k = kT[:, i % 3, t * P:(t + 1) * P]
                    q = slice((i % 2) * S, (i % 2 + 1) * S)
                    pe.matmul(o, k, q_hi[:, (i // 2) % 2, q], start=True, stop=False)
                    mm = pe.matmul(o, k, q_lo[:, (i // 2) % 2, q], start=False, stop=True)
                mm.then_inc(s["score_ps"], 1)

            def weigh_values(i):
                g, h = divmod(i, HG)
                pe.wait_ge(s["clip_done"], i + 1)
                pe.wait_ge(s["v_done"], KC * (g + 1))
                if i == 0:
                    pe.wait_ge(s["consts"], 7)
                if i == HG:
                    pe.wait_ge(s["ones_done"], 1)
                if i:
                    pe.wait_ge(s["ox_done"], i)
                for q in range(TPB):
                    for t in range(KC):
                        mm = pe.matmul(psum[:, 4, q * (DX + 1):(q + 1) * (DX + 1)], e_sb[:, i % 3, t * S + q * P:t * S + (q + 1) * P],
                                       v_sb[g % 2][:, t, h, :], start=(t == 0), stop=(t == KC - 1))
                mm.then_inc(s["pv_ps"], 1)

            def extra(i):
                what, n = extras[i], EXTRA_NO[i]
                q = min((i + 1) // 2 + 1, STEPS // 2)
                pe.wait_ge(s["qx_hi_done"], q)
                pe.wait_ge(s["qx_lo_done"], q)
                extra_read(n)
                if what[0] == "context":
                    turn_context(what[1], 7, "extra_ps")
                elif what[0] == "latents":
                    turn_latents(what[1], 7, "extra_ps")
                elif what[0] == "turn":
                    _, b, t, part = what
                    if part == 0:
                        pe.wait_ge(s["ox_done"], HX * (b + 1))
                    for c in range(CHK // 2):
                        cc = part * CHK // 2 + c
                        mm = pe.transpose(psum[:, 7, c * P:(c + 1) * P], o_sb[:, b % 2, t, cc * P:(cc + 1) * P], ident[:, :])
                    mm.then_inc(s["extra_ps"], 1)
                else:
                    pe.wait_ge(s["ld_wo"], 16)
                    for c in range(CHK):
                        mm = pe.matmul(psum[:, 7, 0:D], oxT[:, c, :], wo_sb[:, c, :], start=(c == 0), stop=(c == CHK - 1))
                    mm.then_inc(s["extra_ps"], 1)

            pe.wait_ge(s["x1_done"], NT)
            pe.wait_ge(s["lat_f_done"], 1)
            turn_keys(0)
            queries(0)
            turn_keys(1)
            pe.wait_ge(s["v_done"], KC)
            scores(0)
            for i in range(STEPS):
                if i + 2 < STEPS:
                    turn_keys(i + 2)
                if i % 2 == 0 and i + 2 < STEPS:
                    queries(i // 2 + 1)
                if i in extras:
                    extra(i)
                if i + 1 < STEPS:
                    scores(i + 1)
                if i + UNITS < NG * UNITS:
                    unit(i + UNITS)
                weigh_values(i)
            for i in extras:
                if i >= STEPS:
                    extra(i)

            def turn_weights(n):
                pe.wait_ge(s[f"ld_w{n % RING}"], 16 * (n // RING + 1))
                if n >= 2:
                    pe.wait_ge(s["wt_lo_done"], n - 1)
                for c in range(HC):
                    mm = pe.transpose(psum[:, 6 + n % 2, c * P:(c + 1) * P], w_raw[:, n % RING, c, :], ident[:, :])
                mm.then_inc(s["wt_ps"], 1)

            def router(half):
                for i in range(4):
                    t = 4 * half + i
                    pe.wait_ge(s["fn_done"], t + 1)
                    mm = pe.transpose(psum[:, 4, i * P:(i + 1) * P], xn[:, t, :], ident[:, :])
                mm.then_inc(s["fT_ps"], 1)
                pe.wait_ge(s["fT_done"], half + 1)
                pe.matmul(bank(5, DADDR), pwT[:, :], xnT[:, :], start=True, stop=True).then_inc(s["addr_ps"], 1)
                pe.wait_ge(s["addr_done"], half + 1)
                for i in range(4):
                    mm = pe.matmul(psum[:, 4, i * NR * NE:(i + 1) * NR * NE], addrT[:, i * P:(i + 1) * P], uT[:, :], start=True, stop=True)
                mm.then_inc(s["z_ps"], 1)

            def router_bias(half):
                pe.wait_ge(s["dw_done"], half + 1)
                for i in range(4):
                    mm = pe.transpose(psum[0:NE, 5, i * P:(i + 1) * P], dw[:, half, i, 2, :], ident[:, :])
                mm.then_inc(s["dw3_ps"], 1)

            def bias_product(half):
                pe.wait_ge(s["dw3_done"], half + 1)
                pe.wait_ge(s["ld_b2"], 16)
                for i in range(4):
                    mm = pe.matmul(psum[:, 4, i * D:(i + 1) * D], dw3T[:, i * P:(i + 1) * P], b2_sb[:, :], start=True, stop=True)
                mm.then_inc(s["bias_ps"], 1)

            def turn_tokens(n):
                pe.wait_ge(s["xe_done"], n + 1)
                if n >= 2:
                    pe.wait_ge(s["xeT_lo_done"], n - 1)
                for i in range(4):
                    mm = pe.transpose(psum[:, 4 + n % 2, i * P:(i + 1) * P], xe[:, n % 3, i, :], ident[:, :])
                mm.then_inc(s["xeT_ps"], 1)

            def first_mixture(n):
                half, e = divmod(n, NE)
                pe.wait_ge(s["xeT_lo_done"], n + 1)
                if half == 0:
                    pe.wait_ge(s["wt_lo_done"], e + 1)
                if half and e == 0:
                    pe.wait_ge(s["h_f_done"], HC)
                hi, lo = xeT_hi[:, n % 3, :], xeT_lo[:, n % 3, :]
                for c in range(HC):
                    pe.matmul(bank(c), w1T_hi[:, e, c, :], hi, start=(e == 0), stop=False)
                    pe.matmul(bank(c), w1T_hi[:, e, c, :], lo, start=False, stop=False)
                    mm = pe.matmul(bank(c), w1T_lo[:, e, c, :], hi, start=False, stop=(e == NE - 1))
                mm.then_inc(s["h_ps"], 1)

            def second_mixture(half):
                pe.wait_ge(s["wt_lo_done"], 2 * NE)
                pe.wait_ge(s["h_lo_done"], HC * (half + 1))
                for i in range(4):
                    for eg in range(NEG):
                        n = (4 * half + i) * NEG + eg
                        if n >= 3:
                            pe.wait_ge(s["y_done"], EG * (n - 2))
                        es = slice(eg * EG, (eg + 1) * EG)
                        o = bank(5 + n % 3)
                        for c in range(HC):
                            hi, lo = (h[:, c, i * P:(i + 1) * P] for h in (h_hi, h_lo))
                            w_hi, w_lo = (w[:, c, es, :].rearrange("p e d -> p (e d)") for w in (w2T_hi, w2T_lo))
                            pe.matmul(o, hi, w_hi, start=(c == 0), stop=False)
                            pe.matmul(o, hi, w_lo, start=False, stop=False)
                            mm = pe.matmul(o, lo, w_hi, start=False, stop=(c == HC - 1))
                        mm.then_inc(s["y_ps"], 1)

            pe.wait_ge(s["ld_pw"], 16)
            pe.wait_ge(s["ld_u"], 48)
            pe.wait_ge(s["x2_done"], NT)
            pe.transpose(psum[:, 5, 0:DADDR], pw_sb[:, :], ident[0:DADDR, 0:DADDR])
            pe.transpose(psum[0:DADDR, 5, P:P + NR * NE], u_sb[:, :], ident[0:NR * NE, 0:NR * NE]).then_inc(s["rt_ps"], 1)
            for n in range(NE):
                turn_weights(n)
            pe.wait_ge(s["rt_done"], 2)
            router(0)
            router_bias(0)
            pe.wait_ge(s["z_done"], 1)
            router(1)
            pe.wait_ge(s["dw3_done"], 1)
            pe.wait_ge(s["z_done"], 2)
            bias_product(0)
            pe.wait_ge(s["bias_done"], 4)
            for half in range(2):
                if half:
                    router_bias(1)
                    bias_product(1)
                    pe.wait_ge(s["bias_done"], 8)
                turn_tokens(half * NE)
                for e in range(NE):
                    n = half * NE + e
                    if e + 1 < NE:
                        turn_tokens(n + 1)
                    if half == 0:
                        turn_weights(NE + e)
                    first_mixture(n)
                pe.wait_ge(s["xeT_lo_done"], NE * (half + 1))
                second_mixture(half)
                if half == 0:
                    pe.wait_ge(s["y_done"], 4 * NE)

        @block.vector
        def _(dve):
            count = [0]

            def link(ins):
                count[0] += 1
                ins.then_inc(s["chain_dve"], 1)
                dve.wait_ge(s["chain_dve"], count[0])

            def statistics(src, lo):
                n = len(src)
                for i, t in enumerate(src):
                    dve.bn_stats(stats[:, lo + i, :], t).then_inc(s["stats_done"], 1)
                dve.wait_ge(s["stats_done"], lo + n)
                for i in range(n):
                    dve.bn_aggr(mv[:, lo + i, :], stats[:, lo + i, :]).then_inc(s["mv_done"], 1)

            def normalize(out_, in_, slot):
                return dve.tensor_scalar(out_, in_, mv[:, slot, 0:1], rstd[:, slot:slot + 1], ALU.subtract, ALU.mult)

            dve.wait_ge(s["ld_x0"], 16)
            dve.wait_ge(s["ld_x1"], 16)
            statistics([x_sb[:, t, :] for t in range(NT)], LN_X)
            dve.wait_ge(s["ld_pds"], 16 * HA)
            dve.scalar_tensor_tensor(pds[:, 1:2], pds[:, 0:1], -1.0, pds[:, 0:1], ALU.mult, ALU.min).then_inc(s["absneg_done"], 1)
            dve.wait_ge(s["chain_pool"], 2)
            dve.tensor_reduce(mask_kg[:, :], ident[0:GK, 0:GK].rearrange("p (k g) -> p g k", g=G), AX_X, ALU.add).then_inc(s["mask_done"], 1)
            dve.wait_ge(s["mask_done"], 1)
            dve.tensor_copy(mask_v[:, :, :], mask_kg[:, :, None].to_broadcast([GK, G, DA])).then_inc(s["mask_done"], 1)
            dve.wait_ge(s["rstd_done"], 1)
            for t in range(NT):
                normalize(xn[:, t, :], x_sb[:, t, :], LN_X + t).then_inc(s["xn_done"], 1)
            for b in range(B):
                dve.wait_ge(s[f"ld_ctx{b}"], 16)
                statistics([ctx_sb[:, KC * b + t, :] for t in range(KC)], LN_C + KC * b)
            dve.wait_ge(s["softplus_done"], 1)
            link(dve.scalar_tensor_tensor(pds[:, 3:4], pds[:, 0:1], 0.0, pds[:, 2:3], ALU.max, ALU.add))
            dve.tensor_scalar(pds[:, 3:4], pds[:, 3:4], Q_SCALE, None, ALU.mult).then_inc(s["qscale_done"], 1)
            dve.wait_ge(s["rel_ps"], 1)
            dve.wait_ge(s["chain_pool"], 6)
            dve.wait_ge(s["consts"], 6)
            for g in range(G):
                dve.tensor_scalar(relM[:, PAST:PAST + NPOS, g], psum[:, 1, 256:256 + NPOS], mask4[:, g:g + 1], None, ALU.mult)\
                   .then_inc(s["relM_done"], 1)
            for j in range(2):
                dve.wait_ge(s["k_ps"], j + 1)
                for g in range(G):
                    dve.tensor_scalar(kM[:, 2 * j:2 * j + 2, PAST:PAST + S, g], bank(6 + j).rearrange("p (a b) -> p a b", a=2),
                                      mask4[:, g:g + 1], K_SCALE, ALU.mult, ALU.mult).then_inc(s["kM_done"], 1)

            def values_masked(u):
                dve.wait_ge(s["vwin_ps"], u + 1)
                if u == NVP:
                    dve.wait_ge(s["oa_ps"], 1)
                at = VG * (u % NVP)
                dve.tensor_tensor(vbd[:, at:at + VG, :].rearrange("p n (h e) -> p (n h) e", h=2),
                                  bank(u % 3, GK).rearrange("p (n e) -> p n e", e=G * DA),
                                  mask_v[:, :, :].rearrange("p g d -> p (g d)")[:, None, :].to_broadcast([GK, 2 * VG, G * DA]),
                                  ALU.mult).then_inc(s["vbd_done"], 1)

            def weight_lo(c):
                dve.wait_ge(s["w_hi_done"], c + 1)
                if c < 4:
                    cols = slice(c * GC, (c + 1) * GC)
                    dve.tensor_tensor(wkv_lo[:, cols], raw[:, c % 2, :], wkv_hi[:, cols].bitcast(F32), ALU.subtract).then_inc(s["w_lo_done"], 1)
                else:
                    heads = slice((c - 4) * HG, (c - 3) * HG)
                    full = raw[:, c % 2, :].rearrange("p (h d) -> p h d", d=DX)
                    dve.tensor_copy(wq_hi[:, heads, 1, :], full)
                    for a in range(2):
                        ins = dve.tensor_tensor(wq_lo[:, heads, a, :], full, wq_hi[:, heads, 0, :].bitcast(F32), ALU.subtract)
                    ins.then_inc(s["w_lo_done"], 1)

            def context_lo(b):
                dve.wait_ge(s["ctx_hi_done"], b + 1)
                dve.tensor_tensor(ctx_lo[:, b % 2, :], ctx_f[:, :], ctx_hi[:, b % 2, :].bitcast(F32), ALU.subtract).then_inc(s["ctx_lo_done"], 1)

            def key_unit(m):
                k, _ = kv_counts(m)
                g, t = divmod(m, UNITS)
                dve.wait_ge(s["unit_ps"], m + 1)
                if k >= 2:
                    dve.wait_ge(s["kf_done"], k - 1)
                ps = bank(3 if g == 0 else 5)
                dve.tensor_tensor(rope_a[:, k % 2, :].rearrange("p (h d) -> p h d", d=DX // 2), ps.rearrange("p (h d) -> p h d", d=DX // 2),
                                  cos_sb[:, t, None, :].to_broadcast([P, 2 * HG, DX // 2]), ALU.mult)
                ph = ps.rearrange("p (h a d) -> p h a d", a=2, d=DX // 2)
                bh = rope_b[:, k % 2, :].rearrange("p (h a d) -> p h a d", a=2, d=DX // 2)
                for a in range(2):
                    ins = dve.tensor_tensor(bh[:, :, a, :], ph[:, :, 1 - a, :],
                                            sin_sb[:, t, a, None, :].to_broadcast([P, HG, DX // 2]), ALU.mult)
                ins.then_inc(s["rope_done"], 1)

            for u in range(3):
                values_masked(u)
            for b in range(B):
                dve.wait_ge(s["rstd_done"], 2 + b)
                for t in range(KC):
                    ct = KC * b + t
                    normalize(ctx_sb[:, ct, :], ctx_sb[:, ct, :], LN_C + ct).then_inc(s["ctxn_done"], 1)
            for u in range(3, NVP):
                values_masked(u)
                if u - 3 < 6:
                    weight_lo(u - 3)
                if u - 3 == 6:
                    context_lo(0)
            dve.wait_ge(s["ld_rope"], 32)
            dve.tensor_scalar(sin_sb[:, :, 0, :], sin_sb[:, :, 1, :], -1.0, None, ALU.mult).then_inc(s["sin_done"], 1)
            dve.wait_ge(s["sin_done"], 1)
            for m in range(KC):
                key_unit(m)

            def local_normalize(bp):
                dve.wait_ge(s["oa_ps"], bp + 1)
                link(dve.reciprocal(rec[:, :], bank(5 + 2 * bp)))
                dve.tensor_tensor(oT[:, BANK * bp:BANK * (bp + 1)], bank(4 + 2 * bp), rec[:, :], ALU.mult).then_inc(s["oT_done"], 1)

            def local_residual(bp):
                dve.wait_ge(s["ya_ps"], bp + 1)
                for i in range(4):
                    t = 4 * bp + i
                    dve.tensor_tensor(x_sb[:, t, :], psum[:, 4 + 2 * bp, i * D:(i + 1) * D], x_sb[:, t, :], ALU.add).then_inc(s["x1_done"], 1)
                dve.wait_ge(s["x1_done"], 4 * (bp + 1))

            def latents(pair):
                before = 1 + B + 2 * pair
                tiles = range(4 * pair, 4 * pair + 4)
                lo = LN_1 + pair * NT
                statistics([x_sb[:, t, :] for t in tiles], lo)
                dve.wait_ge(s["rstd_done"], before + 1)
                for i, t in enumerate(tiles):
                    normalize(xn[:, t, :], x_sb[:, t, :], lo + i).then_inc(s["xn1_done"], 1)
                dve.wait_ge(s["xn1_done"], 4 * (pair + 1))
                statistics([xn[:, t, :] for t in tiles], lo + 4)
                dve.wait_ge(s["ld_bo"], 16)
                for t in tiles:
                    dve.tensor_tensor(x_sb[:, t, :], x_sb[:, t, :], bo_all[:, :], ALU.add).then_inc(s["bo_added"], 1)
                dve.wait_ge(s["rstd_done"], before + 2)
                for i, t in enumerate(tiles):
                    normalize(xn[:, t, :], xn[:, t, :], lo + 4 + i).then_inc(s["lat_in_done"], 1)

            def latents_lo(pair):
                dve.wait_ge(s["lat_hi_done"], pair + 1)
                toks = slice(pair * HALF_TOK, (pair + 1) * HALF_TOK)
                dve.tensor_tensor(lat_lo[:, toks], lat_f[:, :], lat_hi[:, toks].bitcast(F32), ALU.subtract).then_inc(s["lat_lo_done"], 1)

            local_normalize(0)
            for u in range(NVP, NV):
                values_masked(u)
            local_residual(0)
            latents(0)
            local_normalize(1)
            local_residual(1)
            latents_lo(0)
            latents(1)

            def queries_lo(j):
                dve.wait_ge(s["qx_hi_done"], j + 1)
                dve.tensor_tensor(q_lo[:, j % 2, :], bank(7), q_hi[:, j % 2, :].bitcast(F32), ALU.subtract).then_inc(s["qx_lo_done"], 1)

            def clip(i):
                dve.wait_ge(s["exp_done"], i + 1)
                dve.tensor_scalar(e_sb[:, i % 3, :], e_sb[:, i % 3, :], E_LO, E_HI, ALU.max, ALU.min).then_inc(s["clip_done"], 1)

            def divide(i):
                b, h = divmod(i, HX)
                dve.wait_ge(s["pv_ps"], i + 1)
                ps = psum[:, 4, 0:TPB * (DX + 1)].rearrange("p (q d) -> p q d", d=DX + 1)
                dve.reciprocal(den[:, i % 2, :], ps[:, :, DX]).then_inc(s["den_done"], 1)
                dve.wait_ge(s["den_done"], i + 1)
                if h == 0 and b >= 2:
                    dve.wait_ge(s["extra_ps"], last_turn(b - 2))
                dve.tensor_tensor(o_sb[:, b % 2, :, h * DX:(h + 1) * DX], ps[:, :, 0:DX],
                                  den[:, i % 2, :, None].to_broadcast([P, TPB, DX]), ALU.mult).then_inc(s["ox_done"], 1)

            def extra(i):
                what = extras[i]
                if what[0] == "context":
                    context_lo(what[1])
                elif what[0] == "latents":
                    latents_lo(1)
                elif what[0] == "project":
                    _, b, t = what
                    tile = TPB * b + t
                    dve.wait_ge(s["extra_ps"], EXTRA_NO[i] + 1)
                    dve.tensor_tensor(x_sb[:, tile, :], psum[:, 7, 0:D], x_sb[:, tile, :], ALU.add).then_inc(s["x2_done"], 1)

            queries_lo(0)
            clip(0)
            for i in range(STEPS):
                if i % 2 == 0 and i + 2 < STEPS:
                    queries_lo(i // 2 + 1)
                if i in extras:
                    extra(i)
                clip_next = i + 1 < STEPS
                m = i + UNITS
                if m < NG * UNITS and m % UNITS < KC:
                    if clip_next:
                        clip(i + 1)
                    key_unit(m)
                elif clip_next:
                    clip(i + 1)
                divide(i)
            for i in extras:
                if i >= STEPS:
                    extra(i)

            def weights_lo(n):
                dve.wait_ge(s["wt_hi_done"], n + 1)
                ps = bank(6 + n % 2).rearrange("p (c q) -> p c q", q=P)
                hi, lo = (w1T_hi[:, n, :, :], w1T_lo[:, n, :, :]) if n < NE else (w2T_hi[:, :, n - NE, :], w2T_lo[:, :, n - NE, :])
                dve.tensor_tensor(lo, ps, hi.bitcast(F32), ALU.subtract).then_inc(s["wt_lo_done"], 1)

            def router(half):
                dve.wait_ge(s["z_ps"], half + 1)
                dve.tensor_copy(z[:, :, 0:NE], psum[:, 4, 0:4 * NR * NE].rearrange("p (r e) -> p r e", e=NE)).then_inc(s["z_done"], 1)
                dve.wait_ge(s["z_done"], half + 1)
                dve.wait_ge(s["fill_done"], 2)
                for r in range(4 * NR):
                    dve.max(top8[:, r, :], z[:, r, :]).then_inc(s["top_done"], 1)
                dve.wait_ge(s["top_done"], 4 * NR * (half + 1))
                dve.tensor_copy(top3[:, :, 0:TOPK], top8[:, :, 0:TOPK]).then_inc(s["top3_done"], 1)
                dve.tensor_tensor(zsh[:, :, :], z[:, :, 0:NE], top8[:, :, 0:1].to_broadcast([P, 4 * NR, NE]), ALU.subtract)\
                   .then_inc(s["zsh_done"], 1)
                dve.wait_ge(s["top3_done"], half + 1)
                for r in range(4 * NR):
                    dve.match_replace(zr[:, r, :], top3[:, r, :], z[:, r, :], TAKEN).then_inc(s["zr_done"], 1)
                dve.wait_ge(s["zr_done"], 4 * NR * (half + 1))
                dve.tensor_tensor(chosen[:, :, :], zr[:, :, 0:NE], z[:, :, 0:NE], ALU.not_equal).then_inc(s["chosen_done"], 1)
                dve.wait_ge(s["chosen_done"], half + 1)
                dve.wait_ge(s["ez_done"], half + 1)
                dve.tensor_tensor(chosen[:, :, :], chosen[:, :, :], ez[:, :, :], ALU.mult).then_inc(s["wsel_done"], 1)
                dve.wait_ge(s["wsel_done"], half + 1)
                dve.tensor_reduce(zsum[:, :], chosen[:, :, :], AX_X, ALU.add).then_inc(s["zsum_done"], 1)
                dve.wait_ge(s["zsum_done"], half + 1)
                dve.reciprocal(zsum[:, :], zsum[:, :]).then_inc(s["zrec_done"], 1)
                dve.wait_ge(s["zrec_done"], half + 1)
                dve.tensor_tensor(dw[:, half, :, :, :].rearrange("p i r e -> p (i r) e"), chosen[:, :, :],
                                  zsum[:, :, None].to_broadcast([P, 4 * NR, NE]), ALU.mult).then_inc(s["dw_done"], 1)

            def bias_add(half):
                dve.wait_ge(s["bias_ps"], half + 1)
                for i in range(4):
                    t = 4 * half + i
                    dve.tensor_tensor(x_sb[:, t, :], psum[:, 4, i * D:(i + 1) * D], x_sb[:, t, :], ALU.add).then_inc(s["bias_done"], 1)

            dve.wait_ge(s["x2_done"], NT)
            for half in range(2):
                statistics([x_sb[:, 4 * half + i, :] for i in range(4)], LN_F + 4 * half)
            for half in range(2):
                dve.wait_ge(s["rstd_done"], 1 + B + 4 + half + 1)
                for i in range(4):
                    t = 4 * half + i
                    normalize(xn[:, t, :], x_sb[:, t, :], LN_F + t).then_inc(s["fn_done"], 1)
            for n in range(NE):
                weights_lo(n)
            router(0)
            router(1)
            bias_add(0)
            for half in range(2):
                if half:
                    bias_add(1)
                for e in range(NE):
                    n = half * NE + e
                    dve.wait_ge(s["xeT_hi_done"], n + 1)
                    dve.tensor_tensor(xeT_lo[:, n % 3, :], bank(4 + n % 2), xeT_hi[:, n % 3, :].bitcast(F32), ALU.subtract)\
                       .then_inc(s["xeT_lo_done"], 1)
                    if half == 0:
                        weights_lo(NE + e)
                for c in range(HC):
                    n = half * HC + c
                    dve.wait_ge(s["h_hi_done"], n + 1)
                    dve.tensor_tensor(h_lo[:, c, :], h_f[:, n % 2, :], h_hi[:, c, :].bitcast(F32), ALU.subtract).then_inc(s["h_lo_done"], 1)
                if half == 0:
                    dve.wait_ge(s["bias_done"], 4)
                else:
                    dve.wait_ge(s["bias_done"], 8)
                for i in range(4):
                    t = 4 * half + i
                    for eg in range(NEG):
                        n = t * NEG + eg
                        dve.wait_ge(s["y_ps"], n + 1)
                        for j in range(EG):
                            e = eg * EG + j
                            ins = dve.scalar_tensor_tensor(x_sb[:, t, :], psum[:, 5 + n % 3, j * D:(j + 1) * D],
                                                           dw[:, half, i, 1, e:e + 1], x_sb[:, t, :], ALU.mult, ALU.add)
                            ins.then_inc(s["y_done"], 1)
                            dve.wait_ge(s["y_done"], n * EG + j + 1)
                    dve.sem_inc(s["x3_done"], 1)


_INS = ["x", "ctx_1024", "L0_attn_position_embeddings", "L0_attn_Wq", "L0_attn_Wk", "L0_attn_Wv",
        "L0_attn_Wpost", "L0_attn_Wrel", "L0_attn_per_dim_scale", "L0_xattn_cos", "L0_xattn_sin",
        "L0_xattn_ln_lat_g", "L0_xattn_ln_lat_b", "L0_xattn_ln_ctx_g", "L0_xattn_ln_ctx_b", "L0_xattn_Wq",
        "L0_xattn_Wkv", "L0_xattn_Wo", "L0_xattn_bo", "L0_ffn_P_w", "L0_ffn_U1", "L0_ffn_U2", "L0_ffn_U3",
        "L0_ffn_W1", "L0_ffn_W2", "L0_ffn_b2"]
_OUTS = [((4, 256, 128), "float32")]


def kernel(**inputs):
    import numpy as _np
    import concourse.bacc as _bacc
    from concourse import mybir as _mybir
    from concourse.bass_utils import run_bass_kernel_spmd as _run

    nc = _bacc.Bacc("TRN2", target_bir_lowering=False, num_devices=1)
    arrays, args = {}, []
    for name in _INS:
        a = _np.ascontiguousarray(inputs[name])
        arrays[f"in_{name}_dram"] = a
        args.append(nc.dram_tensor(f"in_{name}_dram", a.shape, _mybir.dt.from_np(a.dtype), kind="ExternalInput").ap())
    for i, (shape, dtype) in enumerate(_OUTS):
        dt = _mybir.dt.from_np(_np.dtype(dtype))
        args.append(nc.dram_tensor(f"out_{i}_dram", shape, dt, kind="ExternalOutput").ap())
    decoder_layer(nc, *args)
    r = _run(nc, [arrays], core_ids=[0])
    return r.results[0]["out_0_dram"]
```

```python
from contextlib import ExitStack

import numpy as np

import concourse.bass as bass
from concourse import mybir

P = 128
BANK = 512
F32 = mybir.dt.float32
F32R = mybir.dt.float32r
ALU = mybir.AluOpType
ACT = mybir.ActivationFunctionType
AX_X = mybir.AxisListType.X


def decoder_layer(nc, x, ctx_in, pos, a_wq, a_wk, a_wv, a_wpost, a_wrel, a_pds,
                  rope_cos, rope_sin, lat_g, lat_b, ctx_g, ctx_b, x_wq, x_wkv, x_wo, x_bo,
                  f_pw, f_u1, f_u2, f_u3, f_w1, f_w2, f_b2, out):
    B, S, D = x.shape
    NT = B * S // P
    TPB = S // P
    HALF_TOK = B * S // 2
    EPS = 1e-5

    HA, CH, PAST = 8, 12, 12
    DA = D // HA
    CTX = CH + PAST
    NPOS = pos.shape[0]
    NB = -(-S // CH)
    SPAD = PAST + NB * CH
    G = 4
    GK = G * CTX
    Q_SCALE = DA ** -0.5 / float(np.log(2))
    K_SCALE = float(np.log(1 + np.e) / np.log(2))
    CAP = 50.0
    VG = 4
    NV = B * NB // VG
    VRING = B * NB // 2

    SC = ctx_in.shape[1]
    KC = SC // P
    NCT = B * KC
    HX, DX = 16, 64
    HG = 8
    NG = B * HX // HG
    STEPS = B * HX
    GC = HG * DX
    PAIRS = HX // 2
    X_SCALE = DX ** -0.5
    E_LO, E_HI = float(np.exp(-11.0)), float(np.exp(11.0))
    UNITS = 2 * KC
    CHK = HX * DX // P

    NE, HID = f_w1.shape[0], f_w1.shape[1]
    HC = HID // P
    DADDR = f_pw.shape[0]
    NR, TOPK = 3, 3
    FILL = 8 - TOPK
    LOWEST, TAKEN = -3.0e38, 3.0e38
    RING = 4
    EG = BANK // D
    NEG = NE // EG

    assert B == 4 and S == 256 and D == P and SC == BANK and GC == BANK and VRING % VG == 0 and NPOS == CTX + 1

    with ExitStack() as ctx:
        def sb(name, shape, dt=F32, where=ctx):
            return where.enter_context(nc.sbuf_tensor(name, shape, dt))

        def sem(name):
            return ctx.enter_context(nc.semaphore(name))

        bd_dram = nc.dram_tensor("bd_dram", [CH, NPOS * G, B * 2 * NB], F32, kind="Internal").ap()
        psum = ctx.enter_context(nc.psum_tensor("psum", [P, 8, BANK], F32))

        def bank(i, parts=P):
            return psum[0:parts, i, :]

        ident = sb("ident", [P, P])
        mask8 = sb("mask8", [P, HA])
        mask4 = sb("mask4", [P, G])
        mask_kg = sb("mask_kg", [GK, G])
        mask_v = sb("mask_v", [GK, G, DA])
        neghalf = sb("neghalf", [P, NCT])
        x_sb = sb("x_sb", [P, NT, D])
        xn = sb("xn", [P, NT, D])
        LN_X, LN_C, LN_1, LN_2, LN_F = 0, NT, NT + NCT, NT + NCT + 2, NT + NCT + 2 * NT
        NSTAT = LN_F + NT
        stats = sb("stats", [P, NSTAT, 6])
        mv = sb("mv", [P, NSTAT, 2])
        veps = sb("veps", [P, NSTAT])
        rstd = sb("rstd", [P, NSTAT])
        affine = sb("affine", [P, 4])
        bo_all = sb("bo_all", [P, D])

        cross = ExitStack()
        ctx_sb = sb("ctx_sb", [P, NCT, D], F32, cross)
        ctx_f = sb("ctx_f", [P, SC], F32, cross)
        ctx_hi = sb("ctx_hi", [P, 2, SC], F32R, cross)
        ctx_lo = sb("ctx_lo", [P, 2, SC], F32R, cross)
        raw = sb("raw", [P, 2, GC], F32, cross)
        rope_a = sb("rope_a", [P, 2, GC], F32, cross)
        rope_b = sb("rope_b", [P, 2, GC], F32, cross)
        k_f = sb("k_f", [P, 2, GC], F32, cross)
        wkv_hi = sb("wkv_hi", [P, 2 * HX * DX], F32R, cross)
        wkv_lo = sb("wkv_lo", [P, 2 * HX * DX], F32R, cross)
        wq_hi = sb("wq_hi", [P, HX, 2, DX], F32R, cross)
        wq_lo = sb("wq_lo", [P, HX, 2, DX], F32R, cross)
        wo_sb = sb("wo_sb", [P, CHK, D], F32, cross)
        cos_sb = sb("cos_sb", [P, KC, DX // 2], F32, cross)
        sin_sb = sb("sin_sb", [P, KC, 2, DX // 2], F32, cross)
        k_split = [sb("k_split0", [P, KC, HG, 2, DX], F32R, cross)]
        v_sb = [sb("v_sb0", [P, KC, HG, DX + 1], F32, cross)]

        first = ExitStack()
        xT4 = sb("xT4", [P, B, SPAD, G], F32, first)
        aw = sb("aw", [P, 5, D], F32, first)
        awT = sb("awT", [P, 5, D], F32, first)
        pos_sb = sb("pos_sb", [NPOS, D], F32, first)
        posT = sb("posT", [P, NPOS], F32, first)
        pds_b = sb("pds_b", [P, 2, DA], F32, first)
        mask_d = sb("mask_d", [P, DA], F32, first)
        pds = sb("pds", [P, 4], F32, first)
        relM = sb("relM", [P, NPOS, G], F32, first)
        qM = sb("qM", [P, B, 2, S], F32, first)
        kM = sb("kM", [P, B, SPAD, G], F32, first)
        vbd = sb("vbd", [GK, VRING, D], F32, first)
        bd = sb("bd", [GK, CH, B, 2, NB], F32, first)
        pr = sb("pr", [GK, B, 2, S], F32, first)
        projected = ExitStack()
        xT = sb("xT", [P, B, S], F32, projected)
        bd_raw = sb("bd_raw", [NPOS * G, CH, B, 2, NB], F32, projected)
        projected.close()
        logits = sb("logits", [GK, 2, 2, S], F32, first)
        rec = sb("rec", [P, S], F32, first)
        oT = sb("oT", [P, B * S], F32, first)
        first.close()

        second = ExitStack()
        k_split.append(sb("k_split1", [P, KC, HG, 2, DX], F32R, second))
        v_sb.append(sb("v_sb1", [P, KC, HG, DX + 1], F32, second))
        lat_f = sb("lat_f", [P, BANK], F32, second)
        lat_hi = sb("lat_hi", [P, B * S], F32R, second)
        lat_lo = sb("lat_lo", [P, B * S], F32R, second)
        q_hi = sb("q_hi", [P, 2, 2 * S], F32R, second)
        q_lo = sb("q_lo", [P, 2, 2 * S], F32R, second)
        kT = sb("kT", [P, 3, SC], F32R, second)
        e_sb = sb("e_sb", [P, 3, KC * S], F32, second)
        den = sb("den", [P, 2, TPB], F32, second)
        o_sb = sb("o_sb", [P, 2, TPB, HX * DX], F32, second)
        oxT = sb("oxT", [P, CHK, P], F32, second)
        second.close()
        cross.close()

        third = ExitStack()
        w_raw = sb("w_raw", [P, RING, HC, P], F32, third)
        w1T_hi = sb("w1T_hi", [P, NE, HC, P], F32R, third)
        w1T_lo = sb("w1T_lo", [P, NE, HC, P], F32R, third)
        w2T_hi = sb("w2T_hi", [P, HC, NE, D], F32R, third)
        w2T_lo = sb("w2T_lo", [P, HC, NE, D], F32R, third)
        pw_sb = sb("pw_sb", [DADDR, D], F32, third)
        u_sb = sb("u_sb", [NR * NE, DADDR], F32, third)
        b2_sb = sb("b2_sb", [NE, D], F32, third)
        pwT = sb("pwT", [P, DADDR], F32, third)
        uT = sb("uT", [DADDR, NR * NE], F32, third)
        xnT = sb("xnT", [P, 4 * P], F32, third)
        addrT = sb("addrT", [DADDR, 4 * P], F32, third)
        z = sb("z", [P, 4 * NR, NE + FILL], F32, third)
        zr = sb("zr", [P, 4 * NR, NE + FILL], F32, third)
        top8 = sb("top8", [P, 4 * NR, 8], F32, third)
        top3 = sb("top3", [P, 4 * NR, 8], F32, third)
        chosen = sb("chosen", [P, 4 * NR, NE], F32, third)
        zsh = sb("zsh", [P, 4 * NR, NE], F32, third)
        ez = sb("ez", [P, 4 * NR, NE], F32, third)
        zsum = sb("zsum", [P, 4 * NR], F32, third)
        dw = sb("dw", [P, 2, 4, NR, NE], F32, third)
        dw3T = sb("dw3T", [NE, 4 * P], F32, third)
        xe = sb("xe", [P, 3, 4, P], F32, third)
        xeT_hi = sb("xeT_hi", [P, 3, 4 * P], F32R, third)
        xeT_lo = sb("xeT_lo", [P, 3, 4 * P], F32R, third)
        h_f = sb("h_f", [P, 2, 4 * P], F32, third)
        h_hi = sb("h_hi", [P, HC, 4 * P], F32R, third)
        h_lo = sb("h_lo", [P, HC, 4 * P], F32R, third)
        third.close()

        NAMES = """ld_x0 ld_x1 ld_aw ld_pos ld_pds pds_done ld_ctx0 ld_ctx1 ld_ctx2 ld_ctx3 ld_raw0 ld_raw1 ld_rope ld_affine ld_wo ld_bo bd_stored shifted stored
          consts chain_pool chain_dve chain_act stats_done mv_done rstd_done xn_done
          mask_done absneg_done softplus_done qscale_done
          awT_ps awT_done xT_ps xT_done xT4_done rel_ps relM_done q_ps k_ps qM_done kM_done vwin_ps vbd_done bd_ps bd_raw_done added_done
          logit_ps capped_done prob_done sum_ps oa_ps rec_done oT_done ya_ps x1_done
          w_hi_done w_lo_done ctxn_done sin_done ct_ps ctx_f_done ctx_hi_done ctx_lo_done
          unit_ps rope_done kf_done k_hi_done k_split_done v_done ones_done
          xn1_done lat_in_done lat_ps lat_f_done lat_hi_done lat_lo_done bo_added
          kt_ps kt_done qx_ps qx_hi_done qx_lo_done score_ps exp_done clip_done pv_ps den_done ox_done
          extra_ps turned_done x2_done
          ld_w0 ld_w1 ld_w2 ld_w3 ld_pw ld_u ld_b2 wt_ps wt_hi_done wt_lo_done rt_ps rt_done fn_done fT_ps fT_done
          addr_ps addr_done z_ps z_done fill_done top_done top3_done zr_done chosen_done zsh_done ez_done wsel_done zsum_done zrec_done dw_done
          dw3_ps dw3_done xe_done xeT_ps xeT_hi_done xeT_lo_done h_ps h_f_done h_hi_done h_lo_done y_ps y_done bias_ps bias_done x3_done""".split()
        s = {n: sem(n) for n in NAMES}
        block = ctx.enter_context(nc.Block())

        W_ORDER = (0, 2, 1, 3, 4, 5)

        def kv_counts(m):
            k = KC * (m // UNITS) + min(m % UNITS, KC)
            return k, m - k

        extras = {}
        for b in range(B + 1):
            if b + 1 < B:
                extras[b * HX + 1] = ("context", b + 1)
            if b == 0:
                extras[5] = ("latents", 1)
            else:
                for t in range(TPB):
                    extras[b * HX + 3 + 6 * t] = ("turn", b - 1, t, 0)
                    extras[b * HX + 5 + 6 * t] = ("turn", b - 1, t, 1)
                    extras[b * HX + 7 + 6 * t] = ("project", b - 1, t)
        extras = dict(sorted(extras.items()))
        EXTRA_NO = {i: n for n, i in enumerate(extras)}

        def last_turn(b):
            return EXTRA_NO[(b + 1) * HX + 5 + 6 * (TPB - 1)] + 1

        @block.sync
        def _(sp):
            sp.dma_start(x_sb[:, 0:NT // 2, :], x[0:B // 2].rearrange("b (t p) d -> p (b t) d", p=P)).then_inc(s["ld_x0"], 16)
            for i, w in enumerate((a_wq, a_wk, a_wv, a_wpost, a_wrel)):
                sp.dma_start(aw[:, i, :], w).then_inc(s["ld_aw"], 16)
            def load_context(b):
                sp.dma_start(ctx_sb[:, KC * b:KC * b + KC, :], ctx_in[b].rearrange("(t p) d -> p t d", p=P)).then_inc(s[f"ld_ctx{b}"], 16)
            load_context(0)
            for n, c in enumerate(W_ORDER):
                if n == 4:
                    for c0 in range(0, CH, CH // 2):
                        sp.wait_ge(s["bd_raw_done"], 2 * B)
                        sp.dma_start(bd_dram[c0:c0 + CH // 2].rearrange("c r w -> r c w"),
                                     bd_raw[:, c0:c0 + CH // 2, :, :, :].rearrange("r c b h n -> r c (b h n)")).then_inc(s["bd_stored"], 16)
                    sp.wait_ge(s["bd_stored"], 32)
                    rows = bd_dram.rearrange("c r w -> (c r) w")[0:CH * (NPOS - 1) * G]
                    sp.dma_start(bd[:, :, :, :, :].rearrange("r c b h n -> r c (b h n)"),
                                 rows.rearrange("(c r) w -> r c w", c=CH)).then_inc(s["shifted"], 16)
                if n >= 2:
                    sp.wait_ge(s["w_lo_done"], n - 1)
                src = x_wkv[:, c * GC:(c + 1) * GC] if c < 4 else x_wq[:, (c - 4) * GC:(c - 3) * GC]
                sp.dma_start(raw[:, n % 2, :], src).then_inc(s[f"ld_raw{n % 2}"], 16)
                if n == 1:
                    for i, v in enumerate((lat_g, lat_b, ctx_g, ctx_b)):
                        sp.dma_start(affine[:, i:i + 1], v.rearrange("(d o) -> d o", o=1)).then_inc(s["ld_affine"], 16)
                if n == 3:
                    sp.dma_start(cos_sb[:, :, :], rope_cos.rearrange("(t p) d -> p t d", p=P)).then_inc(s["ld_rope"], 16)
                    sp.dma_start(sin_sb[:, :, 1, :], rope_sin.rearrange("(t p) d -> p t d", p=P)).then_inc(s["ld_rope"], 16)
                    for b in range(1, B):
                        load_context(b)
                    sp.dma_start(bo_all[:, :], x_bo.partition_broadcast(P)).then_inc(s["ld_bo"], 16)
            sp.dma_start(wo_sb[:, :, :], x_wo.rearrange("(c p) n -> p c n", p=P)).then_inc(s["ld_wo"], 16)
            sp.wait_ge(s["x2_done"], NT)
            sp.dma_start(pw_sb[:, :], f_pw).then_inc(s["ld_pw"], 16)
            for i, u in enumerate((f_u1, f_u2, f_u3)):
                sp.dma_start(u_sb[i * NE:(i + 1) * NE, :], u).then_inc(s["ld_u"], 16)
            sp.dma_start(b2_sb[:, :], f_b2).then_inc(s["ld_b2"], 16)
            for n in range(2 * NE):
                if n >= RING:
                    sp.wait_ge(s["wt_ps"], n - RING + 1)
                src = f_w1[n].rearrange("(c p) d -> p c d", p=P) if n < NE else f_w2[n - NE].rearrange("o (c q) -> o c q", q=P)
                sp.dma_start(w_raw[:, n % RING, :, :], src).then_inc(s[f"ld_w{n % RING}"], 16)
            for t in range(NT):
                sp.wait_ge(s["x3_done"], t + 1)
                b, q = divmod(t, TPB)
                sp.dma_start(out[b, q * P:(q + 1) * P, :], x_sb[:, t, :]).then_inc(s["stored"], 16)
            sp.wait_ge(s["stored"], 16 * NT)

        @block.gpsimd
        def _(pool):
            count = [0]

            def link(ins):
                count[0] += 1
                ins.then_inc(s["chain_pool"], 1)
                pool.wait_ge(s["chain_pool"], count[0])

            def rstd_of(lo, n):
                pool.wait_ge(s["mv_done"], lo + n)
                link(pool.tensor_scalar(veps[:, lo:lo + n], mv[:, lo:lo + n, 1], EPS, None, ALU.add))
                pool.tensor_tensor(rstd[:, lo:lo + n], veps[:, lo:lo + n], neghalf[:, 0:n], ALU.pow).then_inc(s["rstd_done"], 1)

            link(pool.memset(ident[:, :], 0.0))
            link(pool.affine_select(out=ident[:, :], in_=ident[:, :], compare_op=ALU.not_equal, fill=1.0,
                                    base=0, pattern=[[-1, P]], channel_multiplier=1))
            pool.memset(neghalf[:, :], -0.5).then_inc(s["consts"], 1)
            link(pool.memset(mask8[:, :], 1.0))
            link(pool.affine_select(out=mask8[:, :], in_=mask8[:, :], compare_op=ALU.is_ge, fill=0.0,
                                    base=0, pattern=[[-DA, HA]], channel_multiplier=1))
            link(pool.affine_select(out=mask8[:, :], in_=mask8[:, :], compare_op=ALU.is_ge, fill=0.0,
                                    base=DA - 1, pattern=[[DA, HA]], channel_multiplier=-1))
            link(pool.tensor_tensor(mask4[:, :], mask8[:, 0:G], mask8[:, G:HA], ALU.add))
            pool.memset(xT4[:, :, 0:PAST, :], 0.0).then_inc(s["consts"], 1)
            pool.memset(xT4[:, :, PAST + S:SPAD, :], 0.0).then_inc(s["consts"], 1)
            pool.memset(kM[:, :, 0:PAST, :], 0.0).then_inc(s["consts"], 1)
            pool.memset(kM[:, :, PAST + S:SPAD, :], 0.0).then_inc(s["consts"], 1)
            for half in range(2):
                other = slice(64 - 64 * half, 128 - 64 * half)
                pool.wait_ge(s["consts"], 5 + half)
                pool.memset(qM[other, :, half, :], 0.0).then_inc(s["consts"], 1)
            pool.wait_ge(s["consts"], 7)
            pool.memset(bd_raw[:, :, :, :, NB - 1], 0.0).then_inc(s["consts"], 1)
            pool.memset(v_sb[0][:, :, :, DX:DX + 1], 1.0).then_inc(s["consts"], 1)
            rstd_of(LN_X, NT)
            rstd_of(LN_C, KC)

            def weight_rest(n):
                pool.wait_ge(s["w_hi_done"], n + 1)
                c = W_ORDER[n]
                if c < 4:
                    cols = slice(c * GC, (c + 1) * GC)
                    pool.tensor_tensor(wkv_lo[:, cols], raw[:, n % 2, :], wkv_hi[:, cols].bitcast(F32), ALU.subtract).then_inc(s["w_lo_done"], 1)
                else:
                    heads = slice((c - 4) * HG, (c - 3) * HG)
                    full = raw[:, n % 2, :].rearrange("p (h d) -> p h d", d=DX)
                    pool.tensor_tensor(wq_lo[:, heads, 0, :], full, wq_hi[:, heads, 0, :].bitcast(F32), ALU.subtract)
                    pool.tensor_tensor(wq_lo[:, heads, 1, :], full, wq_hi[:, heads, 1, :].bitcast(F32), ALU.subtract)\
                        .then_inc(s["w_lo_done"], 1)

            def key_sum(k):
                pool.wait_ge(s["rope_done"], k + 1)
                if k >= 2:
                    pool.wait_ge(s["k_split_done"], k - 1)
                pool.tensor_tensor(k_f[:, k % 2, :], rope_a[:, k % 2, :], rope_b[:, k % 2, :], ALU.add).then_inc(s["kf_done"], 1)

            def key_rest(k):
                g, t = divmod(k, KC)
                pool.wait_ge(s["k_hi_done"], k + 1)
                pool.tensor_tensor(k_split[g % 2][:, t, :, 1, :], k_f[:, k % 2, :].rearrange("p (h d) -> p h d", d=DX),
                                   k_split[g % 2][:, t, :, 0, :].bitcast(F32), ALU.subtract).then_inc(s["k_split_done"], 1)

            def key_step(m):
                if m and (m - 1) % UNITS < KC and (m - 1) // UNITS < NG:
                    k, _ = kv_counts(m - 1)
                    if m % UNITS < KC and m // UNITS < NG:
                        key_sum(k + 1)
                    key_rest(k)
                elif m % UNITS < KC and m // UNITS < NG:
                    key_sum(kv_counts(m)[0])

            for n in range(4):
                weight_rest(n)
            for m in range(KC + 1):
                key_step(m)
            for n in range(4, 6):
                weight_rest(n)
            for b in range(1, B):
                rstd_of(LN_C + KC * b, KC)
            for pair in range(2):
                rstd_of(LN_1 + pair * NT, NT // 2)
                rstd_of(LN_1 + pair * NT + NT // 2, NT // 2)
                if pair == 0:
                    pool.wait_ge(s["lat_f_done"], 1)
                    pool.tensor_copy(lat_hi[:, 0:HALF_TOK], lat_f[:, :]).then_inc(s["lat_hi_done"], 1)
            pool.wait_ge(s["x1_done"], NT)
            pool.memset(v_sb[1][:, :, :, DX:DX + 1], 1.0).then_inc(s["ones_done"], 1)
            for i in range(STEPS):
                if extras.get(i, [0])[0] == "latents":
                    pool.wait_ge(s["lat_f_done"], 2)
                    pool.tensor_copy(lat_hi[:, HALF_TOK:2 * HALF_TOK], lat_f[:, :]).then_inc(s["lat_hi_done"], 1)
                key_step(i + UNITS)

            pool.wait_ge(s["x2_done"], NT)
            pool.memset(z[:, :, NE:NE + FILL], LOWEST).then_inc(s["fill_done"], 1)
            pool.memset(top3[:, :, TOPK:8], LOWEST).then_inc(s["fill_done"], 1)
            for half in range(2):
                rstd_of(LN_F + 4 * half, 4)
            for half in range(2):
                for e in range(NE):
                    n = half * NE + e
                    if e == 0:
                        pool.wait_ge(s["dw_done"], half + 1)
                    if n >= 3:
                        pool.wait_ge(s["xeT_ps"], n - 2)
                    pool.tensor_tensor(xe[:, n % 3, :, :], xn[:, 4 * half:4 * half + 4, :],
                                       dw[:, half, :, 0, e, None].to_broadcast([P, 4, D]), ALU.mult).then_inc(s["xe_done"], 1)
                for c in range(HC):
                    n = half * HC + c
                    pool.wait_ge(s["h_f_done"], n + 1)
                    if half and c == 0:
                        pool.wait_ge(s["y_ps"], 4 * NEG)
                    pool.tensor_copy(h_hi[:, c, :], h_f[:, n % 2, :]).then_inc(s["h_hi_done"], 1)

        @block.scalar
        def _(act):
            act.dma_start(x_sb[:, NT // 2:NT, :], x[B // 2:B].rearrange("b (t p) d -> p (b t) d", p=P)).then_inc(s["ld_x1"], 16)
            act.dma_start(pds_b[:, 0, :], a_pds.partition_broadcast(P)).then_inc(s["ld_pds"], 16)
            act.dma_start(pos_sb[:, :], pos).then_inc(s["ld_pos"], 16)
            act.preload_act_table(ACT.Exp)
            def weight_hi(n):
                act.wait_ge(s[f"ld_raw{n % 2}"], 16 * (n // 2 + 1))
                c = W_ORDER[n]
                if c < 4:
                    act.activation(wkv_hi[:, c * GC:(c + 1) * GC], raw[:, n % 2, :], ACT.Copy).then_inc(s["w_hi_done"], 1)
                else:
                    heads = slice((c - 4) * HG, (c - 3) * HG)
                    full = raw[:, n % 2, :].rearrange("p (h d) -> p h d", d=DX)
                    act.activation(wq_hi[:, heads, 0, :], full, ACT.Copy)
                    act.activation(wq_hi[:, heads, 1, :], full, ACT.Copy).then_inc(s["w_hi_done"], 1)

            act.wait_ge(s["absneg_done"], 1)
            act.activation(pds[:, 2:3], pds[:, 1:2], ACT.Exp).then_inc(s["chain_act"], 1)
            act.wait_ge(s["chain_act"], 1)
            act.activation(pds[:, 2:3], pds[:, 2:3], ACT.Ln, bias=1.0).then_inc(s["softplus_done"], 1)
            act.preload_act_table(ACT.Exp)
            act.wait_ge(s["awT_ps"], 1)
            act.activation(awT[:, 0:4, :].rearrange("p a b -> p (a b)"), bank(0), ACT.Copy).then_inc(s["awT_done"], 1)
            act.wait_ge(s["awT_ps"], 2)
            act.activation(awT[:, 4, :], psum[:, 1, 0:D], ACT.Copy).then_inc(s["awT_done"], 1)
            act.activation(posT[:, :], psum[:, 1, D:D + NPOS], ACT.Copy).then_inc(s["awT_done"], 1)
            for j in range(2):
                act.wait_ge(s["xT_ps"], j + 1)
                act.activation(xT[:, 2 * j:2 * j + 2, :], bank(2 + j).rearrange("p (a b) -> p a b", a=2), ACT.Copy).then_inc(s["xT_done"], 1)
            act.wait_ge(s["consts"], 3)

            def replicate(b):
                act.wait_ge(s["xT_done"], b // 2 + 1)
                act.activation(xT4[:, b, PAST:PAST + S, :], xT[:, b, :, None].to_broadcast([P, S, G]), ACT.Copy).then_inc(s["xT4_done"], 1)

            replicate(0)
            act.wait_ge(s["consts"], 8)
            act.wait_ge(s["qscale_done"], 1)
            for j in range(2):
                act.wait_ge(s["q_ps"], j + 1)
                for half in range(2):
                    r = slice(64 * half, 64 * half + 64)
                    act.activation(qM[r, 2 * j:2 * j + 2, half, :], psum[r, 4 + j, :].rearrange("p (b t) -> p b t", b=2),
                                   ACT.Copy, scale=pds[r, 3:4]).then_inc(s["qM_done"], 1)
            weight_hi(0)
            full, tail = NB - 1, S - (NB - 1) * CH
            for b in range(B):
                act.wait_ge(s["bd_ps"], b + 1)
                ps = psum[0:NPOS * G, 4 + b, :].rearrange("p (h t) -> p h t", h=2)
                act.activation(bd_raw[:, :, b, :, 0:full].rearrange("p c h n -> p h n c"),
                               ps[:, :, 0:full * CH].rearrange("p h (n c) -> p h n c", c=CH), ACT.Copy).then_inc(s["bd_raw_done"], 1)
                act.activation(bd_raw[:, 0:tail, b, :, full].rearrange("p c h -> p h c"), ps[:, :, full * CH:S], ACT.Copy)\
                   .then_inc(s["bd_raw_done"], 1)
                if b == 0:
                    weight_hi(1)
                if b == 1:
                    replicate(1)
            act.wait_ge(s["ld_affine"], 64)

            def context_f(b):
                if b >= 1:
                    act.wait_ge(s["ctx_lo_done"], b)
                act.activation(ctx_f[:, :], bank(3 if b == 0 else 7), ACT.Identity, scale=affine[:, 2:3], bias=affine[:, 3:4])\
                   .then_inc(s["ctx_f_done"], 1)
                act.wait_ge(s["ctx_f_done"], b + 1)
                act.activation(ctx_hi[:, b % 2, :], ctx_f[:, :], ACT.Copy).then_inc(s["ctx_hi_done"], 1)

            act.wait_ge(s["ct_ps"], 1)
            context_f(0)
            for n in range(2, 4):
                weight_hi(n)
            for b in range(2, B):
                replicate(b)

            def value_unit(m):
                _, v = kv_counts(m)
                g, w = divmod(m, UNITS)
                act.wait_ge(s["unit_ps"], m + 1)
                if g >= 2:
                    act.wait_ge(s["pv_ps"], HG * (g - 1))
                act.activation(v_sb[g % 2][:, w - KC, :, 0:DX], bank(3 if g == 0 else 5).rearrange("p (h d) -> p h d", d=DX),
                               ACT.Copy).then_inc(s["v_done"], 1)

            def key_hi(k):
                g, t = divmod(k, KC)
                act.wait_ge(s["kf_done"], k + 1)
                if g >= 2:
                    act.wait_ge(s["kt_ps"], HG * (g - 1))
                act.activation(k_split[g % 2][:, t, :, 0, :], k_f[:, k % 2, :].rearrange("p (h d) -> p h d", d=DX), ACT.Copy)\
                   .then_inc(s["k_hi_done"], 1)

            def local_softmax(b):
                act.wait_ge(s["added_done"], 2 * (b + 1))
                at = logits[:, b % 2, :, :]
                act.activation(at, at, ACT.Tanh, scale=1.0 / CAP).then_inc(s["capped_done"], 1)
                act.wait_ge(s["capped_done"], b + 1)
                act.activation(pr[:, b, :, :], at, ACT.Exp, scale=CAP).then_inc(s["prob_done"], 1)

            for k in range(KC):
                key_hi(k)
            for b in range(B):
                if b < 2:
                    value_unit(KC + 2 * b)
                    value_unit(KC + 2 * b + 1)
                local_softmax(b)
                if b >= 2:
                    weight_hi(b + 2)

            def latents_f(pair):
                if pair:
                    act.wait_ge(s["lat_lo_done"], pair)
                else:
                    act.wait_ge(s["x1_done"], NT)
                act.activation(lat_f[:, :], bank(7 if pair else 0), ACT.Identity, scale=affine[:, 0:1], bias=affine[:, 1:2])\
                   .then_inc(s["lat_f_done"], 1)

            act.wait_ge(s["lat_ps"], 1)
            latents_f(0)

            def keys_turned(i):
                act.wait_ge(s["kt_ps"], i + 1)
                if i >= 3:
                    act.wait_ge(s["score_ps"], i - 2)
                act.activation(kT[:, i % 3, :], bank(6), ACT.Copy).then_inc(s["kt_done"], 1)

            def queries_hi(j):
                act.wait_ge(s["qx_ps"], j + 1)
                if j >= 2:
                    act.wait_ge(s["score_ps"], 2 * (j - 1))
                act.activation(q_hi[:, j % 2, :], bank(7), ACT.Copy).then_inc(s["qx_hi_done"], 1)

            def exponent(i):
                act.wait_ge(s["score_ps"], i + 1)
                if i >= 3:
                    act.wait_ge(s["pv_ps"], i - 2)
                a = 2 * (i % 2)
                act.activation(e_sb[:, i % 3, :], psum[:, a:a + 2, :].rearrange("p a b -> p (a b)"), ACT.Exp, scale=X_SCALE)\
                   .then_inc(s["exp_done"], 1)

            def extra(i):
                what = extras[i]
                if what[0] == "project":
                    return
                act.wait_ge(s["extra_ps"], EXTRA_NO[i] + 1)
                if what[0] == "context":
                    context_f(what[1])
                elif what[0] == "latents":
                    latents_f(what[1])
                else:
                    _, b, t, part = what
                    n = CHK // 2
                    act.activation(oxT[:, n * part:n * part + n, :].rearrange("p c q -> p (c q)"), bank(7), ACT.Copy)\
                       .then_inc(s["turned_done"], 1)

            keys_turned(0)
            keys_turned(1)
            queries_hi(0)
            exponent(0)
            for i in range(STEPS):
                if i + 2 < STEPS:
                    keys_turned(i + 2)
                if i % 2 == 0 and i + 2 < STEPS:
                    queries_hi(i // 2 + 1)
                if i in extras:
                    extra(i)
                if i + 1 < STEPS:
                    exponent(i + 1)
                m = i + UNITS
                if (m - 1) // UNITS < NG and (m - 1) % UNITS < KC:
                    key_hi(kv_counts(m - 1)[0])
                if m < NG * UNITS and m % UNITS >= KC:
                    value_unit(m)
            for i in extras:
                if i >= STEPS:
                    extra(i)

            def weights_hi(n):
                act.wait_ge(s["wt_ps"], n + 1)
                ps = bank(6 + n % 2).rearrange("p (c q) -> p c q", q=P)
                dst = w1T_hi[:, n, :, :] if n < NE else w2T_hi[:, :, n - NE, :]
                act.activation(dst, ps, ACT.Copy).then_inc(s["wt_hi_done"], 1)

            def router(half):
                act.wait_ge(s["fT_ps"], half + 1)
                act.activation(xnT[:, :], bank(4), ACT.Copy).then_inc(s["fT_done"], 1)
                act.wait_ge(s["addr_ps"], half + 1)
                act.activation(addrT[:, :], bank(5, DADDR), ACT.Copy).then_inc(s["addr_done"], 1)
                act.wait_ge(s["zsh_done"], half + 1)
                act.activation(ez[:, :, :], zsh[:, :, :], ACT.Exp).then_inc(s["ez_done"], 1)

            def router_bias(half):
                act.wait_ge(s["dw3_ps"], half + 1)
                act.activation(dw3T[:, :], bank(5, NE), ACT.Copy).then_inc(s["dw3_done"], 1)

            def expert_tokens_hi(n):
                act.wait_ge(s["xeT_ps"], n + 1)
                if n >= 3:
                    act.wait_ge(s["h_ps"], n - 2)
                act.activation(xeT_hi[:, n % 3, :], bank(4 + n % 2), ACT.Copy).then_inc(s["xeT_hi_done"], 1)

            act.wait_ge(s["rt_ps"], 1)
            act.activation(pwT[:, :], psum[:, 5, 0:DADDR], ACT.Copy).then_inc(s["rt_done"], 1)
            act.activation(uT[:, :], psum[0:DADDR, 5, P:P + NR * NE], ACT.Copy).then_inc(s["rt_done"], 1)
            for n in range(NE):
                weights_hi(n)
            router(0)
            router_bias(0)
            router(1)
            for half in range(2):
                for e in range(NE):
                    expert_tokens_hi(half * NE + e)
                    if half == 0:
                        weights_hi(NE + e)
                for c in range(HC):
                    n = half * HC + c
                    act.wait_ge(s["h_ps"], NE * (half + 1))
                    if n >= 2:
                        act.wait_ge(s["h_lo_done"], n - 1)
                    act.activation(h_f[:, n % 2, :], bank(c), ACT.Gelu).then_inc(s["h_f_done"], 1)
                if half == 0:
                    router_bias(1)

        @block.tensor
        def _(pe):
            pe.wait_ge(s["chain_pool"], 2)
            pe.wait_ge(s["ld_aw"], 80)
            for i in range(4):
                mm = pe.transpose(psum[:, 0, i * P:(i + 1) * P], aw[:, i, :], ident[:, :])
            mm.then_inc(s["awT_ps"], 1)
            pe.wait_ge(s["ld_pos"], 16)
            pe.transpose(psum[:, 1, 0:P], aw[:, 4, :], ident[:, :])
            pe.transpose(psum[:, 1, P:P + NPOS], pos_sb[:, :], ident[0:NPOS, 0:NPOS]).then_inc(s["awT_ps"], 1)
            for i in range(NT):
                pe.wait_ge(s["xn_done"], i + 1)
                mm = pe.transpose(psum[:, 2 + i // 4, (i % 4) * P:(i % 4 + 1) * P], xn[:, i, :], ident[:, :])
                if i % 4 == 3:
                    mm.then_inc(s["xT_ps"], 1)
            pe.wait_ge(s["awT_done"], 3)
            pe.matmul(psum[:, 1, 256:256 + NPOS], awT[:, 4, :], posT[:, :], start=True, stop=True).then_inc(s["rel_ps"], 1)
            for w, at, ps in ((0, 4, "q_ps"), (1, 6, "k_ps")):
                for j in range(2):
                    pe.wait_ge(s["xT_done"], j + 1)
                    pe.matmul(bank(at + j), awT[:, w, :], xT[:, 2 * j:2 * j + 2, :], start=True, stop=True).then_inc(s[ps], 1)

            def window(n):
                u, i = divmod(n, VG)
                if i == 0 and u >= 3:
                    pe.wait_ge(s["vbd_done"], u - 2)
                b, m = divmod(n, NB)
                pe.wait_ge(s["xT4_done"], b + 1)
                mm = pe.matmul(psum[0:GK, u % 3, i * D:(i + 1) * D],
                               xT4[:, b, CH * m:CH * m + CTX, :].rearrange("p t g -> p (t g)"), awT[:, 2, :], start=True, stop=True)
                if i == VG - 1:
                    mm.then_inc(s["vwin_ps"], 1)

            def turn_context(b, at, done):
                pe.wait_ge(s["ctxn_done"], KC * (b + 1))
                for t in range(KC):
                    mm = pe.transpose(psum[:, at, t * P:(t + 1) * P], ctx_sb[:, KC * b + t, :], ident[:, :])
                mm.then_inc(s[done], 1)

            def unit(m):
                g, w = divmod(m, UNITS)
                b, hg = divmod(g, HX // HG)
                k, v = kv_counts(m)
                if m and (m - 1) % UNITS < KC:
                    pe.wait_ge(s["rope_done"], k)
                elif m:
                    pe.wait_ge(s["v_done"], v)
                pe.wait_ge(s["ctx_lo_done"], b + 1)
                wc = (0 if w < KC else HX * DX) + hg * GC
                if m < 2 * UNITS:
                    pe.wait_ge(s["w_lo_done"], W_ORDER.index(wc // GC) + 1)
                t = w % KC
                o = bank(3 if g == 0 else 5)
                hi, lo = (c[:, b % 2, t * P:(t + 1) * P] for c in (ctx_hi, ctx_lo))
                pe.matmul(o, hi, wkv_hi[:, wc:wc + GC], start=True, stop=False)
                pe.matmul(o, hi, wkv_lo[:, wc:wc + GC], start=False, stop=False)
                pe.matmul(o, lo, wkv_hi[:, wc:wc + GC], start=False, stop=True).then_inc(s["unit_ps"], 1)

            def relative(b):
                pe.wait_ge(s["qM_done"], 2 * (b // 2 + 1))
                if b >= 2:
                    pe.wait_ge(s["kM_done"], G * (b - 1))
                elif b == 1:
                    pe.wait_ge(s["qM_done"], 4)
                pe.matmul(psum[0:NPOS * G, 4 + b, :], relM[:, :, :].rearrange("p n g -> p (n g)"),
                          qM[:, b, :, :], start=True, stop=True).then_inc(s["bd_ps"], 1)

            def local_logits(b):
                pe.wait_ge(s["bd_raw_done"], 2 * (b + 1))
                out3 = bank(4 + b, GK).rearrange("p (h t) -> p h t", h=2)
                for n in range(NB):
                    e = min(CH * (n + 1), S)
                    mm = pe.matmul(out3[:, :, CH * n:e], kM[:, b, CH * n:CH * n + CTX, :].rearrange("p t g -> p (t g)"),
                                   qM[:, b, :, CH * n:e], start=True, stop=True)
                    if n % (NB // 2) == NB // 4:
                        unit(2 * b + n // (NB // 2))
                mm.then_inc(s["logit_ps"], 1)

            def local_values(b, between):
                pe.wait_ge(s["prob_done"], b + 1)
                if b:
                    pe.wait_ge(s["rec_done"], b)
                else:
                    pe.wait_ge(s["v_done"], KC)
                for half in range(2):
                    r = slice(64 * half, 64 * half + 64)
                    mm = pe.matmul(psum[r, 3, 0:S], mask_v[:, :, :].rearrange("p g d -> p (g d)"), pr[:, b, half, :],
                                   start=True, stop=True)
                mm.then_inc(s["sum_ps"], 1)
                between = list(between)
                for n in range(NB):
                    bn = NB * b + n
                    e = min(CH * (n + 1), S)
                    pe.wait_ge(s["vbd_done"], bn // VG + 1)
                    for half in range(2):
                        r = slice(64 * half, 64 * half + 64)
                        mm = pe.matmul(psum[r, 4 + b, CH * n:e], vbd[:, bn % VRING, r], pr[:, b, half, CH * n:e], start=True, stop=True)
                    if n == NB - 1:
                        mm.then_inc(s["oa_ps"], 1)
                    for what, arg in between[n * len(between) // NB:(n + 1) * len(between) // NB]:
                        if what == "window":
                            window(arg)
                        else:
                            local_project(arg)

            def local_project(b):
                pe.wait_ge(s["oT_done"], b + 1)
                for i in range(TPB):
                    t = TPB * b + i
                    mm = pe.matmul(psum[:, 4 + b, i * D:(i + 1) * D], oT[:, t * P:(t + 1) * P], awT[:, 3, :], start=True, stop=True)
                mm.then_inc(s["ya_ps"], 1)

            def turn_latents(pair, at, done):
                for i in range(4):
                    t = 4 * pair + i
                    pe.wait_ge(s["lat_in_done"], t + 1)
                    mm = pe.transpose(psum[:, at, i * P:(i + 1) * P], xn[:, t, :], ident[:, :])
                mm.then_inc(s[done], 1)

            pe.wait_ge(s["xT_done"], 2)
            for n in range(VG):
                window(n)
            pe.wait_ge(s["relM_done"], G)
            for b in range(B):
                relative(b)
            for n in range(VG, 3 * VG):
                window(n)
            turn_context(0, 3, "ct_ps")
            for n in range(3 * VG, 6 * VG):
                window(n)
            pe.wait_ge(s["kM_done"], 2 * G)
            pe.wait_ge(s["ctx_f_done"], 1)
            for b in range(B):
                local_logits(b)
            pe.wait_ge(s["mask_done"], 2)
            windows = [range(6 * VG, VRING), range(VRING, VRING + 5 * VG), range(VRING + 5 * VG, B * NB), ()]
            for b in range(B):
                between = [("window", n) for n in windows[b]]
                if b:
                    between.insert(len(between) // 2, ("project", b - 1))
                local_values(b, between)
            turn_latents(0, 0, "lat_ps")
            local_project(B - 1)

            def turn_keys(i):
                g, h = divmod(i, HG)
                pe.wait_ge(s["k_split_done"], KC * (g + 1))
                if i:
                    pe.wait_ge(s["kt_done"], i)
                for t in range(KC):
                    mm = pe.transpose(psum[:, 6, t * P:(t + 1) * P],
                                      k_split[g % 2][:, t, h, :, :].rearrange("p a d -> p (a d)").bitcast(F32), ident[:, :])
                mm.then_inc(s["kt_ps"], 1)

            def extra_read(n):
                if n:
                    done = list(extras.values())[:n]
                    what = done[-1]
                    if what[0] == "context":
                        pe.wait_ge(s["ctx_f_done"], what[1] + 1)
                    elif what[0] == "latents":
                        pe.wait_ge(s["lat_f_done"], 2)
                    elif what[0] == "turn":
                        pe.wait_ge(s["turned_done"], sum(w[0] == "turn" for w in done))
                    else:
                        pe.wait_ge(s["x2_done"], TPB * what[1] + what[2] + 1)

            def queries(j):
                b, pair = divmod(j, PAIRS)
                pe.wait_ge(s["lat_lo_done"], b // 2 + 1)
                if j < PAIRS:
                    pe.wait_ge(s["w_lo_done"], 5 + 2 * pair // HG)
                if j:
                    pe.wait_ge(s["qx_hi_done"], j)
                    pe.wait_ge(s["qx_lo_done"], j)
                extra_read(sum(e < 2 * j - 2 for e in extras))
                toks = slice(b * S, (b + 1) * S)
                for a in range(2):
                    h = 2 * pair + a
                    o = psum[:, 7, a * S:(a + 1) * S]
                    hi, lo = (w[:, h, :, :].rearrange("p a d -> p (a d)") for w in (wq_hi, wq_lo))
                    pe.matmul(o, hi, lat_hi[:, toks], start=True, stop=False)
                    pe.matmul(o, hi, lat_lo[:, toks], start=False, stop=False)
                    mm = pe.matmul(o, lo, lat_hi[:, toks], start=False, stop=True)
                mm.then_inc(s["qx_ps"], 1)

            def scores(i):
                pe.wait_ge(s["kt_done"], i + 1)
                pe.wait_ge(s["qx_hi_done"], i // 2 + 1)
                pe.wait_ge(s["qx_lo_done"], i // 2 + 1)
                if i >= 2:
                    pe.wait_ge(s["exp_done"], i - 1)
                for t in range(KC):
                    o = psum[:, 2 * (i % 2) + t // 2, (t % 2) * S:(t % 2 + 1) * S]
                    k = kT[:, i % 3, t * P:(t + 1) * P]
                    q = slice((i % 2) * S, (i % 2 + 1) * S)
                    pe.matmul(o, k, q_hi[:, (i // 2) % 2, q], start=True, stop=False)
                    mm = pe.matmul(o, k, q_lo[:, (i // 2) % 2, q], start=False, stop=True)
                mm.then_inc(s["score_ps"], 1)

            def weigh_values(i):
                g, h = divmod(i, HG)
                pe.wait_ge(s["clip_done"], i + 1)
                pe.wait_ge(s["v_done"], KC * (g + 1))
                if i == 0:
                    pe.wait_ge(s["consts"], 9)
                if i == HG:
                    pe.wait_ge(s["ones_done"], 1)
                if i:
                    pe.wait_ge(s["ox_done"], i)
                for q in range(TPB):
                    for t in range(KC):
                        mm = pe.matmul(psum[:, 4, q * (DX + 1):(q + 1) * (DX + 1)], e_sb[:, i % 3, t * S + q * P:t * S + (q + 1) * P],
                                       v_sb[g % 2][:, t, h, :], start=(t == 0), stop=(t == KC - 1))
                mm.then_inc(s["pv_ps"], 1)

            def extra(i):
                what, n = extras[i], EXTRA_NO[i]
                q = min((i + 1) // 2 + 1, STEPS // 2)
                pe.wait_ge(s["qx_hi_done"], q)
                pe.wait_ge(s["qx_lo_done"], q)
                extra_read(n)
                if what[0] == "context":
                    turn_context(what[1], 7, "extra_ps")
                elif what[0] == "latents":
                    turn_latents(what[1], 7, "extra_ps")
                elif what[0] == "turn":
                    _, b, t, part = what
                    if part == 0:
                        pe.wait_ge(s["ox_done"], HX * (b + 1))
                    for c in range(CHK // 2):
                        cc = part * CHK // 2 + c
                        mm = pe.transpose(psum[:, 7, c * P:(c + 1) * P], o_sb[:, b % 2, t, cc * P:(cc + 1) * P], ident[:, :])
                    mm.then_inc(s["extra_ps"], 1)
                else:
                    pe.wait_ge(s["ld_wo"], 16)
                    for c in range(CHK):
                        mm = pe.matmul(psum[:, 7, 0:D], oxT[:, c, :], wo_sb[:, c, :], start=(c == 0), stop=(c == CHK - 1))
                    mm.then_inc(s["extra_ps"], 1)

            pe.wait_ge(s["x1_done"], NT)
            pe.wait_ge(s["lat_f_done"], 1)
            turn_keys(0)
            queries(0)
            turn_keys(1)
            pe.wait_ge(s["v_done"], KC)
            scores(0)
            for i in range(STEPS):
                if i + 2 < STEPS:
                    turn_keys(i + 2)
                if i % 2 == 0 and i + 2 < STEPS:
                    queries(i // 2 + 1)
                if i in extras:
                    extra(i)
                if i + 1 < STEPS:
                    scores(i + 1)
                if i + UNITS < NG * UNITS:
                    unit(i + UNITS)
                weigh_values(i)
            for i in extras:
                if i >= STEPS:
                    extra(i)

            def turn_weights(n):
                pe.wait_ge(s[f"ld_w{n % RING}"], 16 * (n // RING + 1))
                if n >= 2:
                    pe.wait_ge(s["wt_lo_done"], n - 1)
                for c in range(HC):
                    mm = pe.transpose(psum[:, 6 + n % 2, c * P:(c + 1) * P], w_raw[:, n % RING, c, :], ident[:, :])
                mm.then_inc(s["wt_ps"], 1)

            def router(half):
                for i in range(4):
                    t = 4 * half + i
                    pe.wait_ge(s["fn_done"], t + 1)
                    mm = pe.transpose(psum[:, 4, i * P:(i + 1) * P], xn[:, t, :], ident[:, :])
                mm.then_inc(s["fT_ps"], 1)
                pe.wait_ge(s["fT_done"], half + 1)
                pe.matmul(bank(5, DADDR), pwT[:, :], xnT[:, :], start=True, stop=True).then_inc(s["addr_ps"], 1)
                pe.wait_ge(s["addr_done"], half + 1)
                for i in range(4):
                    mm = pe.matmul(psum[:, 4, i * NR * NE:(i + 1) * NR * NE], addrT[:, i * P:(i + 1) * P], uT[:, :], start=True, stop=True)
                mm.then_inc(s["z_ps"], 1)

            def router_bias(half):
                pe.wait_ge(s["dw_done"], half + 1)
                for i in range(4):
                    mm = pe.transpose(psum[0:NE, 5, i * P:(i + 1) * P], dw[:, half, i, 2, :], ident[:, :])
                mm.then_inc(s["dw3_ps"], 1)

            def bias_product(half):
                pe.wait_ge(s["dw3_done"], half + 1)
                pe.wait_ge(s["ld_b2"], 16)
                for i in range(4):
                    mm = pe.matmul(psum[:, 4, i * D:(i + 1) * D], dw3T[:, i * P:(i + 1) * P], b2_sb[:, :], start=True, stop=True)
                mm.then_inc(s["bias_ps"], 1)

            def turn_tokens(n):
                pe.wait_ge(s["xe_done"], n + 1)
                if n >= 2:
                    pe.wait_ge(s["xeT_lo_done"], n - 1)
                for i in range(4):
                    mm = pe.transpose(psum[:, 4 + n % 2, i * P:(i + 1) * P], xe[:, n % 3, i, :], ident[:, :])
                mm.then_inc(s["xeT_ps"], 1)

            def first_mixture(n):
                half, e = divmod(n, NE)
                pe.wait_ge(s["xeT_lo_done"], n + 1)
                if half == 0:
                    pe.wait_ge(s["wt_lo_done"], e + 1)
                if half and e == 0:
                    pe.wait_ge(s["h_f_done"], HC)
                hi, lo = xeT_hi[:, n % 3, :], xeT_lo[:, n % 3, :]
                for c in range(HC):
                    pe.matmul(bank(c), w1T_hi[:, e, c, :], hi, start=(e == 0), stop=False)
                    pe.matmul(bank(c), w1T_hi[:, e, c, :], lo, start=False, stop=False)
                    mm = pe.matmul(bank(c), w1T_lo[:, e, c, :], hi, start=False, stop=(e == NE - 1))
                mm.then_inc(s["h_ps"], 1)

            def second_mixture(half):
                pe.wait_ge(s["wt_lo_done"], 2 * NE)
                pe.wait_ge(s["h_lo_done"], HC * (half + 1))
                for i in range(4):
                    for eg in range(NEG):
                        n = (4 * half + i) * NEG + eg
                        if n >= 3:
                            pe.wait_ge(s["y_done"], EG * (n - 2))
                        es = slice(eg * EG, (eg + 1) * EG)
                        o = bank(5 + n % 3)
                        for c in range(HC):
                            hi, lo = (h[:, c, i * P:(i + 1) * P] for h in (h_hi, h_lo))
                            w_hi, w_lo = (w[:, c, es, :].rearrange("p e d -> p (e d)") for w in (w2T_hi, w2T_lo))
                            pe.matmul(o, hi, w_hi, start=(c == 0), stop=False)
                            pe.matmul(o, hi, w_lo, start=False, stop=False)
                            mm = pe.matmul(o, lo, w_hi, start=False, stop=(c == HC - 1))
                        mm.then_inc(s["y_ps"], 1)

            pe.wait_ge(s["ld_pw"], 16)
            pe.wait_ge(s["ld_u"], 48)
            pe.wait_ge(s["x2_done"], NT)
            pe.transpose(psum[:, 5, 0:DADDR], pw_sb[:, :], ident[0:DADDR, 0:DADDR])
            pe.transpose(psum[0:DADDR, 5, P:P + NR * NE], u_sb[:, :], ident[0:NR * NE, 0:NR * NE]).then_inc(s["rt_ps"], 1)
            for n in range(NE):
                turn_weights(n)
            pe.wait_ge(s["rt_done"], 2)
            router(0)
            router_bias(0)
            pe.wait_ge(s["z_done"], 1)
            router(1)
            pe.wait_ge(s["dw3_done"], 1)
            pe.wait_ge(s["z_done"], 2)
            bias_product(0)
            pe.wait_ge(s["bias_done"], 4)
            for half in range(2):
                if half:
                    router_bias(1)
                    bias_product(1)
                    pe.wait_ge(s["bias_done"], 8)
                turn_tokens(half * NE)
                for e in range(NE):
                    n = half * NE + e
                    if e + 1 < NE:
                        turn_tokens(n + 1)
                    if half == 0:
                        turn_weights(NE + e)
                    first_mixture(n)
                pe.wait_ge(s["xeT_lo_done"], NE * (half + 1))
                second_mixture(half)
                if half == 0:
                    pe.wait_ge(s["y_done"], 4 * NE)

        @block.vector
        def _(dve):
            count = [0]

            def link(ins):
                count[0] += 1
                ins.then_inc(s["chain_dve"], 1)
                dve.wait_ge(s["chain_dve"], count[0])

            def statistics(src, lo):
                n = len(src)
                for i, t in enumerate(src):
                    dve.bn_stats(stats[:, lo + i, :], t).then_inc(s["stats_done"], 1)
                dve.wait_ge(s["stats_done"], lo + n)
                for i in range(n):
                    dve.bn_aggr(mv[:, lo + i, :], stats[:, lo + i, :]).then_inc(s["mv_done"], 1)

            def normalize(out_, in_, slot):
                return dve.tensor_scalar(out_, in_, mv[:, slot, 0:1], rstd[:, slot:slot + 1], ALU.subtract, ALU.mult)

            dve.wait_ge(s["chain_pool"], 2)
            link(dve.tensor_reduce(mask_d[:, :], ident[:, :].rearrange("p (h d) -> p d h", d=DA), AX_X, ALU.add))
            dve.wait_ge(s["ld_pds"], 16)
            link(dve.tensor_tensor(pds_b[:, 1, :], pds_b[:, 0, :], mask_d[:, :], ALU.mult))
            dve.tensor_reduce(pds[:, 0:1], pds_b[:, 1, :], AX_X, ALU.add).then_inc(s["pds_done"], 1)
            dve.wait_ge(s["pds_done"], 1)
            dve.scalar_tensor_tensor(pds[:, 1:2], pds[:, 0:1], -1.0, pds[:, 0:1], ALU.mult, ALU.min).then_inc(s["absneg_done"], 1)
            for half in range(2):
                dve.wait_ge(s[f"ld_x{half}"], 16)
                statistics([x_sb[:, 4 * half + t, :] for t in range(NT // 2)], LN_X + 4 * half)
            dve.wait_ge(s["chain_pool"], 2)
            dve.tensor_reduce(mask_kg[:, :], ident[0:GK, 0:GK].rearrange("p (k g) -> p g k", g=G), AX_X, ALU.add).then_inc(s["mask_done"], 1)
            dve.wait_ge(s["mask_done"], 1)
            dve.tensor_copy(mask_v[:, :, :], mask_kg[:, :, None].to_broadcast([GK, G, DA])).then_inc(s["mask_done"], 1)
            dve.wait_ge(s["rstd_done"], 1)
            for t in range(NT):
                normalize(xn[:, t, :], x_sb[:, t, :], LN_X + t).then_inc(s["xn_done"], 1)

            def context_statistics(b):
                dve.wait_ge(s[f"ld_ctx{b}"], 16)
                statistics([ctx_sb[:, KC * b + t, :] for t in range(KC)], LN_C + KC * b)

            def context_normalize(b):
                dve.wait_ge(s["rstd_done"], 2 + b)
                for t in range(KC):
                    ct = KC * b + t
                    normalize(ctx_sb[:, ct, :], ctx_sb[:, ct, :], LN_C + ct).then_inc(s["ctxn_done"], 1)

            context_statistics(0)
            dve.wait_ge(s["softplus_done"], 1)
            link(dve.scalar_tensor_tensor(pds[:, 3:4], pds[:, 0:1], 0.0, pds[:, 2:3], ALU.max, ALU.add))
            dve.tensor_scalar(pds[:, 3:4], pds[:, 3:4], Q_SCALE, None, ALU.mult).then_inc(s["qscale_done"], 1)
            dve.wait_ge(s["rel_ps"], 1)
            dve.wait_ge(s["chain_pool"], 6)
            dve.wait_ge(s["consts"], 5)
            for g in range(G):
                dve.tensor_scalar(relM[:, :, g], psum[:, 1, 256:256 + NPOS], mask4[:, g:g + 1], None, ALU.mult)\
                   .then_inc(s["relM_done"], 1)
            for j in range(2):
                dve.wait_ge(s["k_ps"], j + 1)
                for g in range(G):
                    dve.tensor_scalar(kM[:, 2 * j:2 * j + 2, PAST:PAST + S, g], bank(6 + j).rearrange("p (a b) -> p a b", a=2),
                                      mask4[:, g:g + 1], K_SCALE, ALU.mult, ALU.mult).then_inc(s["kM_done"], 1)

            def values_masked(u):
                dve.wait_ge(s["vwin_ps"], u + 1)
                if VG * u >= VRING:
                    dve.wait_ge(s["oa_ps"], (VG * (u + 1) - 1 - VRING) // NB + 1)
                at = VG * u % VRING
                dve.tensor_tensor(vbd[:, at:at + VG, :].rearrange("p n (h e) -> p (n h) e", h=2),
                                  bank(u % 3, GK).rearrange("p (n e) -> p n e", e=G * DA),
                                  mask_v[:, :, :].rearrange("p g d -> p (g d)")[:, None, :].to_broadcast([GK, 2 * VG, G * DA]),
                                  ALU.mult).then_inc(s["vbd_done"], 1)

            def context_lo(b):
                dve.wait_ge(s["ctx_hi_done"], b + 1)
                dve.tensor_tensor(ctx_lo[:, b % 2, :], ctx_f[:, :], ctx_hi[:, b % 2, :].bitcast(F32), ALU.subtract).then_inc(s["ctx_lo_done"], 1)

            def key_unit(m):
                k, _ = kv_counts(m)
                g, t = divmod(m, UNITS)
                dve.wait_ge(s["unit_ps"], m + 1)
                if k >= 2:
                    dve.wait_ge(s["kf_done"], k - 1)
                ps = bank(3 if g == 0 else 5)
                dve.tensor_tensor(rope_a[:, k % 2, :].rearrange("p (h d) -> p h d", d=DX // 2), ps.rearrange("p (h d) -> p h d", d=DX // 2),
                                  cos_sb[:, t, None, :].to_broadcast([P, 2 * HG, DX // 2]), ALU.mult)
                ph = ps.rearrange("p (h a d) -> p h a d", a=2, d=DX // 2)
                bh = rope_b[:, k % 2, :].rearrange("p (h a d) -> p h a d", a=2, d=DX // 2)
                for a in range(2):
                    ins = dve.tensor_tensor(bh[:, :, a, :], ph[:, :, 1 - a, :],
                                            sin_sb[:, t, a, None, :].to_broadcast([P, HG, DX // 2]), ALU.mult)
                ins.then_inc(s["rope_done"], 1)

            values_masked(0)
            context_normalize(0)
            for u in range(1, 6):
                values_masked(u)
                if u == 3:
                    context_lo(0)
            dve.wait_ge(s["ld_rope"], 32)
            dve.tensor_scalar(sin_sb[:, :, 0, :], sin_sb[:, :, 1, :], -1.0, None, ALU.mult).then_inc(s["sin_done"], 1)
            dve.wait_ge(s["sin_done"], 1)

            def add_positions(b):
                dve.wait_ge(s["logit_ps"], b + 1)
                dve.wait_ge(s["shifted"], 16)
                dve.wait_ge(s["xT4_done"], B)
                if b >= 2:
                    dve.wait_ge(s["prob_done"], b - 1)
                full, tail = NB - 1, S - (NB - 1) * CH
                ps = psum[0:GK, 4 + b, :].rearrange("p (h t) -> p h t", h=2)
                dst = logits[:, b % 2, :, :]
                for h in range(2):
                    ins = dve.tensor_tensor(dst[:, h, 0:full * CH].rearrange("p (n c) -> p n c", c=CH),
                                            ps[:, h, 0:full * CH].rearrange("p (n c) -> p n c", c=CH),
                                            bd[:, :, b, h, 0:full].rearrange("p c n -> p n c"), ALU.add)
                ins.then_inc(s["added_done"], 1)
                dve.tensor_tensor(dst[:, :, full * CH:S], ps[:, :, full * CH:S],
                                  bd[:, 0:tail, b, :, full].rearrange("p c h -> p h c"), ALU.add).then_inc(s["added_done"], 1)

            for m in range(KC):
                key_unit(m)
            for b in range(B):
                add_positions(b)
                if b < B - 1:
                    context_statistics(b + 1)

            def local_reciprocal(b):
                dve.wait_ge(s["sum_ps"], b + 1)
                if b:
                    dve.wait_ge(s["oT_done"], b)
                dve.reciprocal(rec[:, :], psum[:, 3, 0:S]).then_inc(s["rec_done"], 1)

            def local_normalize(b):
                dve.wait_ge(s["oa_ps"], b + 1)
                dve.wait_ge(s["rec_done"], b + 1)
                dve.tensor_tensor(oT[:, S * b:S * (b + 1)], psum[:, 4 + b, 0:S], rec[:, :], ALU.mult).then_inc(s["oT_done"], 1)

            def local_residual(b):
                dve.wait_ge(s["ya_ps"], b + 1)
                for i in range(TPB):
                    t = TPB * b + i
                    dve.tensor_tensor(x_sb[:, t, :], psum[:, 4 + b, i * D:(i + 1) * D], x_sb[:, t, :], ALU.add).then_inc(s["x1_done"], 1)
                dve.wait_ge(s["x1_done"], TPB * (b + 1))

            def latents(pair):
                before = 1 + B + 2 * pair
                tiles = range(4 * pair, 4 * pair + 4)
                lo = LN_1 + pair * NT
                statistics([x_sb[:, t, :] for t in tiles], lo)
                dve.wait_ge(s["rstd_done"], before + 1)
                for i, t in enumerate(tiles):
                    normalize(xn[:, t, :], x_sb[:, t, :], lo + i).then_inc(s["xn1_done"], 1)
                dve.wait_ge(s["xn1_done"], 4 * (pair + 1))
                statistics([xn[:, t, :] for t in tiles], lo + 4)
                dve.wait_ge(s["ld_bo"], 16)
                for t in tiles:
                    dve.tensor_tensor(x_sb[:, t, :], x_sb[:, t, :], bo_all[:, :], ALU.add).then_inc(s["bo_added"], 1)
                dve.wait_ge(s["rstd_done"], before + 2)
                for i, t in enumerate(tiles):
                    normalize(xn[:, t, :], xn[:, t, :], lo + 4 + i).then_inc(s["lat_in_done"], 1)

            def latents_lo(pair):
                dve.wait_ge(s["lat_hi_done"], pair + 1)
                toks = slice(pair * HALF_TOK, (pair + 1) * HALF_TOK)
                dve.tensor_tensor(lat_lo[:, toks], lat_f[:, :], lat_hi[:, toks].bitcast(F32), ALU.subtract).then_inc(s["lat_lo_done"], 1)

            local_reciprocal(0)
            for u in range(6, 11):
                values_masked(u)
            local_normalize(0)
            local_reciprocal(1)
            for u in range(11, 14):
                values_masked(u)
            local_residual(0)
            for u in range(14, 16):
                values_masked(u)
            context_normalize(1)
            local_normalize(1)
            local_reciprocal(2)
            for u in range(16, 19):
                values_masked(u)
            local_residual(1)
            for u in range(19, NV):
                values_masked(u)
            latents(0)
            local_normalize(2)
            local_reciprocal(3)
            local_residual(2)
            for b in range(2, B):
                context_normalize(b)
            local_normalize(3)
            local_residual(3)
            latents_lo(0)
            latents(1)

            def queries_lo(j):
                dve.wait_ge(s["qx_hi_done"], j + 1)
                dve.tensor_tensor(q_lo[:, j % 2, :], bank(7), q_hi[:, j % 2, :].bitcast(F32), ALU.subtract).then_inc(s["qx_lo_done"], 1)

            def clip(i):
                dve.wait_ge(s["exp_done"], i + 1)
                dve.tensor_scalar(e_sb[:, i % 3, :], e_sb[:, i % 3, :], E_LO, E_HI, ALU.max, ALU.min).then_inc(s["clip_done"], 1)

            def divide(i):
                b, h = divmod(i, HX)
                dve.wait_ge(s["pv_ps"], i + 1)
                ps = psum[:, 4, 0:TPB * (DX + 1)].rearrange("p (q d) -> p q d", d=DX + 1)
                dve.reciprocal(den[:, i % 2, :], ps[:, :, DX]).then_inc(s["den_done"], 1)
                dve.wait_ge(s["den_done"], i + 1)
                if h == 0 and b >= 2:
                    dve.wait_ge(s["extra_ps"], last_turn(b - 2))
                dve.tensor_tensor(o_sb[:, b % 2, :, h * DX:(h + 1) * DX], ps[:, :, 0:DX],
                                  den[:, i % 2, :, None].to_broadcast([P, TPB, DX]), ALU.mult).then_inc(s["ox_done"], 1)

            def extra(i):
                what = extras[i]
                if what[0] == "context":
                    context_lo(what[1])
                elif what[0] == "latents":
                    latents_lo(1)
                elif what[0] == "project":
                    _, b, t = what
                    tile = TPB * b + t
                    dve.wait_ge(s["extra_ps"], EXTRA_NO[i] + 1)
                    dve.tensor_tensor(x_sb[:, tile, :], psum[:, 7, 0:D], x_sb[:, tile, :], ALU.add).then_inc(s["x2_done"], 1)

            queries_lo(0)
            clip(0)
            for i in range(STEPS):
                if i % 2 == 0 and i + 2 < STEPS:
                    queries_lo(i // 2 + 1)
                if i in extras:
                    extra(i)
                clip_next = i + 1 < STEPS
                m = i + UNITS
                if m < NG * UNITS and m % UNITS < KC:
                    if clip_next:
                        clip(i + 1)
                    key_unit(m)
                elif clip_next:
                    clip(i + 1)
                divide(i)
            for i in extras:
                if i >= STEPS:
                    extra(i)

            def weights_lo(n):
                dve.wait_ge(s["wt_hi_done"], n + 1)
                ps = bank(6 + n % 2).rearrange("p (c q) -> p c q", q=P)
                hi, lo = (w1T_hi[:, n, :, :], w1T_lo[:, n, :, :]) if n < NE else (w2T_hi[:, :, n - NE, :], w2T_lo[:, :, n - NE, :])
                dve.tensor_tensor(lo, ps, hi.bitcast(F32), ALU.subtract).then_inc(s["wt_lo_done"], 1)

            def router(half):
                dve.wait_ge(s["z_ps"], half + 1)
                dve.tensor_copy(z[:, :, 0:NE], psum[:, 4, 0:4 * NR * NE].rearrange("p (r e) -> p r e", e=NE)).then_inc(s["z_done"], 1)
                dve.wait_ge(s["z_done"], half + 1)
                dve.wait_ge(s["fill_done"], 2)
                for r in range(4 * NR):
                    dve.max(top8[:, r, :], z[:, r, :]).then_inc(s["top_done"], 1)
                dve.wait_ge(s["top_done"], 4 * NR * (half + 1))
                dve.tensor_copy(top3[:, :, 0:TOPK], top8[:, :, 0:TOPK]).then_inc(s["top3_done"], 1)
                dve.tensor_tensor(zsh[:, :, :], z[:, :, 0:NE], top8[:, :, 0:1].to_broadcast([P, 4 * NR, NE]), ALU.subtract)\
                   .then_inc(s["zsh_done"], 1)
                dve.wait_ge(s["top3_done"], half + 1)
                for r in range(4 * NR):
                    dve.match_replace(zr[:, r, :], top3[:, r, :], z[:, r, :], TAKEN).then_inc(s["zr_done"], 1)
                dve.wait_ge(s["zr_done"], 4 * NR * (half + 1))
                dve.tensor_tensor(chosen[:, :, :], zr[:, :, 0:NE], z[:, :, 0:NE], ALU.not_equal).then_inc(s["chosen_done"], 1)
                dve.wait_ge(s["chosen_done"], half + 1)
                dve.wait_ge(s["ez_done"], half + 1)
                dve.tensor_tensor(chosen[:, :, :], chosen[:, :, :], ez[:, :, :], ALU.mult).then_inc(s["wsel_done"], 1)
                dve.wait_ge(s["wsel_done"], half + 1)
                dve.tensor_reduce(zsum[:, :], chosen[:, :, :], AX_X, ALU.add).then_inc(s["zsum_done"], 1)
                dve.wait_ge(s["zsum_done"], half + 1)
                dve.reciprocal(zsum[:, :], zsum[:, :]).then_inc(s["zrec_done"], 1)
                dve.wait_ge(s["zrec_done"], half + 1)
                dve.tensor_tensor(dw[:, half, :, :, :].rearrange("p i r e -> p (i r) e"), chosen[:, :, :],
                                  zsum[:, :, None].to_broadcast([P, 4 * NR, NE]), ALU.mult).then_inc(s["dw_done"], 1)

            def bias_add(half):
                dve.wait_ge(s["bias_ps"], half + 1)
                for i in range(4):
                    t = 4 * half + i
                    dve.tensor_tensor(x_sb[:, t, :], psum[:, 4, i * D:(i + 1) * D], x_sb[:, t, :], ALU.add).then_inc(s["bias_done"], 1)

            dve.wait_ge(s["x2_done"], NT)
            for half in range(2):
                statistics([x_sb[:, 4 * half + i, :] for i in range(4)], LN_F + 4 * half)
            for half in range(2):
                dve.wait_ge(s["rstd_done"], 1 + B + 4 + half + 1)
                for i in range(4):
                    t = 4 * half + i
                    normalize(xn[:, t, :], x_sb[:, t, :], LN_F + t).then_inc(s["fn_done"], 1)
            for n in range(NE):
                weights_lo(n)
            router(0)
            router(1)
            bias_add(0)
            for half in range(2):
                if half:
                    bias_add(1)
                for e in range(NE):
                    n = half * NE + e
                    dve.wait_ge(s["xeT_hi_done"], n + 1)
                    dve.tensor_tensor(xeT_lo[:, n % 3, :], bank(4 + n % 2), xeT_hi[:, n % 3, :].bitcast(F32), ALU.subtract)\
                       .then_inc(s["xeT_lo_done"], 1)
                    if half == 0:
                        weights_lo(NE + e)
                for c in range(HC):
                    n = half * HC + c
                    dve.wait_ge(s["h_hi_done"], n + 1)
                    dve.tensor_tensor(h_lo[:, c, :], h_f[:, n % 2, :], h_hi[:, c, :].bitcast(F32), ALU.subtract).then_inc(s["h_lo_done"], 1)
                if half == 0:
                    dve.wait_ge(s["bias_done"], 4)
                else:
                    dve.wait_ge(s["bias_done"], 8)
                for i in range(4):
                    t = 4 * half + i
                    for eg in range(NEG):
                        n = t * NEG + eg
                        dve.wait_ge(s["y_ps"], n + 1)
                        for j in range(EG):
                            e = eg * EG + j
                            ins = dve.scalar_tensor_tensor(x_sb[:, t, :], psum[:, 5 + n % 3, j * D:(j + 1) * D],
                                                           dw[:, half, i, 1, e:e + 1], x_sb[:, t, :], ALU.mult, ALU.add)
                            ins.then_inc(s["y_done"], 1)
                            dve.wait_ge(s["y_done"], n * EG + j + 1)
                    dve.sem_inc(s["x3_done"], 1)


_INS = ["x", "ctx_1024", "L0_attn_position_embeddings", "L0_attn_Wq", "L0_attn_Wk", "L0_attn_Wv",
        "L0_attn_Wpost", "L0_attn_Wrel", "L0_attn_per_dim_scale", "L0_xattn_cos", "L0_xattn_sin",
        "L0_xattn_ln_lat_g", "L0_xattn_ln_lat_b", "L0_xattn_ln_ctx_g", "L0_xattn_ln_ctx_b", "L0_xattn_Wq",
        "L0_xattn_Wkv", "L0_xattn_Wo", "L0_xattn_bo", "L0_ffn_P_w", "L0_ffn_U1", "L0_ffn_U2", "L0_ffn_U3",
        "L0_ffn_W1", "L0_ffn_W2", "L0_ffn_b2"]
_OUTS = [((4, 256, 128), "float32")]


def kernel(**inputs):
    import numpy as _np
    import concourse.bacc as _bacc
    from concourse import mybir as _mybir
    from concourse.bass_utils import run_bass_kernel_spmd as _run

    nc = _bacc.Bacc("TRN2", target_bir_lowering=False, num_devices=1)
    arrays, args = {}, []
    for name in _INS:
        a = _np.ascontiguousarray(inputs[name])
        arrays[f"in_{name}_dram"] = a
        args.append(nc.dram_tensor(f"in_{name}_dram", a.shape, _mybir.dt.from_np(a.dtype), kind="ExternalInput").ap())
    for i, (shape, dtype) in enumerate(_OUTS):
        dt = _mybir.dt.from_np(_np.dtype(dtype))
        args.append(nc.dram_tensor(f"out_{i}_dram", shape, dt, kind="ExternalOutput").ap())
    decoder_layer(nc, *args)
    r = _run(nc, [arrays], core_ids=[0])
    return r.results[0]["out_0_dram"]
```

```python
from contextlib import ExitStack

import numpy as np

import concourse.bass as bass
from concourse import mybir

P = 128
BANK = 512
F32 = mybir.dt.float32
F32R = mybir.dt.float32r
ALU = mybir.AluOpType
ACT = mybir.ActivationFunctionType
AX_X = mybir.AxisListType.X


def decoder_layer(nc, x, ctx_in, pos, a_wq, a_wk, a_wv, a_wpost, a_wrel, a_pds,
                  rope_cos, rope_sin, lat_g, lat_b, ctx_g, ctx_b, x_wq, x_wkv, x_wo, x_bo,
                  f_pw, f_u1, f_u2, f_u3, f_w1, f_w2, f_b2, out):
    B, S, D = x.shape
    NT = B * S // P
    TPB = S // P
    HALF_TOK = B * S // 2
    EPS = 1e-5

    HA, CH, PAST = 8, 12, 12
    DA = D // HA
    CTX = CH + PAST
    NPOS = pos.shape[0]
    NB = -(-S // CH)
    SPAD = PAST + NB * CH
    G = 4
    GK = G * CTX
    Q_SCALE = DA ** -0.5 / float(np.log(2))
    K_SCALE = float(np.log(1 + np.e) / np.log(2))
    CAP = 50.0
    VG = 4
    NV = B * NB // VG
    VRING = B * NB // 2

    SC = ctx_in.shape[1]
    KC = SC // P
    NCT = B * KC
    HX, DX = 16, 64
    HG = 8
    NG = B * HX // HG
    STEPS = B * HX
    GC = HG * DX
    QH = 4
    NQ = B * HX // QH
    X_SCALE = DX ** -0.5
    E_LO, E_HI = float(np.exp(-11.0)), float(np.exp(11.0))
    UNITS = 2 * KC
    LEAD = UNITS + 1
    CHK = HX * DX // P

    NE, HID = f_w1.shape[0], f_w1.shape[1]
    HC = HID // P
    DADDR = f_pw.shape[0]
    NR, TOPK = 3, 3
    FILL = 8 - TOPK
    LOWEST, TAKEN = -3.0e38, 3.0e38
    RING = 4
    REST = 32
    SPLIT = REST + NE
    EG = BANK // D
    NEG = NE // EG

    assert B == 4 and S == 256 and D == P and SC == BANK and GC == BANK and VRING % VG == 0 and NPOS == CTX + 1

    with ExitStack() as ctx:
        def sb(name, shape, dt=F32, where=ctx):
            return where.enter_context(nc.sbuf_tensor(name, shape, dt))

        def sem(name):
            return ctx.enter_context(nc.semaphore(name))

        bd_dram = nc.dram_tensor("bd_dram", [CH, NPOS * G, B * 2 * NB], F32, kind="Internal").ap()
        psum = ctx.enter_context(nc.psum_tensor("psum", [P, 8, BANK], F32))

        def local_bank(b):
            return 7 - b

        def bank(i, parts=P):
            return psum[0:parts, i, :]

        ident = sb("ident", [P, P])
        ident_r = sb("ident_r", [P, P], F32R)
        mask8 = sb("mask8", [P, HA])
        mask4 = sb("mask4", [P, G])
        mask_kg = sb("mask_kg", [GK, G])
        mask_v = sb("mask_v", [GK, G, DA])
        neghalf = sb("neghalf", [P, NCT])
        x_sb = sb("x_sb", [P, NT, D])
        xn = sb("xn", [P, NT, D])
        LN_X, LN_C, LN_1, LN_2, LN_F = 0, NT, NT + NCT, NT + NCT + 2, NT + NCT + 2 * NT
        NSTAT = LN_F + NT
        stats = sb("stats", [P, NSTAT, 6])
        mv = sb("mv", [P, NSTAT, 2])
        veps = sb("veps", [P, NSTAT])
        rstd = sb("rstd", [P, NSTAT])
        affine = sb("affine", [P, 4])
        bo_all = sb("bo_all", [P, D])
        wo_sb = sb("wo_sb", [P, CHK, D])

        cross = ExitStack()
        ctx_sb = sb("ctx_sb", [P, NCT, D], F32, cross)
        ctx_f = sb("ctx_f", [P, SC], F32, cross)
        ctx_hi = sb("ctx_hi", [P, 2, SC], F32R, cross)
        ctx_lo = sb("ctx_lo", [P, 2, SC], F32R, cross)
        raw = sb("raw", [P, 2, GC], F32, cross)
        rope_a = sb("rope_a", [P, 2, GC], F32, cross)
        rope_b = sb("rope_b", [P, 2, GC], F32, cross)
        k_f = sb("k_f", [P, 2, GC], F32, cross)
        wkv_hi = sb("wkv_hi", [P, 2 * HX * DX], F32R, cross)
        wkv_lo = sb("wkv_lo", [P, 2 * HX * DX], F32R, cross)
        cos_sb = sb("cos_sb", [P, KC, DX // 2], F32, cross)
        sin_sb = sb("sin_sb", [P, KC, 2, DX // 2], F32, cross)
        k_split = [sb("k_split0", [P, KC, HG, 2, DX], F32R, cross)]
        v_sb = [sb("v_sb0", [P, KC, HG, DX + 1], F32, cross)]

        wq_hi = sb("wq_hi", [P, HX * DX], F32R, cross)
        wq_lo = sb("wq_lo", [P, HX * DX], F32R, cross)

        first = ExitStack()
        qM = sb("qM", [P, B, 2, S], F32, first)
        kM = sb("kM", [P, B, SPAD, G], F32, first)
        bd = sb("bd", [GK, CH, B, 2, NB], F32, first)
        xT4 = sb("xT4", [P, B, SPAD, G], F32, first)
        aw = sb("aw", [P, 5, D], F32, first)
        awT = sb("awT", [P, 5, D], F32, first)
        pos_sb = sb("pos_sb", [NPOS, D], F32, first)
        posT = sb("posT", [P, NPOS], F32, first)
        pds_b = sb("pds_b", [P, 2, DA], F32, first)
        mask_d = sb("mask_d", [P, DA], F32, first)
        pds = sb("pds", [P, 4], F32, first)
        relM = sb("relM", [P, NPOS, G], F32, first)
        vbd = sb("vbd", [GK, VRING, D], F32, first)
        pr = sb("pr", [GK, B, 2, S], F32, first)
        projected = ExitStack()
        xT = sb("xT", [P, B, S], F32, projected)
        bd_raw = sb("bd_raw", [NPOS * G, CH, B, 2, NB], F32, projected)
        projected.close()
        logits = sb("logits", [GK, 2, 2, S], F32, first)
        rec = sb("rec", [P, S], F32, first)
        oT = sb("oT", [P, B * S], F32, first)
        first.close()

        second = ExitStack()
        lat_f = sb("lat_f", [P, BANK], F32, second)
        lat_hi = sb("lat_hi", [P, B * S], F32R, second)
        lat_lo = sb("lat_lo", [P, B * S], F32R, second)
        q_pair = sb("q_pair", [P, 2, 2, QH // 2, S], F32R, second)
        q_twice = sb("q_twice", [P, 2, 2, QH, S], F32R, second)
        kT = sb("kT", [P, 3, SC], F32R, second)
        e_sb = sb("e_sb", [P, 3, KC * S], F32, second)
        k_split.append(sb("k_split1", [P, KC, HG, 2, DX], F32R, second))
        v_sb.append(sb("v_sb1", [P, KC, HG, DX + 1], F32, second))
        den = sb("den", [P, 2, TPB], F32, second)
        o_sb = sb("o_sb", [P, 2, TPB, HX * DX], F32, second)
        oxT = sb("oxT", [P, TPB, CHK, P], F32, second)
        second.close()
        cross.close()

        third = ExitStack()
        w_raw = sb("w_raw", [P, RING, HC, P], F32, third)
        pw_sb = sb("pw_sb", [DADDR, D], F32, third)
        u_sb = sb("u_sb", [NR * NE, DADDR], F32, third)
        b2_sb = sb("b2_sb", [NE, D], F32, third)
        pwT = sb("pwT", [P, DADDR], F32, third)
        uT = sb("uT", [DADDR, NR * NE], F32, third)
        pick = sb("pick", [SPLIT, NE], F32, third)
        spread = sb("spread", [SPLIT, NE, P], F32R, third)
        xnT = sb("xnT", [P, 2, 4 * P], F32, third)
        addrT = sb("addrT", [DADDR, 4 * P], F32, third)
        z = sb("z", [P, 4 * NR, NE + FILL], F32, third)
        zr = sb("zr", [P, 4 * NR, NE + FILL], F32, third)
        top8 = sb("top8", [P, 4 * NR, 8], F32, third)
        top3 = sb("top3", [P, 4 * NR, 8], F32, third)
        chosen = sb("chosen", [P, 4 * NR, NE], F32, third)
        zsh = sb("zsh", [P, 4 * NR, NE], F32, third)
        ez = sb("ez", [P, 4 * NR, NE], F32, third)
        zsum = sb("zsum", [P, 4 * NR], F32, third)
        dw = sb("dw", [P, 2, 4, NR, NE], F32, third)
        dw1T = sb("dw1T", [SPLIT, 2, 4 * P], F32R, third)
        dw3T = sb("dw3T", [NE, 4 * P], F32, third)
        w1T_hi = sb("w1T_hi", [P, NE, HC, P], F32R, third)
        w1T_lo = sb("w1T_lo", [P, NE, HC, P], F32R, third)
        xeT = sb("xeT", [P, 2, 4 * P], F32, third)
        xeT_hi = sb("xeT_hi", [P, 3, 4 * P], F32R, third)
        xeT_lo = sb("xeT_lo", [P, 3, 4 * P], F32R, third)
        w2T_hi = sb("w2T_hi", [P, HC, NE, D], F32R, third)
        w2T_lo = sb("w2T_lo", [P, HC, NE, D], F32R, third)
        h_f = sb("h_f", [P, HC, 4 * P], F32, third)
        h_hi = sb("h_hi", [P, 2, HC, 4 * P], F32R, third)
        h_lo = sb("h_lo", [P, 2, HC, 4 * P], F32R, third)
        third.close()

        NAMES = """ld_x0 ld_x1 ld_aw ld_pos ld_pds pds_done ld_ctx0 ld_ctx1 ld_ctx2 ld_ctx3 ld_raw0 ld_raw1 ld_rope
            ld_affine ld_wo ld_bo bd_stored shifted stored consts chain_pool chain_dve chain_act stats_done mv_done
            rstd_done xn_done mask_done absneg_done softplus_done qscale_done awT_ps awT_done xT_ps xT_done xT4_done
            rel_ps relM_done q_ps k_ps qM_done kM_done vwin_ps vbd_done bd_ps bd_raw_done added_done logit_ps
            capped_done prob_done sum_ps oa_ps rec_done oT_done ya_ps x1_done w_hi_done w_lo_done ctxn_done sin_done
            ct_ps ctx_f_done ctx_hi_done ctx_lo_done unit_ps rope_done kf_done k_hi_done k_split_done v_done
            ones_done xn1_done lat_in_done lat_ps lat_f_done lat_hi_done lat_lo_done bo_added ident_r_done kt_ps
            kt_done qx_ps qx_hi_done qx_lo_done q_first_hi_done q_first_lo_done q_copied0 q_copied1 score_ps exp_done
            clip_done pv_ps den_done ox_done extra_ps turned_done tail_ps tail_done x2_done ld_w0 ld_w1 ld_w2 ld_w3
            ld_pw ld_u ld_b2 wt_ps wt_hi_done wt_lo_done rt_ps rt_done fn_done fT_ps fT_done addr_ps addr_done z_ps
            z_done fill_done top_done top3_done zr_done chosen_done zsh_done ez_done wsel_done zsum_done zrec_done
            dw_done pick_done spread_done dw1_ps dw1_hi_done dw1_lo_done dw3_ps dw3_done spread_ps xe_done
            xeT_hi_done xeT_lo_done h_ps h_f_done h_hi_done h_lo_done y_ps y_done bias_ps bias_done x3_done""".split()
        s = {n: sem(n) for n in NAMES}
        block = ctx.enter_context(nc.Block())

        FIRST_COPIES = [(a, slice(DX * a, DX * a + DX), slice(DX * copy, DX * copy + DX)) for a in range(2) for copy in range(2)]

        def copies_done(j):
            return 64 * (j // 2 + j % 2)

        W_ORDER = (0, 2, 1, 3, 4, 5)

        def unit_bank(m):
            return 5 if m >= UNITS else 3 - m % 2

        def kv_counts(m):
            k = KC * (m // UNITS) + min(m % UNITS, KC)
            return k, m - k

        LATENT_STEPS, LATENTS_TURN = (2, 4, 6), 9
        extras = {}
        for b in range(B):
            if b + 1 < B:
                extras[b * HX + 1] = ("context", b + 1)
            if b == 0:
                extras[LATENTS_TURN] = ("latents", 1)
            else:
                at = b * HX + (3 if b + 1 < B else 1)
                for t in range(TPB):
                    extras[at + 6 * t] = ("turn", b - 1, t, 0)
                    extras[at + 6 * t + 2] = ("turn", b - 1, t, 1)
                    extras[at + 6 * t + 4] = ("project", b - 1, t)
        for t in range(TPB):
            extras[STEPS - 2 * (TPB - t) + 1] = ("turn", B - 1, t, 0)
        extras = dict(sorted(extras.items()))
        EXTRA_NO = {i: n for n, i in enumerate(extras)}

        def last_turn(b):
            return max(n for n, what in enumerate(extras.values()) if what[0:2] == ("turn", b)) + 1

        FREED = STEPS - HG + 1
        ROUTE = {"weights": FREED, "tokens": FREED + 1, "address": FREED + 2, "scores": FREED + 3,
                 "chosen": FREED + 4, "softmax": FREED + 5, "turn": FREED + 6}
        NORM_STEP = (B - 1) * HX - 1
        ROUTE_2 = {"tokens": 2, "address": 3, "scores": 4, "chosen": 5, "softmax": 6, "turn": 7}
        TAIL_BANK = (7, 0)
        HIDDEN = {NE: [(0, range(0, HC // 2))], NE + 1: [(0, range(HC // 2, HC))], 2 * NE - 1: [(1, range(HC))]}
        BIAS = {0: ("turn", 0), 1: ("product", 0), 8: ("turn", 1), 9: ("product", 1)}

        @block.sync
        def _(sp):
            sp.dma_start(x_sb[:, 0:NT // 2, :], x[0:B // 2].rearrange("b (t p) d -> p (b t) d", p=P)).then_inc(s["ld_x0"], 16)
            for i, w in enumerate((a_wq, a_wk, a_wv, a_wpost, a_wrel)):
                sp.dma_start(aw[:, i, :], w).then_inc(s["ld_aw"], 16)
            def load_context(b):
                sp.dma_start(ctx_sb[:, KC * b:KC * b + KC, :], ctx_in[b].rearrange("(t p) d -> p t d", p=P)).then_inc(s[f"ld_ctx{b}"], 16)
            load_context(0)
            for n, c in enumerate(W_ORDER):
                if n == 4:
                    for c0 in range(0, CH, CH // 2):
                        sp.wait_ge(s["bd_raw_done"], 2 * B)
                        sp.dma_start(bd_dram[c0:c0 + CH // 2].rearrange("c r w -> r c w"),
                                     bd_raw[:, c0:c0 + CH // 2, :, :, :].rearrange("r c b h n -> r c (b h n)")).then_inc(s["bd_stored"], 16)
                    sp.wait_ge(s["bd_stored"], 32)
                    rows = bd_dram.rearrange("c r w -> (c r) w")[0:CH * (NPOS - 1) * G]
                    sp.dma_start(bd[:, :, :, :, :].rearrange("r c b h n -> r c (b h n)"),
                                 rows.rearrange("(c r) w -> r c w", c=CH)).then_inc(s["shifted"], 16)
                if n >= 2:
                    sp.wait_ge(s["w_lo_done"], n - 1)
                src = x_wkv[:, c * GC:(c + 1) * GC] if c < 4 else x_wq[:, (c - 4) * GC:(c - 3) * GC]
                sp.dma_start(raw[:, n % 2, :], src).then_inc(s[f"ld_raw{n % 2}"], 16)
                if n == 1:
                    for i, v in enumerate((lat_g, lat_b, ctx_g, ctx_b)):
                        sp.dma_start(affine[:, i:i + 1], v.rearrange("(d o) -> d o", o=1)).then_inc(s["ld_affine"], 16)
                if n == 3:
                    sp.dma_start(cos_sb[:, :, :], rope_cos.rearrange("(t p) d -> p t d", p=P)).then_inc(s["ld_rope"], 16)
                    sp.dma_start(sin_sb[:, :, 1, :], rope_sin.rearrange("(t p) d -> p t d", p=P)).then_inc(s["ld_rope"], 16)
                    for b in range(1, B):
                        load_context(b)
                    sp.dma_start(bo_all[:, :], x_bo.partition_broadcast(P)).then_inc(s["ld_bo"], 16)
            sp.dma_start(wo_sb[:, :, :], x_wo.rearrange("(c p) n -> p c n", p=P)).then_inc(s["ld_wo"], 16)

            def copy_queries(j):
                sp.wait_ge(s["qx_lo_done"], j)
                if j >= 2:
                    sp.wait_ge(s["score_ps"], QH * (j - 1))
                for a in range(2):
                    for half in range(2):
                        sp.dma_start(q_twice[DX * half:DX * half + DX, j % 2, :, a:QH:2, :].bitcast(F32),
                                     q_pair[DX * a:DX * a + DX, j % 2, :, :, :].bitcast(F32)).then_inc(s[f"q_copied{j % 2}"], 16)

            for j in range(1, NQ - 1):
                copy_queries(j)
            sp.wait_ge(s["unit_ps"], NG * UNITS)
            sp.wait_ge(s["k_split_done"], NG * KC)
            sp.wait_ge(s["pv_ps"], STEPS - HG)
            sp.dma_start(pw_sb[:, :], f_pw).then_inc(s["ld_pw"], 16)
            for i, u in enumerate((f_u1, f_u2, f_u3)):
                sp.dma_start(u_sb[i * NE:(i + 1) * NE, :], u).then_inc(s["ld_u"], 16)
            sp.dma_start(b2_sb[:, :], f_b2).then_inc(s["ld_b2"], 16)
            copy_queries(NQ - 1)
            for n in range(2 * NE):
                if n >= RING:
                    sp.wait_ge(s["wt_ps"], n - RING + 1)
                src = f_w1[n].rearrange("(c p) d -> p c d", p=P) if n < NE else f_w2[n - NE].rearrange("o (c q) -> o c q", q=P)
                sp.dma_start(w_raw[:, n % RING, :, :], src).then_inc(s[f"ld_w{n % RING}"], 16)
            for t in range(NT):
                sp.wait_ge(s["x3_done"], t + 1)
                b, q = divmod(t, TPB)
                sp.dma_start(out[b, q * P:(q + 1) * P, :], x_sb[:, t, :]).then_inc(s["stored"], 16)
            sp.wait_ge(s["stored"], 16 * NT)

        @block.gpsimd
        def _(pool):
            count = [0]

            def link(ins):
                count[0] += 1
                ins.then_inc(s["chain_pool"], 1)
                pool.wait_ge(s["chain_pool"], count[0])

            def rstd_of(lo, n):
                pool.wait_ge(s["mv_done"], lo + n)
                link(pool.tensor_scalar(veps[:, lo:lo + n], mv[:, lo:lo + n, 1], EPS, None, ALU.add))
                pool.tensor_tensor(rstd[:, lo:lo + n], veps[:, lo:lo + n], neghalf[:, 0:n], ALU.pow).then_inc(s["rstd_done"], 1)

            link(pool.memset(ident[:, :], 0.0))
            link(pool.affine_select(out=ident[:, :], in_=ident[:, :], compare_op=ALU.not_equal, fill=1.0,
                                    base=0, pattern=[[-1, P]], channel_multiplier=1))
            pool.memset(neghalf[:, :], -0.5).then_inc(s["consts"], 1)
            link(pool.memset(mask8[:, :], 1.0))
            link(pool.affine_select(out=mask8[:, :], in_=mask8[:, :], compare_op=ALU.is_ge, fill=0.0,
                                    base=0, pattern=[[-DA, HA]], channel_multiplier=1))
            link(pool.affine_select(out=mask8[:, :], in_=mask8[:, :], compare_op=ALU.is_ge, fill=0.0,
                                    base=DA - 1, pattern=[[DA, HA]], channel_multiplier=-1))
            link(pool.tensor_tensor(mask4[:, :], mask8[:, 0:G], mask8[:, G:HA], ALU.add))
            pool.memset(xT4[:, :, 0:PAST, :], 0.0).then_inc(s["consts"], 1)
            pool.memset(xT4[:, :, PAST + S:SPAD, :], 0.0).then_inc(s["consts"], 1)
            pool.memset(kM[:, :, 0:PAST, :], 0.0).then_inc(s["consts"], 1)
            pool.memset(kM[:, :, PAST + S:SPAD, :], 0.0).then_inc(s["consts"], 1)
            for half in range(2):
                other = slice(64 - 64 * half, 128 - 64 * half)
                pool.wait_ge(s["consts"], 5 + half)
                pool.memset(qM[other, :, half, :], 0.0).then_inc(s["consts"], 1)
            pool.wait_ge(s["consts"], 7)
            pool.memset(bd_raw[:, :, :, :, NB - 1], 0.0).then_inc(s["consts"], 1)
            pool.memset(v_sb[0][:, :, :, DX:DX + 1], 1.0).then_inc(s["consts"], 1)
            rstd_of(LN_X, NT // 2)
            rstd_of(LN_X + NT // 2, NT // 2)
            rstd_of(LN_C, KC)

            def weight_rest(n):
                pool.wait_ge(s["w_hi_done"], n + 1)
                c = W_ORDER[n]
                if c < 4:
                    cols = slice(c * GC, (c + 1) * GC)
                    pool.tensor_tensor(wkv_lo[:, cols], raw[:, n % 2, :], wkv_hi[:, cols].bitcast(F32), ALU.subtract).then_inc(s["w_lo_done"], 1)
                else:
                    cols = slice((c - 4) * GC, (c - 3) * GC)
                    pool.tensor_tensor(wq_lo[:, cols], raw[:, n % 2, :], wq_hi[:, cols].bitcast(F32), ALU.subtract).then_inc(s["w_lo_done"], 1)

            def key_sum(k):
                pool.wait_ge(s["rope_done"], k + 1)
                if k >= 2:
                    pool.wait_ge(s["k_split_done"], k - 1)
                pool.tensor_tensor(k_f[:, k % 2, :], rope_a[:, k % 2, :], rope_b[:, k % 2, :], ALU.add).then_inc(s["kf_done"], 1)

            def key_rest(k):
                g, t = divmod(k, KC)
                pool.wait_ge(s["k_hi_done"], k + 1)
                pool.tensor_tensor(k_split[g % 2][:, t, :, 1, :], k_f[:, k % 2, :].rearrange("p (h d) -> p h d", d=DX),
                                   k_split[g % 2][:, t, :, 0, :].bitcast(F32), ALU.subtract).then_inc(s["k_split_done"], 1)

            def key_step(m):
                if m and (m - 1) % UNITS < KC and (m - 1) // UNITS < NG:
                    k, _ = kv_counts(m - 1)
                    if m % UNITS < KC and m // UNITS < NG:
                        key_sum(k + 1)
                    key_rest(k)
                elif m % UNITS < KC and m // UNITS < NG:
                    key_sum(kv_counts(m)[0])

            for n in range(4):
                weight_rest(n)
            for m in range(KC + 1):
                key_step(m)
            for n in range(4, 6):
                weight_rest(n)
            for b in range(1, B):
                rstd_of(LN_C + KC * b, KC)
            rstd_of(LN_1, NT // 2)
            rstd_of(LN_1 + NT // 2, NT // 2)
            pool.wait_ge(s["x1_done"], NT)
            pool.memset(v_sb[1][:, :, :, DX:DX + 1], 1.0).then_inc(s["ones_done"], 1)

            def token_rest(n):
                pool.wait_ge(s["xeT_hi_done"], n + 1)
                if n >= 3:
                    pool.wait_ge(s["h_ps"], n - 2)
                pool.tensor_tensor(xeT_lo[:, n % 3, :], xeT[:, n % 2, :], xeT_hi[:, n % 3, :].bitcast(F32), ALU.subtract)\
                    .then_inc(s["xeT_lo_done"], 1)

            key_step(UNITS)
            for i in range(STEPS):
                if i == LATENT_STEPS[0]:
                    rstd_of(LN_1 + NT, NT // 2)
                if i == LATENT_STEPS[1]:
                    rstd_of(LN_1 + NT + NT // 2, NT // 2)
                key_step(i + LEAD)
                if i == NORM_STEP:
                    rstd_of(LN_F, NT // 2)
                if i == FREED:
                    pool.wait_ge(s["ld_pw"], 16)
                    pool.memset(z[:, :, NE:NE + FILL], LOWEST).then_inc(s["fill_done"], 1)
                    pool.memset(top3[:, :, TOPK:8], LOWEST).then_inc(s["fill_done"], 1)
                    pool.memset(dw1T[:, :, :].bitcast(F32), 0.0).then_inc(s["fill_done"], 1)
                    pool.tensor_tensor(pick[:, :], ident[0:SPLIT, 0:NE], ident[0:SPLIT, REST:SPLIT], ALU.add).then_inc(s["pick_done"], 1)
                    pool.wait_ge(s["pick_done"], 1)
                    pool.tensor_copy(spread[:, :, :], pick[:, :, None].to_broadcast([SPLIT, NE, P])).then_inc(s["spread_done"], 1)

            token_rest(0)
            rstd_of(LN_F + NT // 2, NT // 2)
            for n in range(1, 2 * NE):
                token_rest(n)

        @block.scalar
        def _(act):
            act.dma_start(x_sb[:, NT // 2:NT, :], x[B // 2:B].rearrange("b (t p) d -> p (b t) d", p=P)).then_inc(s["ld_x1"], 16)
            act.dma_start(pds_b[:, 0, :], a_pds.partition_broadcast(P)).then_inc(s["ld_pds"], 16)
            act.dma_start(pos_sb[:, :], pos).then_inc(s["ld_pos"], 16)
            act.preload_act_table(ACT.Exp)
            def weight_hi(n):
                act.wait_ge(s[f"ld_raw{n % 2}"], 16 * (n // 2 + 1))
                c = W_ORDER[n]
                if c < 4:
                    act.activation(wkv_hi[:, c * GC:(c + 1) * GC], raw[:, n % 2, :], ACT.Copy).then_inc(s["w_hi_done"], 1)
                else:
                    act.activation(wq_hi[:, (c - 4) * GC:(c - 3) * GC], raw[:, n % 2, :], ACT.Copy).then_inc(s["w_hi_done"], 1)

            act.wait_ge(s["absneg_done"], 1)
            act.activation(pds[:, 2:3], pds[:, 1:2], ACT.Exp).then_inc(s["chain_act"], 1)
            act.wait_ge(s["chain_act"], 1)
            act.activation(pds[:, 2:3], pds[:, 2:3], ACT.Ln, bias=1.0).then_inc(s["softplus_done"], 1)
            act.wait_ge(s["awT_ps"], 1)
            act.activation(awT[:, 0:4, :].rearrange("p a b -> p (a b)"), bank(0), ACT.Copy).then_inc(s["awT_done"], 1)
            act.wait_ge(s["awT_ps"], 2)
            act.activation(awT[:, 4, :], psum[:, 1, 0:D], ACT.Copy).then_inc(s["awT_done"], 1)
            act.activation(posT[:, :], psum[:, 1, D:D + NPOS], ACT.Copy).then_inc(s["awT_done"], 1)
            for j in range(2):
                act.wait_ge(s["xT_ps"], j + 1)
                act.activation(xT[:, 2 * j:2 * j + 2, :], bank(2 + j).rearrange("p (a b) -> p a b", a=2), ACT.Copy).then_inc(s["xT_done"], 1)
            act.wait_ge(s["consts"], 3)

            def replicate(b):
                act.wait_ge(s["xT_done"], b // 2 + 1)
                act.activation(xT4[:, b, PAST:PAST + S, :], xT[:, b, :, None].to_broadcast([P, S, G]), ACT.Copy).then_inc(s["xT4_done"], 1)

            replicate(0)
            act.wait_ge(s["consts"], 8)
            act.wait_ge(s["qscale_done"], 1)
            for j in range(2):
                act.wait_ge(s["q_ps"], j + 1)
                for half in range(2):
                    r = slice(64 * half, 64 * half + 64)
                    act.activation(qM[r, 2 * j:2 * j + 2, half, :], psum[r, 7 - j, :].rearrange("p (b t) -> p b t", b=2),
                                   ACT.Copy, scale=pds[r, 3:4]).then_inc(s["qM_done"], 1)
            weight_hi(0)
            full, tail = NB - 1, S - (NB - 1) * CH
            for b in range(B):
                act.wait_ge(s["bd_ps"], b + 1)
                ps = psum[0:NPOS * G, local_bank(b), :].rearrange("p (h t) -> p h t", h=2)
                act.activation(bd_raw[:, :, b, :, 0:full].rearrange("p c h n -> p h n c"),
                               ps[:, :, 0:full * CH].rearrange("p h (n c) -> p h n c", c=CH), ACT.Copy).then_inc(s["bd_raw_done"], 1)
                act.activation(bd_raw[:, 0:tail, b, :, full].rearrange("p c h -> p h c"), ps[:, :, full * CH:S], ACT.Copy)\
                   .then_inc(s["bd_raw_done"], 1)
                if b == 0:
                    weight_hi(1)
                if b == 1:
                    replicate(1)
            act.wait_ge(s["ld_affine"], 64)

            def context_f(b):
                if b >= 1:
                    act.wait_ge(s["ctx_lo_done"], b)
                act.activation(ctx_f[:, :], bank(3 if b == 0 else 7), ACT.Identity, scale=affine[:, 2:3], bias=affine[:, 3:4])\
                   .then_inc(s["ctx_f_done"], 1)
                act.wait_ge(s["ctx_f_done"], b + 1)
                act.activation(ctx_hi[:, b % 2, :], ctx_f[:, :], ACT.Copy).then_inc(s["ctx_hi_done"], 1)

            act.wait_ge(s["ct_ps"], 1)
            context_f(0)
            for n in range(2, 4):
                weight_hi(n)
            for b in range(2, B):
                replicate(b)

            def value_unit(m):
                _, v = kv_counts(m)
                g, w = divmod(m, UNITS)
                act.wait_ge(s["unit_ps"], m + 1)
                if g >= 2:
                    act.wait_ge(s["pv_ps"], HG * (g - 1))
                act.activation(v_sb[g % 2][:, w - KC, :, 0:DX], bank(unit_bank(m)).rearrange("p (h d) -> p h d", d=DX),
                               ACT.Copy).then_inc(s["v_done"], 1)

            def key_hi(k):
                g, t = divmod(k, KC)
                act.wait_ge(s["kf_done"], k + 1)
                if g >= 2:
                    act.wait_ge(s["kt_ps"], HG * (g - 1))
                act.activation(k_split[g % 2][:, t, :, 0, :], k_f[:, k % 2, :].rearrange("p (h d) -> p h d", d=DX), ACT.Copy)\
                   .then_inc(s["k_hi_done"], 1)

            def local_softmax(b):
                act.wait_ge(s["added_done"], 2 * (b + 1))
                at = logits[:, b % 2, :, :]
                act.activation(at, at, ACT.Tanh, scale=1.0 / CAP).then_inc(s["capped_done"], 1)
                act.wait_ge(s["capped_done"], b + 1)
                act.activation(pr[:, b, :, :], at, ACT.Exp, scale=CAP).then_inc(s["prob_done"], 1)

            act.preload_act_table(ACT.Exp)
            for k in range(KC):
                key_hi(k)
            for b in range(B):
                if b < 2:
                    value_unit(KC + 2 * b)
                    value_unit(KC + 2 * b + 1)
                local_softmax(b)
                if b >= 2:
                    weight_hi(b + 2)

            def latents_f(pair):
                if pair:
                    act.wait_ge(s["lat_lo_done"], pair)
                else:
                    act.wait_ge(s["logit_ps"], B)
                act.activation(lat_f[:, :], bank(7 if pair else 1), ACT.Identity, scale=affine[:, 0:1], bias=affine[:, 1:2])\
                   .then_inc(s["lat_f_done"], 1)
                act.wait_ge(s["lat_f_done"], pair + 1)
                act.activation(lat_hi[:, pair * HALF_TOK:(pair + 1) * HALF_TOK], lat_f[:, :], ACT.Copy).then_inc(s["lat_hi_done"], 1)

            act.wait_ge(s["lat_ps"], 1)
            latents_f(0)

            def keys_turned(i):
                act.wait_ge(s["kt_ps"], i + 1)
                if i >= 3:
                    act.wait_ge(s["score_ps"], i - 2)
                act.activation(kT[:, i % 3, :], bank(6), ACT.Copy).then_inc(s["kt_done"], 1)

            def queries_hi(j):
                act.wait_ge(s["qx_ps"], j + 1)
                if j == 0:
                    for a, rows, to in FIRST_COPIES:
                        act.activation(q_twice[to, 0, 0, a:QH:2, :], psum[rows, 7, :].rearrange("p (h t) -> p h t", t=S), ACT.Copy)\
                           .then_inc(s["q_first_hi_done"], 1)
                    return
                if j >= 3:
                    act.wait_ge(s[f"q_copied{j % 2}"], copies_done(j - 2))
                act.activation(q_pair[:, j % 2, 0, :, :], bank(7).rearrange("p (h t) -> p h t", t=S), ACT.Copy).then_inc(s["qx_hi_done"], 1)

            def exponent(i):
                act.wait_ge(s["score_ps"], i + 1)
                if i >= 3:
                    act.wait_ge(s["pv_ps"], i - 2)
                a = 2 * (i % 2)
                act.activation(e_sb[:, i % 3, :], psum[:, a:a + 2, :].rearrange("p a b -> p (a b)"), ACT.Exp, scale=X_SCALE)\
                   .then_inc(s["exp_done"], 1)

            def extra(i):
                what = extras[i]
                if what[0] == "project":
                    return
                act.wait_ge(s["extra_ps"], EXTRA_NO[i] + 1)
                if what[0] == "context":
                    context_f(what[1])
                elif what[0] == "latents":
                    latents_f(what[1])
                else:
                    _, b, t, part = what
                    n = CHK // 2
                    act.activation(oxT[:, t, n * part:n * part + n, :].rearrange("p c q -> p (c q)"), bank(7), ACT.Copy)\
                       .then_inc(s["turned_done"], 1)

            def weights_hi(n):
                act.wait_ge(s["wt_ps"], n + 1)
                ps = bank(6).rearrange("p (c q) -> p c q", q=P)
                dst = w1T_hi[:, n, :, :] if n < NE else w2T_hi[:, :, n - NE, :]
                act.activation(dst, ps, ACT.Copy).then_inc(s["wt_hi_done"], 1)

            def tokens_hi(n):
                act.wait_ge(s["xe_done"], n + 1)
                if n >= 3:
                    act.wait_ge(s["h_ps"], n - 2)
                act.activation(xeT_hi[:, n % 3, :], xeT[:, n % 2, :], ACT.Copy).then_inc(s["xeT_hi_done"], 1)

            def route(half, stage, at):
                if stage == "tokens":
                    act.wait_ge(s["fT_ps"], half + 1)
                    act.activation(xnT[:, half, :], bank(at), ACT.Copy).then_inc(s["fT_done"], 1)
                elif stage == "address":
                    act.wait_ge(s["addr_ps"], half + 1)
                    act.activation(addrT[:, :], bank(at, DADDR), ACT.Copy).then_inc(s["addr_done"], 1)
                elif stage == "chosen":
                    act.wait_ge(s["zsh_done"], half + 1)
                    act.activation(ez[:, :, :], zsh[:, :, :], ACT.Exp).then_inc(s["ez_done"], 1)
                elif stage == "turn":
                    act.wait_ge(s["dw1_ps"], half + 1)
                    if half == 0:
                        act.wait_ge(s["fill_done"], 3)
                    act.activation(dw1T[0:NE, half, :], bank(at, NE), ACT.Copy).then_inc(s["dw1_hi_done"], 1)

            def route_2(n):
                for stage in ROUTE_2:
                    if ROUTE_2[stage] == n:
                        route(1, stage, 7)

            keys_turned(0)
            keys_turned(1)
            queries_hi(0)
            exponent(0)
            for i in range(STEPS):
                if i + 2 < STEPS:
                    keys_turned(i + 2)
                if i % QH == 0 and i + QH < STEPS:
                    queries_hi(i // QH + 1)
                if i in extras:
                    extra(i)
                if i + 1 < STEPS:
                    exponent(i + 1)
                m = i + LEAD
                if (m - 1) // UNITS < NG and (m - 1) % UNITS < KC:
                    key_hi(kv_counts(m - 1)[0])
                if m < NG * UNITS and m % UNITS >= KC:
                    value_unit(m)
                if i == ROUTE["weights"]:
                    act.wait_ge(s["rt_ps"], 1)
                    act.activation(pwT[:, :], psum[:, 5, 0:DADDR], ACT.Copy).then_inc(s["rt_done"], 1)
                    act.activation(uT[:, :], psum[0:DADDR, 5, P:P + NR * NE], ACT.Copy).then_inc(s["rt_done"], 1)
                for stage in ROUTE:
                    if ROUTE[stage] == i:
                        route(0, stage, 5)
            weights_hi(0)
            for t in range(TPB):
                act.wait_ge(s["tail_ps"], t + 1)
                act.activation(oxT[:, t, CHK // 2:CHK, :].rearrange("p c q -> p (c q)"), bank(TAIL_BANK[t]), ACT.Copy).then_inc(s["tail_done"], 1)

            tokens_hi(0)
            tokens_hi(1)
            for n in range(2 * NE):
                if n < 2 * NE - 2:
                    tokens_hi(n + 2)
                if n < 2 * NE - 1:
                    weights_hi(n + 1)
                if n in BIAS and BIAS[n][0] == "turn":
                    half = BIAS[n][1]
                    act.wait_ge(s["dw3_ps"], half + 1)
                    act.activation(dw3T[:, :], bank(7, NE), ACT.Copy).then_inc(s["dw3_done"], 1)
                route_2(n)
                if n % NE == NE - 1:
                    half = n // NE
                    for c in range(HC):
                        act.wait_ge(s["h_ps"], n + 1)
                        if half:
                            act.wait_ge(s["h_lo_done"], c + 1)
                        act.activation(h_f[:, c, :], bank(c), ACT.Gelu).then_inc(s["h_f_done"], 1)
                for half, chunks in HIDDEN.get(n, []):
                    for c in chunks:
                        act.wait_ge(s["h_f_done"], half * HC + c + 1)
                        act.activation(h_hi[:, half, c, :], h_f[:, c, :], ACT.Copy).then_inc(s["h_hi_done"], 1)

        @block.tensor
        def _(pe):
            pe.wait_ge(s["chain_pool"], 2)
            pe.wait_ge(s["ld_aw"], 80)
            for i in range(4):
                mm = pe.transpose(psum[:, 0, i * P:(i + 1) * P], aw[:, i, :], ident[:, :])
            mm.then_inc(s["awT_ps"], 1)
            pe.wait_ge(s["ld_pos"], 16)
            pe.transpose(psum[:, 1, 0:P], aw[:, 4, :], ident[:, :])
            pe.transpose(psum[:, 1, P:P + NPOS], pos_sb[:, :], ident[0:NPOS, 0:NPOS]).then_inc(s["awT_ps"], 1)
            for i in range(NT):
                pe.wait_ge(s["xn_done"], i + 1)
                mm = pe.transpose(psum[:, 2 + i // 4, (i % 4) * P:(i % 4 + 1) * P], xn[:, i, :], ident[:, :])
                if i % 4 == 3:
                    mm.then_inc(s["xT_ps"], 1)
            pe.wait_ge(s["awT_done"], 3)
            pe.matmul(psum[:, 1, 256:256 + NPOS], awT[:, 4, :], posT[:, :], start=True, stop=True).then_inc(s["rel_ps"], 1)
            for w, at, ps in ((0, 7, "q_ps"), (1, 5, "k_ps")):
                for j in range(2):
                    pe.wait_ge(s["xT_done"], j + 1)
                    pe.matmul(bank(at - j), awT[:, w, :], xT[:, 2 * j:2 * j + 2, :], start=True, stop=True).then_inc(s[ps], 1)

            def window(n):
                u, i = divmod(n, VG)
                if i == 0 and u >= 3:
                    pe.wait_ge(s["vbd_done"], u - 2)
                if i == 0 and u == 8:
                    pe.wait_ge(s["v_done"], KC)
                b, m = divmod(n, NB)
                pe.wait_ge(s["xT4_done"], b + 1)
                mm = pe.matmul(psum[0:GK, u % 3, i * D:(i + 1) * D],
                               xT4[:, b, CH * m:CH * m + CTX, :].rearrange("p t g -> p (t g)"), awT[:, 2, :], start=True, stop=True)
                if i == VG - 1:
                    mm.then_inc(s["vwin_ps"], 1)

            def turn_context(b, at, done):
                pe.wait_ge(s["ctxn_done"], KC * (b + 1))
                for t in range(KC):
                    mm = pe.transpose(psum[:, at, t * P:(t + 1) * P], ctx_sb[:, KC * b + t, :], ident[:, :])
                mm.then_inc(s[done], 1)

            def unit(m, parts=range(3)):
                g, w = divmod(m, UNITS)
                b, hg = divmod(g, HX // HG)
                wc = (0 if w < KC else HX * DX) + hg * GC
                t = w % KC
                if 0 in parts:
                    before = m - (2 if g == 0 else 1)
                    if before >= 0:
                        k, v = kv_counts(before + 1)
                        if before % UNITS < KC:
                            pe.wait_ge(s["rope_done"], k)
                        else:
                            pe.wait_ge(s["v_done"], v)
                    elif m == 1:
                        pe.wait_ge(s["vbd_done"], 6)
                    pe.wait_ge(s["ctx_lo_done"], b + 1)
                    if m < 2 * UNITS:
                        pe.wait_ge(s["w_lo_done"], W_ORDER.index(wc // GC) + 1)
                o = bank(unit_bank(m))
                hi, lo = (c[:, b % 2, t * P:(t + 1) * P] for c in (ctx_hi, ctx_lo))
                for part in parts:
                    c, w_ = ((hi, wkv_hi), (hi, wkv_lo), (lo, wkv_hi))[part]
                    mm = pe.matmul(o, c, w_[:, wc:wc + GC], start=(part == 0), stop=(part == 2))
                if 2 in parts:
                    mm.then_inc(s["unit_ps"], 1)

            def relative(b):
                pe.wait_ge(s["qM_done"], 2 * (b // 2 + 1))
                if b >= 2:
                    pe.wait_ge(s["kM_done"], G * (b - 1))
                else:
                    pe.wait_ge(s["qM_done"], 2 * (b + 1))
                pe.matmul(psum[0:NPOS * G, local_bank(b), :], relM[:, :, :].rearrange("p n g -> p (n g)"),
                          qM[:, b, :, :], start=True, stop=True).then_inc(s["bd_ps"], 1)

            def local_logits(b):
                pe.wait_ge(s["bd_raw_done"], 2 * (b + 1))
                out3 = bank(local_bank(b), GK).rearrange("p (h t) -> p h t", h=2)
                for n in range(NB):
                    e = min(CH * (n + 1), S)
                    mm = pe.matmul(out3[:, :, CH * n:e], kM[:, b, CH * n:CH * n + CTX, :].rearrange("p t g -> p (t g)"),
                                   qM[:, b, :, CH * n:e], start=True, stop=True)
                    for k in range(6):
                        if n == (2 * k + 1) * NB // 12:
                            unit(2 * b + k // 3, [k % 3])
                mm.then_inc(s["logit_ps"], 1)

            def local_values(b, between):
                pe.wait_ge(s["prob_done"], b + 1)
                if b:
                    pe.wait_ge(s["rec_done"], b)
                else:
                    pe.wait_ge(s["v_done"], KC)
                for half in range(2):
                    r = slice(64 * half, 64 * half + 64)
                    mm = pe.matmul(psum[r, 3, 0:S], mask_v[:, :, :].rearrange("p g d -> p (g d)"), pr[:, b, half, :],
                                   start=True, stop=True)
                mm.then_inc(s["sum_ps"], 1)
                between = list(between)
                for n in range(NB):
                    bn = NB * b + n
                    e = min(CH * (n + 1), S)
                    pe.wait_ge(s["vbd_done"], bn // VG + 1)
                    for half in range(2):
                        r = slice(64 * half, 64 * half + 64)
                        mm = pe.matmul(psum[r, local_bank(b), CH * n:e], vbd[:, bn % VRING, r], pr[:, b, half, CH * n:e], start=True, stop=True)
                    if n == NB - 1:
                        mm.then_inc(s["oa_ps"], 1)
                    for what, arg in between[n * len(between) // NB:(n + 1) * len(between) // NB]:
                        if what == "window":
                            window(arg)
                        elif what == "project":
                            local_project(arg)
                        elif what == "latents":
                            pe.wait_ge(s["vbd_done"], NV - 2)
                            turn_latents(0, 1, "lat_ps")
                        elif what == "keys":
                            if arg == 0:
                                pe.wait_ge(s["x1_done"], 2 * TPB)
                            turn_keys(arg)
                        else:
                            queries(arg)

            def local_project(b):
                pe.wait_ge(s["oT_done"], b + 1)
                for i in range(TPB):
                    t = TPB * b + i
                    mm = pe.matmul(psum[:, local_bank(b), i * D:(i + 1) * D], oT[:, t * P:(t + 1) * P], awT[:, 3, :], start=True, stop=True)
                mm.then_inc(s["ya_ps"], 1)

            def turn_latents(pair, at, done):
                for i in range(4):
                    t = 4 * pair + i
                    pe.wait_ge(s["lat_in_done"], t + 1)
                    mm = pe.transpose(psum[:, at, i * P:(i + 1) * P], xn[:, t, :], ident[:, :])
                mm.then_inc(s[done], 1)

            def turn_keys(i):
                g, h = divmod(i, HG)
                pe.wait_ge(s["k_split_done"], KC * (g + 1))
                if i:
                    pe.wait_ge(s["kt_done"], i)
                if i == 0:
                    pe.wait_ge(s["ident_r_done"], 1)
                for t in range(KC):
                    mm = pe.transpose(psum[:, 6, t * P:(t + 1) * P].bitcast(F32R),
                                      k_split[g % 2][:, t, h, :, :].rearrange("p a d -> p (a d)"), ident_r[:, :])
                mm.then_inc(s["kt_ps"], 1)

            def extra_read(n):
                if n:
                    done = list(extras.values())[:n]
                    what = done[-1]
                    if what[0] == "context":
                        pe.wait_ge(s["ctx_f_done"], what[1] + 1)
                    elif what[0] == "latents":
                        pe.wait_ge(s["lat_f_done"], 2)
                    elif what[0] == "turn":
                        pe.wait_ge(s["turned_done"], sum(w[0] == "turn" for w in done))
                    else:
                        pe.wait_ge(s["x2_done"], TPB * what[1] + what[2] + 1)

            def query_bank_read(n):
                pe.wait_ge(s["q_first_lo_done"], len(FIRST_COPIES))
                if n > 1:
                    pe.wait_ge(s["qx_hi_done"], n - 1)
                    pe.wait_ge(s["qx_lo_done"], n - 1)

            def queries(j):
                b, four = divmod(j, HX // QH)
                pe.wait_ge(s["lat_lo_done"], b // 2 + 1)
                if b == 0:
                    pe.wait_ge(s["w_lo_done"], 5 + QH * four // HG)
                if j:
                    query_bank_read(j)
                extra_read(sum(e < QH * (j - 1) for e in extras))
                toks = slice(b * S, (b + 1) * S)
                for a in range(QH // 2):
                    cols = slice((QH * four + 2 * a) * DX, (QH * four + 2 * a + 2) * DX)
                    o = psum[:, 7, a * S:(a + 1) * S]
                    pe.matmul(o, wq_hi[:, cols], lat_hi[:, toks], start=True, stop=False)
                    pe.matmul(o, wq_hi[:, cols], lat_lo[:, toks], start=False, stop=False)
                    mm = pe.matmul(o, wq_lo[:, cols], lat_hi[:, toks], start=False, stop=True)
                mm.then_inc(s["qx_ps"], 1)

            pe.wait_ge(s["xT_done"], 2)
            for n in range(VG):
                window(n)
            pe.wait_ge(s["relM_done"], G)
            for b in range(B):
                relative(b)
                if b in (1, 2):
                    for n in range(b * VG, (b + 1) * VG):
                        window(n)
            turn_context(0, 3, "ct_ps")
            for n in range(3 * VG, 6 * VG):
                window(n)
            pe.wait_ge(s["kM_done"], 2 * G)
            pe.wait_ge(s["ctx_f_done"], 1)
            for b in range(B):
                local_logits(b)
            for n in range(6 * VG, 8 * VG):
                window(n)
            pe.wait_ge(s["mask_done"], 2)
            LATE = B * NB - 2 * VG
            windows = [range(8 * VG, VRING), range(VRING, VRING + 5 * VG), range(VRING + 5 * VG, LATE)]
            for b in range(B - 1):
                between = [("window", n) for n in windows[b]]
                if b:
                    between.insert(len(between) // 2, ("project", b - 1))
                local_values(b, between)
            local_values(B - 1, [("window", n) for n in range(LATE, B * NB)] + [("keys", 0), ("project", B - 2), ("latents", 0), ("keys", 1), ("queries", 0)])

            def scores(i):
                pe.wait_ge(s["kt_done"], i + 1)
                j = i // QH
                if j:
                    pe.wait_ge(s[f"q_copied{j % 2}"], copies_done(j))
                else:
                    pe.wait_ge(s["q_first_lo_done"], 2 * (i % 2 + 1))
                if i >= 2:
                    pe.wait_ge(s["exp_done"], i - 1)
                for t in range(KC):
                    o = psum[:, 2 * (i % 2) + t // 2, (t % 2) * S:(t % 2 + 1) * S]
                    k = kT[:, i % 3, t * P:(t + 1) * P]
                    pe.matmul(o, k, q_twice[:, j % 2, 0, i % QH, :], start=True, stop=False)
                    mm = pe.matmul(o, k, q_twice[:, j % 2, 1, i % QH, :], start=False, stop=True)
                mm.then_inc(s["score_ps"], 1)

            def weigh_values(i):
                g, h = divmod(i, HG)
                pe.wait_ge(s["clip_done"], i + 1)
                pe.wait_ge(s["v_done"], KC * (g + 1))
                if i == 0:
                    pe.wait_ge(s["consts"], 9)
                if i == HG:
                    pe.wait_ge(s["ones_done"], 1)
                if i:
                    pe.wait_ge(s["ox_done"], i)
                for q in range(TPB):
                    for t in range(KC):
                        mm = pe.matmul(psum[:, 4, q * (DX + 1):(q + 1) * (DX + 1)], e_sb[:, i % 3, t * S + q * P:t * S + (q + 1) * P],
                                       v_sb[g % 2][:, t, h, :], start=(t == 0), stop=(t == KC - 1))
                mm.then_inc(s["pv_ps"], 1)

            def extra(i):
                what, n = extras[i], EXTRA_NO[i]
                q = min(i // QH + 2, NQ)
                query_bank_read(q)
                extra_read(n)
                if what[0] == "context":
                    turn_context(what[1], 7, "extra_ps")
                elif what[0] == "latents":
                    turn_latents(what[1], 7, "extra_ps")
                elif what[0] == "turn":
                    _, b, t, part = what
                    pe.wait_ge(s["ox_done"], HX * b + HX // 2 * (part + 1))
                    for c in range(CHK // 2):
                        cc = part * CHK // 2 + c
                        mm = pe.transpose(psum[:, 7, c * P:(c + 1) * P], o_sb[:, b % 2, t, cc * P:(cc + 1) * P], ident[:, :])
                    mm.then_inc(s["extra_ps"], 1)
                else:
                    pe.wait_ge(s["ld_wo"], 16)
                    for c in range(CHK):
                        mm = pe.matmul(psum[:, 7, 0:D], oxT[:, what[2], c, :], wo_sb[:, c, :], start=(c == 0), stop=(c == CHK - 1))
                    mm.then_inc(s["extra_ps"], 1)

            pe.wait_ge(s["vbd_done"], NV)
            pe.wait_ge(s["lat_f_done"], 1)
            local_project(B - 1)
            pe.wait_ge(s["x1_done"], NT - TPB)
            unit(UNITS)
            scores(0)
            pe.wait_ge(s["rec_done"], B)
            pe.wait_ge(s["x1_done"], NT)
            def turn_weights(n):
                pe.wait_ge(s[f"ld_w{n % RING}"], 16 * (n // RING + 1))
                if n:
                    pe.wait_ge(s["wt_lo_done"], n)
                for c in range(HC):
                    mm = pe.transpose(psum[:, 6, c * P:(c + 1) * P], w_raw[:, n % RING, c, :], ident[:, :])
                mm.then_inc(s["wt_ps"], 1)

            def spread_weights(n):
                half, e = divmod(n, NE)
                pe.wait_ge(s["dw1_lo_done"], half + 1)
                if n == 0:
                    pe.wait_ge(s["spread_done"], 1)
                elif n == 1:
                    pe.wait_ge(s["ox_done"], STEPS)
                else:
                    pe.wait_ge(s["xe_done"], n - 1)
                pe.matmul(bank(5 - n % 2), spread[:, e, :], dw1T[:, half, :], start=True, stop=True).then_inc(s["spread_ps"], 1)

            def route(half, stage, at):
                if stage == "tokens":
                    if half:
                        pe.wait_ge(s["bias_done"], 4)
                    for i in range(4):
                        t = 4 * half + i
                        pe.wait_ge(s["fn_done"], t + 1)
                        mm = pe.transpose(psum[:, at, i * P:(i + 1) * P], xn[:, t, :], ident[:, :])
                    mm.then_inc(s["fT_ps"], 1)
                elif stage == "address":
                    pe.wait_ge(s["fT_done"], half + 1)
                    pe.matmul(bank(at, DADDR), pwT[:, :], xnT[:, half, :], start=True, stop=True).then_inc(s["addr_ps"], 1)
                elif stage == "scores":
                    pe.wait_ge(s["addr_done"], half + 1)
                    for i in range(4):
                        mm = pe.matmul(psum[:, at, i * NR * NE:(i + 1) * NR * NE], addrT[:, i * P:(i + 1) * P], uT[:, :], start=True, stop=True)
                    mm.then_inc(s["z_ps"], 1)
                elif stage == "turn":
                    pe.wait_ge(s["dw_done"], half + 1)
                    for i in range(4):
                        mm = pe.transpose(psum[0:NE, at, i * P:(i + 1) * P], dw[:, half, i, 0, :], ident[:, :])
                    mm.then_inc(s["dw1_ps"], 1)

            for i in range(STEPS):
                if i + 2 < STEPS:
                    turn_keys(i + 2)
                if i % QH == 0 and i + QH < STEPS:
                    queries(i // QH + 1)
                if i in extras:
                    extra(i)
                if i + 1 < STEPS:
                    scores(i + 1)
                if i + LEAD < NG * UNITS:
                    unit(i + LEAD)
                weigh_values(i)
                if i == ROUTE["weights"]:
                    pe.wait_ge(s["v_done"], NG * KC)
                    pe.wait_ge(s["ld_pw"], 16)
                    pe.wait_ge(s["ld_u"], 48)
                    pe.transpose(psum[:, 5, 0:DADDR], pw_sb[:, :], ident[0:DADDR, 0:DADDR])
                    pe.transpose(psum[0:DADDR, 5, P:P + NR * NE], u_sb[:, :], ident[0:NR * NE, 0:NR * NE]).then_inc(s["rt_ps"], 1)
                if i == ROUTE["tokens"]:
                    pe.wait_ge(s["rt_done"], 2)
                for stage in ROUTE:
                    if ROUTE[stage] == i:
                        route(0, stage, 5)

            pe.wait_ge(s["kt_done"], STEPS)
            turn_weights(0)
            extra_read(len(extras))
            pe.wait_ge(s["exp_done"], STEPS)
            pe.wait_ge(s["ox_done"], STEPS)
            for t in range(TPB):
                for c in range(CHK // 2):
                    cc = CHK // 2 + c
                    mm = pe.transpose(psum[:, TAIL_BANK[t], c * P:(c + 1) * P], o_sb[:, (B - 1) % 2, t, cc * P:(cc + 1) * P], ident[:, :])
                mm.then_inc(s["tail_ps"], 1)
            spread_weights(0)
            spread_weights(1)
            pe.wait_ge(s["tail_done"], TPB)
            for t in range(TPB):
                for c in range(CHK):
                    mm = pe.matmul(psum[:, 7, t * D:(t + 1) * D], oxT[:, t, c, :], wo_sb[:, c, :], start=(c == 0), stop=(c == CHK - 1))
            mm.then_inc(s["tail_ps"], 1)

            def first_mixture(n):
                half, e = divmod(n, NE)
                pe.wait_ge(s["xeT_lo_done"], n + 1)
                if half == 0:
                    pe.wait_ge(s["wt_lo_done"], e + 1)
                hi, lo = xeT_hi[:, n % 3, :], xeT_lo[:, n % 3, :]
                for c in range(HC):
                    if n == 0:
                        pe.wait_ge(s["exp_done"], STEPS)
                    if half and e == 0:
                        pe.wait_ge(s["h_f_done"], c + 1)
                    pe.matmul(bank(c), w1T_hi[:, e, c, :], hi, start=(e == 0), stop=False)
                    pe.matmul(bank(c), w1T_hi[:, e, c, :], lo, start=False, stop=False)
                    mm = pe.matmul(bank(c), w1T_lo[:, e, c, :], hi, start=False, stop=(e == NE - 1))
                mm.then_inc(s["h_ps"], 1)

            def bias(stage, half):
                if stage == "turn":
                    if half == 0:
                        pe.wait_ge(s["x2_done"], NT)
                    else:
                        pe.wait_ge(s["dw1_lo_done"], 2)
                    for i in range(4):
                        mm = pe.transpose(psum[0:NE, 7, i * P:(i + 1) * P], dw[:, half, i, 2, :], ident[:, :])
                    mm.then_inc(s["dw3_ps"], 1)
                else:
                    pe.wait_ge(s["dw3_done"], half + 1)
                    pe.wait_ge(s["ld_b2"], 16)
                    for i in range(4):
                        mm = pe.matmul(psum[:, 7, i * D:(i + 1) * D], dw3T[:, i * P:(i + 1) * P], b2_sb[:, :], start=True, stop=True)
                    mm.then_inc(s["bias_ps"], 1)

            def second_mixture(half):
                for i in range(4):
                    for eg in range(NEG):
                        n = (4 * half + i) * NEG + eg
                        if n >= 3:
                            pe.wait_ge(s["y_done"], EG * (n - 2))
                        es = slice(eg * EG, (eg + 1) * EG)
                        o = bank(5 + n % 3)
                        for c in range(HC):
                            if i == 0 and eg == 0:
                                pe.wait_ge(s["h_lo_done"], HC * half + c + 1)
                            hi, lo = (h[:, half, c, i * P:(i + 1) * P] for h in (h_hi, h_lo))
                            w_hi, w_lo = (w[:, c, es, :].rearrange("p e d -> p (e d)") for w in (w2T_hi, w2T_lo))
                            pe.matmul(o, hi, w_hi, start=(c == 0), stop=False)
                            pe.matmul(o, hi, w_lo, start=False, stop=False)
                            mm = pe.matmul(o, lo, w_hi, start=False, stop=(c == HC - 1))
                        mm.then_inc(s["y_ps"], 1)

            for n in range(2 * NE):
                if n < 2 * NE - 2:
                    spread_weights(n + 2)
                if n < 2 * NE - 1:
                    turn_weights(n + 1)
                if n in BIAS:
                    bias(*BIAS[n])
                for stage in ROUTE_2:
                    if ROUTE_2[stage] == n:
                        route(1, stage, 7)
                first_mixture(n)
            pe.wait_ge(s["xe_done"], 2 * NE)
            pe.wait_ge(s["wt_lo_done"], 2 * NE)
            for half in range(2):
                second_mixture(half)

        @block.vector
        def _(dve):
            count = [0]

            def link(ins):
                count[0] += 1
                ins.then_inc(s["chain_dve"], 1)
                dve.wait_ge(s["chain_dve"], count[0])

            def statistics(src, lo):
                n = len(src)
                for i, t in enumerate(src):
                    dve.bn_stats(stats[:, lo + i, :], t).then_inc(s["stats_done"], 1)
                dve.wait_ge(s["stats_done"], lo + n)
                for i in range(n):
                    dve.bn_aggr(mv[:, lo + i, :], stats[:, lo + i, :]).then_inc(s["mv_done"], 1)

            def normalize(out_, in_, slot):
                return dve.tensor_scalar(out_, in_, mv[:, slot, 0:1], rstd[:, slot:slot + 1], ALU.subtract, ALU.mult)

            def first_statistics(half):
                dve.wait_ge(s[f"ld_x{half}"], 16)
                statistics([x_sb[:, NT // 2 * half + t, :] for t in range(NT // 2)], LN_X + NT // 2 * half)

            def first_normalize(half):
                dve.wait_ge(s["rstd_done"], half + 1)
                for t in range(NT // 2 * half, NT // 2 * (half + 1)):
                    normalize(xn[:, t, :], x_sb[:, t, :], LN_X + t).then_inc(s["xn_done"], 1)

            first_statistics(0)
            first_statistics(1)
            dve.wait_ge(s["chain_pool"], 2)
            dve.tensor_copy(ident_r[:, :], ident[:, :]).then_inc(s["ident_r_done"], 1)
            link(dve.tensor_reduce(mask_d[:, :], ident[:, :].rearrange("p (h d) -> p d h", d=DA), AX_X, ALU.add))
            dve.wait_ge(s["ld_pds"], 16)
            link(dve.tensor_tensor(pds_b[:, 1, :], pds_b[:, 0, :], mask_d[:, :], ALU.mult))
            dve.tensor_reduce(pds[:, 0:1], pds_b[:, 1, :], AX_X, ALU.add).then_inc(s["pds_done"], 1)
            dve.wait_ge(s["pds_done"], 1)
            dve.scalar_tensor_tensor(pds[:, 1:2], pds[:, 0:1], -1.0, pds[:, 0:1], ALU.mult, ALU.min).then_inc(s["absneg_done"], 1)
            first_normalize(0)
            first_normalize(1)
            dve.tensor_reduce(mask_kg[:, :], ident[0:GK, 0:GK].rearrange("p (k g) -> p g k", g=G), AX_X, ALU.add).then_inc(s["mask_done"], 1)
            dve.wait_ge(s["mask_done"], 1)
            dve.tensor_copy(mask_v[:, :, :], mask_kg[:, :, None].to_broadcast([GK, G, DA])).then_inc(s["mask_done"], 1)

            def context_statistics(b):
                dve.wait_ge(s[f"ld_ctx{b}"], 16)
                statistics([ctx_sb[:, KC * b + t, :] for t in range(KC)], LN_C + KC * b)

            def context_normalize(b):
                dve.wait_ge(s["rstd_done"], 3 + b)
                for t in range(KC):
                    ct = KC * b + t
                    normalize(ctx_sb[:, ct, :], ctx_sb[:, ct, :], LN_C + ct).then_inc(s["ctxn_done"], 1)

            context_statistics(0)
            dve.wait_ge(s["softplus_done"], 1)
            link(dve.scalar_tensor_tensor(pds[:, 3:4], pds[:, 0:1], 0.0, pds[:, 2:3], ALU.max, ALU.add))
            dve.tensor_scalar(pds[:, 3:4], pds[:, 3:4], Q_SCALE, None, ALU.mult).then_inc(s["qscale_done"], 1)
            dve.wait_ge(s["rel_ps"], 1)
            dve.wait_ge(s["chain_pool"], 6)
            dve.wait_ge(s["consts"], 5)
            for g in range(G):
                dve.tensor_scalar(relM[:, :, g], psum[:, 1, 256:256 + NPOS], mask4[:, g:g + 1], None, ALU.mult)\
                   .then_inc(s["relM_done"], 1)
            def values_masked(u):
                dve.wait_ge(s["vwin_ps"], u + 1)
                if VG * u >= VRING:
                    dve.wait_ge(s["oa_ps"], (VG * (u + 1) - 1 - VRING) // NB + 1)
                at = VG * u % VRING
                dve.tensor_tensor(vbd[:, at:at + VG, :].rearrange("p n (h e) -> p (n h) e", h=2),
                                  bank(u % 3, GK).rearrange("p (n e) -> p n e", e=G * DA),
                                  mask_v[:, :, :].rearrange("p g d -> p (g d)")[:, None, :].to_broadcast([GK, 2 * VG, G * DA]),
                                  ALU.mult).then_inc(s["vbd_done"], 1)

            def context_lo(b):
                dve.wait_ge(s["ctx_hi_done"], b + 1)
                dve.tensor_tensor(ctx_lo[:, b % 2, :], ctx_f[:, :], ctx_hi[:, b % 2, :].bitcast(F32), ALU.subtract).then_inc(s["ctx_lo_done"], 1)

            def key_unit(m):
                k, _ = kv_counts(m)
                g, t = divmod(m, UNITS)
                dve.wait_ge(s["unit_ps"], m + 1)
                if k >= 2:
                    dve.wait_ge(s["kf_done"], k - 1)
                ps = bank(unit_bank(m))
                dve.tensor_tensor(rope_a[:, k % 2, :].rearrange("p (h d) -> p h d", d=DX // 2), ps.rearrange("p (h d) -> p h d", d=DX // 2),
                                  cos_sb[:, t, None, :].to_broadcast([P, 2 * HG, DX // 2]), ALU.mult)
                ph = ps.rearrange("p (h a d) -> p h a d", a=2, d=DX // 2)
                bh = rope_b[:, k % 2, :].rearrange("p (h a d) -> p h a d", a=2, d=DX // 2)
                for a in range(2):
                    ins = dve.tensor_tensor(bh[:, :, a, :], ph[:, :, 1 - a, :],
                                            sin_sb[:, t, a, None, :].to_broadcast([P, HG, DX // 2]), ALU.mult)
                ins.then_inc(s["rope_done"], 1)

            for j in range(2):
                dve.wait_ge(s["k_ps"], j + 1)
                for g in range(G):
                    dve.tensor_scalar(kM[:, 2 * j:2 * j + 2, PAST:PAST + S, g], bank(5 - j).rearrange("p (a b) -> p a b", a=2),
                                      mask4[:, g:g + 1], K_SCALE, ALU.mult, ALU.mult).then_inc(s["kM_done"], 1)
                if j == 0:
                    values_masked(0)
            context_normalize(0)
            for u in range(1, 6):
                values_masked(u)
                if u == 3:
                    context_lo(0)
            dve.wait_ge(s["ld_rope"], 32)
            dve.tensor_scalar(sin_sb[:, :, 0, :], sin_sb[:, :, 1, :], -1.0, None, ALU.mult).then_inc(s["sin_done"], 1)
            dve.wait_ge(s["sin_done"], 1)

            def add_positions(b):
                dve.wait_ge(s["logit_ps"], b + 1)
                dve.wait_ge(s["shifted"], 16)
                dve.wait_ge(s["xT4_done"], B)
                if b >= 2:
                    dve.wait_ge(s["prob_done"], b - 1)
                full, tail = NB - 1, S - (NB - 1) * CH
                ps = psum[0:GK, local_bank(b), :].rearrange("p (h t) -> p h t", h=2)
                dst = logits[:, b % 2, :, :]
                for h in range(2):
                    ins = dve.tensor_tensor(dst[:, h, 0:full * CH].rearrange("p (n c) -> p n c", c=CH),
                                            ps[:, h, 0:full * CH].rearrange("p (n c) -> p n c", c=CH),
                                            bd[:, :, b, h, 0:full].rearrange("p c n -> p n c"), ALU.add)
                ins.then_inc(s["added_done"], 1)
                dve.tensor_tensor(dst[:, :, full * CH:S], ps[:, :, full * CH:S],
                                  bd[:, 0:tail, b, :, full].rearrange("p c h -> p h c"), ALU.add).then_inc(s["added_done"], 1)

            for m in range(KC):
                key_unit(m)
            for b in range(B):
                add_positions(b)
                if b < B - 1:
                    context_statistics(b + 1)

            def local_reciprocal(b):
                dve.wait_ge(s["sum_ps"], b + 1)
                if b:
                    dve.wait_ge(s["oT_done"], b)
                dve.reciprocal(rec[:, :], psum[:, 3, 0:S]).then_inc(s["rec_done"], 1)

            def local_normalize(b):
                dve.wait_ge(s["oa_ps"], b + 1)
                dve.wait_ge(s["rec_done"], b + 1)
                dve.tensor_tensor(oT[:, S * b:S * (b + 1)], psum[:, local_bank(b), 0:S], rec[:, :], ALU.mult).then_inc(s["oT_done"], 1)

            def local_residual(b):
                dve.wait_ge(s["ya_ps"], b + 1)
                for i in range(TPB):
                    t = TPB * b + i
                    dve.tensor_tensor(x_sb[:, t, :], psum[:, local_bank(b), i * D:(i + 1) * D], x_sb[:, t, :], ALU.add).then_inc(s["x1_done"], 1)
                dve.wait_ge(s["x1_done"], TPB * (b + 1))

            def latents(pair, part):
                before = 2 + B + 2 * pair
                tiles = range(4 * pair, 4 * pair + 4)
                lo = LN_1 + pair * NT
                if part == 0:
                    statistics([x_sb[:, t, :] for t in tiles], lo)
                elif part == 1:
                    dve.wait_ge(s["rstd_done"], before + 1)
                    for i, t in enumerate(tiles):
                        normalize(xn[:, t, :], x_sb[:, t, :], lo + i).then_inc(s["xn1_done"], 1)
                    dve.wait_ge(s["xn1_done"], 4 * (pair + 1))
                    statistics([xn[:, t, :] for t in tiles], lo + 4)
                else:
                    dve.wait_ge(s["rstd_done"], before + 2)
                    for i, t in enumerate(tiles):
                        normalize(xn[:, t, :], xn[:, t, :], lo + 4 + i).then_inc(s["lat_in_done"], 1)

            def output_bias(pair):
                dve.wait_ge(s["ld_bo"], 16)
                for t in range(4 * pair, 4 * pair + 4):
                    dve.tensor_tensor(x_sb[:, t, :], x_sb[:, t, :], bo_all[:, :], ALU.add).then_inc(s["bo_added"], 1)

            def latents_lo(pair):
                dve.wait_ge(s["lat_hi_done"], pair + 1)
                toks = slice(pair * HALF_TOK, (pair + 1) * HALF_TOK)
                dve.tensor_tensor(lat_lo[:, toks], lat_f[:, :], lat_hi[:, toks].bitcast(F32), ALU.subtract).then_inc(s["lat_lo_done"], 1)

            local_reciprocal(0)
            for u in range(6, 11):
                values_masked(u)
            local_normalize(0)
            local_reciprocal(1)
            for u in range(11, 14):
                values_masked(u)
            local_residual(0)
            for u in range(14, 16):
                values_masked(u)
            context_normalize(1)
            local_normalize(1)
            local_reciprocal(2)
            for u in range(16, 18):
                values_masked(u)
            local_residual(1)
            latents(0, 0)
            values_masked(18)
            values_masked(19)
            latents(0, 1)
            local_normalize(2)
            values_masked(20)
            values_masked(21)
            latents(0, 2)
            local_reciprocal(3)
            local_residual(2)
            latents_lo(0)

            def queries_lo(j):
                if j == 0:
                    for n, (a, rows, to) in enumerate(FIRST_COPIES):
                        dve.wait_ge(s["q_first_hi_done"], 2 * (n // 2 + 1))
                        dve.tensor_tensor(q_twice[to, 0, 1, a:QH:2, :], psum[rows, 7, :].rearrange("p (h t) -> p h t", t=S),
                                          q_twice[to, 0, 0, a:QH:2, :].bitcast(F32), ALU.subtract).then_inc(s["q_first_lo_done"], 1)
                    return
                dve.wait_ge(s["qx_hi_done"], j)
                dve.tensor_tensor(q_pair[:, j % 2, 1, :, :], bank(7).rearrange("p (h t) -> p h t", t=S),
                                  q_pair[:, j % 2, 0, :, :].bitcast(F32), ALU.subtract).then_inc(s["qx_lo_done"], 1)

            def clip(i):
                dve.wait_ge(s["exp_done"], i + 1)
                dve.tensor_scalar(e_sb[:, i % 3, :], e_sb[:, i % 3, :], E_LO, E_HI, ALU.max, ALU.min).then_inc(s["clip_done"], 1)

            def divide(i):
                b, h = divmod(i, HX)
                dve.wait_ge(s["pv_ps"], i + 1)
                ps = psum[:, 4, 0:TPB * (DX + 1)].rearrange("p (q d) -> p q d", d=DX + 1)
                dve.reciprocal(den[:, i % 2, :], ps[:, :, DX]).then_inc(s["den_done"], 1)
                dve.wait_ge(s["den_done"], i + 1)
                if h == 0 and b >= 2:
                    dve.wait_ge(s["extra_ps"], last_turn(b - 2))
                dve.tensor_tensor(o_sb[:, b % 2, :, h * DX:(h + 1) * DX], ps[:, :, 0:DX],
                                  den[:, i % 2, :, None].to_broadcast([P, TPB, DX]), ALU.mult).then_inc(s["ox_done"], 1)

            def extra(i):
                what = extras[i]
                if what[0] == "context":
                    context_lo(what[1])
                elif what[0] == "latents":
                    latents_lo(1)
                elif what[0] == "project":
                    _, b, t = what
                    tile = TPB * b + t
                    dve.wait_ge(s["extra_ps"], EXTRA_NO[i] + 1)
                    dve.tensor_tensor(x_sb[:, tile, :], psum[:, 7, 0:D], x_sb[:, tile, :], ALU.add).then_inc(s["x2_done"], 1)

            def weights_lo(n):
                dve.wait_ge(s["wt_hi_done"], n + 1)
                ps = bank(6).rearrange("p (c q) -> p c q", q=P)
                hi, lo = (w1T_hi[:, n, :, :], w1T_lo[:, n, :, :]) if n < NE else (w2T_hi[:, :, n - NE, :], w2T_lo[:, :, n - NE, :])
                dve.tensor_tensor(lo, ps, hi.bitcast(F32), ALU.subtract).then_inc(s["wt_lo_done"], 1)

            def expert_tokens(n):
                dve.wait_ge(s["spread_ps"], n + 1)
                if n >= 2:
                    dve.wait_ge(s["xeT_lo_done"], n - 1)
                dve.tensor_tensor(xeT[:, n % 2, :], bank(5 - n % 2), xnT[:, n // NE, :], ALU.mult).then_inc(s["xe_done"], 1)

            def final_norm(half, part):
                if part == 0:
                    dve.wait_ge(s["x2_done"], 4 * (half + 1))
                    statistics([x_sb[:, 4 * half + i, :] for i in range(4)], LN_F + 4 * half)
                else:
                    dve.wait_ge(s["rstd_done"], 2 + B + 4 + half + 1)
                    for i in range(4):
                        t = 4 * half + i
                        normalize(xn[:, t, :], x_sb[:, t, :], LN_F + t).then_inc(s["fn_done"], 1)

            def route(half, stage, at):
                if stage == "scores":
                    dve.wait_ge(s["z_ps"], half + 1)
                    dve.wait_ge(s["fill_done"], 2)
                    dve.tensor_copy(z[:, :, 0:NE], psum[:, at, 0:4 * NR * NE].rearrange("p (r e) -> p r e", e=NE)).then_inc(s["z_done"], 1)
                    dve.wait_ge(s["z_done"], half + 1)
                    for r in range(4 * NR):
                        dve.max(top8[:, r, :], z[:, r, :]).then_inc(s["top_done"], 1)
                    dve.wait_ge(s["top_done"], 4 * NR * (half + 1))
                    dve.tensor_copy(top3[:, :, 0:TOPK], top8[:, :, 0:TOPK]).then_inc(s["top3_done"], 1)
                    dve.tensor_tensor(zsh[:, :, :], z[:, :, 0:NE], top8[:, :, 0:1].to_broadcast([P, 4 * NR, NE]), ALU.subtract)\
                       .then_inc(s["zsh_done"], 1)
                    return
                if stage == "turn":
                    dve.wait_ge(s["dw1_hi_done"], half + 1)
                    dve.tensor_tensor(dw1T[REST:SPLIT, half, :], bank(at, NE), dw1T[0:NE, half, :].bitcast(F32), ALU.subtract)\
                       .then_inc(s["dw1_lo_done"], 1)
                if stage not in ("chosen", "softmax"):
                    return
                if stage == "softmax":
                    route_softmax(half)
                    return
                dve.wait_ge(s["top3_done"], half + 1)
                for r in range(4 * NR):
                    dve.match_replace(zr[:, r, :], top3[:, r, :], z[:, r, :], TAKEN).then_inc(s["zr_done"], 1)
                dve.wait_ge(s["zr_done"], 4 * NR * (half + 1))
                dve.tensor_tensor(chosen[:, :, :], zr[:, :, 0:NE], z[:, :, 0:NE], ALU.not_equal).then_inc(s["chosen_done"], 1)

            def route_softmax(half):
                dve.wait_ge(s["chosen_done"], half + 1)
                dve.wait_ge(s["ez_done"], half + 1)
                dve.tensor_tensor(chosen[:, :, :], chosen[:, :, :], ez[:, :, :], ALU.mult).then_inc(s["wsel_done"], 1)
                dve.wait_ge(s["wsel_done"], half + 1)
                dve.tensor_reduce(zsum[:, :], chosen[:, :, :], AX_X, ALU.add).then_inc(s["zsum_done"], 1)
                dve.wait_ge(s["zsum_done"], half + 1)
                dve.reciprocal(zsum[:, :], zsum[:, :]).then_inc(s["zrec_done"], 1)
                dve.wait_ge(s["zrec_done"], half + 1)
                dve.tensor_tensor(dw[:, half, :, :, :].rearrange("p i r e -> p (i r) e"), chosen[:, :, :],
                                  zsum[:, :, None].to_broadcast([P, 4 * NR, NE]), ALU.mult).then_inc(s["dw_done"], 1)

            def bias_add(half):
                dve.wait_ge(s["bias_ps"], half + 1)
                for i in range(4):
                    t = 4 * half + i
                    dve.tensor_tensor(x_sb[:, t, :], psum[:, 7, i * D:(i + 1) * D], x_sb[:, t, :], ALU.add).then_inc(s["bias_done"], 1)

            def hidden_lo(half, chunks):
                for c in chunks:
                    dve.wait_ge(s["h_hi_done"], half * HC + c + 1)
                    dve.tensor_tensor(h_lo[:, half, c, :], h_f[:, c, :], h_hi[:, half, c, :].bitcast(F32), ALU.subtract)\
                       .then_inc(s["h_lo_done"], 1)

            local_normalize(3)
            queries_lo(0)
            local_residual(3)
            key_unit(UNITS)
            clip(0)
            beside = {1: (output_bias, 0), 3: (context_normalize, 2), 8: (output_bias, 1), 10: (context_normalize, 3)}
            for i in range(STEPS):
                if i in LATENT_STEPS:
                    latents(1, LATENT_STEPS.index(i))
                if i in beside:
                    work, arg = beside[i]
                    work(arg)
                if i % QH == 0 and i + QH < STEPS:
                    queries_lo(i // QH + 1)
                if i in extras:
                    extra(i)
                if i + 1 < STEPS:
                    clip(i + 1)
                m = i + LEAD
                if m < NG * UNITS and m % UNITS < KC:
                    key_unit(m)
                divide(i)
                if i == NORM_STEP:
                    final_norm(0, 0)
                if i == NORM_STEP + 1:
                    final_norm(0, 1)
                for stage in ROUTE:
                    if ROUTE[stage] == i:
                        route(0, stage, 5)

            weights_lo(0)
            expert_tokens(0)
            expert_tokens(1)
            dve.wait_ge(s["tail_ps"], TPB + 1)
            for t in range(TPB):
                tile = TPB * (B - 1) + t
                dve.tensor_tensor(x_sb[:, tile, :], psum[:, 7, t * D:(t + 1) * D], x_sb[:, tile, :], ALU.add).then_inc(s["x2_done"], 1)
            final_norm(1, 0)
            for n in range(2 * NE):
                if n < 2 * NE - 2:
                    expert_tokens(n + 2)
                if n < 2 * NE - 1:
                    weights_lo(n + 1)
                if n == 0:
                    final_norm(1, 1)
                if n in BIAS and BIAS[n][0] == "product":
                    bias_add(BIAS[n][1])
                for stage in ROUTE_2:
                    if ROUTE_2[stage] == n:
                        route(1, stage, 7)
                for half, chunks in HIDDEN.get(n, []):
                    if half == 0:
                        hidden_lo(half, chunks)

            for half in range(2):
                dve.wait_ge(s["bias_done"], 4 * (half + 1))
                for i in range(4):
                    t = 4 * half + i
                    for eg in range(NEG):
                        n = t * NEG + eg
                        dve.wait_ge(s["y_ps"], n + 1)
                        for j in range(EG):
                            e = eg * EG + j
                            dve.scalar_tensor_tensor(x_sb[:, t, :], psum[:, 5 + n % 3, j * D:(j + 1) * D],
                                                     dw[:, half, i, 1, e:e + 1], x_sb[:, t, :], ALU.mult, ALU.add)\
                               .then_inc(s["y_done"], 1)
                            dve.wait_ge(s["y_done"], n * EG + j + 1)
                    dve.sem_inc(s["x3_done"], 1)
                    if t == 0:
                        hidden_lo(1, range(HC))


_INS = ["x", "ctx_1024", "L0_attn_position_embeddings", "L0_attn_Wq", "L0_attn_Wk", "L0_attn_Wv",
        "L0_attn_Wpost", "L0_attn_Wrel", "L0_attn_per_dim_scale", "L0_xattn_cos", "L0_xattn_sin",
        "L0_xattn_ln_lat_g", "L0_xattn_ln_lat_b", "L0_xattn_ln_ctx_g", "L0_xattn_ln_ctx_b", "L0_xattn_Wq",
        "L0_xattn_Wkv", "L0_xattn_Wo", "L0_xattn_bo", "L0_ffn_P_w", "L0_ffn_U1", "L0_ffn_U2", "L0_ffn_U3",
        "L0_ffn_W1", "L0_ffn_W2", "L0_ffn_b2"]
_OUTS = [((4, 256, 128), "float32")]


def kernel(**inputs):
    import numpy as _np
    import concourse.bacc as _bacc
    from concourse import mybir as _mybir
    from concourse.bass_utils import run_bass_kernel_spmd as _run

    nc = _bacc.Bacc("TRN2", target_bir_lowering=False, num_devices=1)
    arrays, args = {}, []
    for name in _INS:
        a = _np.ascontiguousarray(inputs[name])
        arrays[f"in_{name}_dram"] = a
        args.append(nc.dram_tensor(f"in_{name}_dram", a.shape, _mybir.dt.from_np(a.dtype), kind="ExternalInput").ap())
    for i, (shape, dtype) in enumerate(_OUTS):
        dt = _mybir.dt.from_np(_np.dtype(dtype))
        args.append(nc.dram_tensor(f"out_{i}_dram", shape, dt, kind="ExternalOutput").ap())
    decoder_layer(nc, *args)
    r = _run(nc, [arrays], core_ids=[0])
    return r.results[0]["out_0_dram"]
```
